# Optimizing a Trainium2 kernel written in Bass

```python
import numpy as np
import jax
import jax.numpy as jnp

def _softmax(x, axis=-1):
    return jax.nn.softmax(x, axis=axis)

def _gelu(x):
    return jax.nn.gelu(x, approximate=True)

def _silu(x):
    return jax.nn.silu(x)

def _sigmoid(x):
    return jax.nn.sigmoid(x)

def _layernorm(x, axis=-1, eps=1e-05):
    m = jnp.mean(x, axis=axis, keepdims=True)
    v = jnp.var(x, axis=axis, keepdims=True)
    return (x - m) / jnp.sqrt(v + eps)

def _scatter_add(tgt, idx, src, axis=0):
    return tgt.at[idx].add(src)

def _segment_sum(src, seg, n):
    return jax.ops.segment_sum(src, seg, n)
kernel_name = 'mk_cond_seq_d2_seqx_r2_c47fb6'

def setup_inputs(seed: int=0):
    np.random.seed(seed)
    _w = jnp.asarray

    def _rec_inputs():
        import jax
        import jax.numpy as jnp
        _rk = jax.random.key(seed)
        x = -0.0003929 + 0.9999 * jax.random.normal(jax.random.fold_in(_rk, 1), (32, 128, 512), jnp.float32)
        _lenS = 128 - jax.random.randint(jax.random.fold_in(_rk, 7), (32,), 0, max(1, 128 // 4) + 1, jnp.int32)
        _lenS2 = 128 - jax.random.randint(jax.random.fold_in(_rk, 8), (32,), 0, max(1, 128 // 4) + 1, jnp.int32)
        cond_1024 = 0.00782532 + 1.00527 * jax.random.normal(jax.random.fold_in(_rk, 11), (32, 512), jnp.float32)
        _validS = jnp.arange(128)[None, :] < _lenS[:, None]
        _validS2 = jnp.arange(128)[None, :] < _lenS2[:, None]
        _causal = jnp.tril(jnp.ones((128, 128), dtype=bool))
        mask_BxS_bk0 = jnp.logical_not(jnp.broadcast_to(_validS[:, :], (32, 128)))
        return (x, cond_1024, mask_BxS_bk0)
    x, cond_1024, mask_BxS_bk0 = _rec_inputs()

    def _L0_cond_setup():
        import jax, jax.numpy as jnp
        import numpy as np
        B, L, D = (8, 1024, 512)
        FF_MULT = 2
        EPS = 1e-06

        def _layernorm(x):
            mu = jnp.mean(x, axis=-1, keepdims=True)
            var = jnp.mean(jnp.square(x - mu), axis=-1, keepdims=True)
            return (x - mu) / jnp.sqrt(var + EPS)

        def _ssm_fallback(u, w1, b1, w2, b2):
            h = jax.nn.gelu(u @ w1 + b1, approximate=False)
            return h @ w2 + b2
        key = jax.random.key(seed)
        ks = jax.random.split(key, 20)
        s = 0.02
        inp = {'x': jax.random.normal(ks[0], (B, L, D), jnp.float32), 't': jax.random.normal(ks[1], (B, D), jnp.float32), 'mask': jax.random.randint(ks[2], (B, L), 0, 2) > 0, 'ada_w': jax.random.normal(ks[3], (D, 3 * D), jnp.float32) * s, 'ada_b': jnp.zeros((3 * D,), jnp.float32), 'ssm_w1': jax.random.normal(ks[4], (D, D), jnp.float32) * s, 'ssm_b1': jnp.zeros((D,), jnp.float32), 'ssm_w2': jax.random.normal(ks[5], (D, D), jnp.float32) * s, 'ssm_b2': jnp.zeros((D,), jnp.float32), 'bwd_w1': jax.random.normal(ks[6], (D, D), jnp.float32) * s, 'bwd_b1': jnp.zeros((D,), jnp.float32), 'bwd_w2': jax.random.normal(ks[7], (D, D), jnp.float32) * s, 'bwd_b2': jnp.zeros((D,), jnp.float32), 'ffada_w': jax.random.normal(ks[8], (D, 3 * D), jnp.float32) * s, 'ffada_b': jnp.zeros((3 * D,), jnp.float32), 'ff_w1': jax.random.normal(ks[9], (D, FF_MULT * D), jnp.float32) * s, 'ff_b1': jnp.zeros((FF_MULT * D,), jnp.float32), 'ff_w2': jax.random.normal(ks[10], (FF_MULT * D, D), jnp.float32) * s, 'ff_b2': jnp.zeros((D,), jnp.float32)}
        return inp
    _L0_cond_all = _L0_cond_setup()
    _L0_cond_in = {k: v for k, v in _L0_cond_all.items() if k in ('ada_w', 'ada_b', 'ssm_w1', 'ssm_b1', 'ssm_w2', 'ssm_b2', 'bwd_w1', 'bwd_b1', 'bwd_w2', 'bwd_b2', 'ffada_w', 'ffada_b', 'ff_w1', 'ff_b1', 'ff_w2', 'ff_b2')}
    del _L0_cond_all

    def _L1_cond_setup():
        import math
        import jax, jax.numpy as jnp
        import numpy as np
        D_MODEL = 512
        N_HEADS = 16
        FFN_DIM = 2048
        EPS = 1e-05

        def _layernorm(x, w, b):
            mu = jnp.mean(x, axis=-1, keepdims=True)
            var = jnp.var(x, axis=-1, keepdims=True)
            return (x - mu) * jax.lax.rsqrt(var + EPS) * w + b

        def _modulate(x, shift, scale):
            return x * (1.0 + scale[:, None, :]) + shift[:, None, :]
        key = jax.random.key(seed)
        ks = jax.random.split(key, 16)
        B, S, D, F = (2, 1024, D_MODEL, FFN_DIM)
        s = 0.02
        return {'x': jax.random.normal(ks[0], (B, S, D), jnp.float32), 't_emb': jax.random.normal(ks[1], (B, D), jnp.float32), 'ln1_w': jnp.ones((D,), jnp.float32), 'ln1_b': jnp.zeros((D,), jnp.float32), 'ln2_w': jnp.ones((D,), jnp.float32), 'ln2_b': jnp.zeros((D,), jnp.float32), 'wq': jax.random.normal(ks[2], (D, D), jnp.float32) * s, 'bq': jnp.zeros((D,), jnp.float32), 'wk': jax.random.normal(ks[3], (D, D), jnp.float32) * s, 'bk': jnp.zeros((D,), jnp.float32), 'wv': jax.random.normal(ks[4], (D, D), jnp.float32) * s, 'bv': jnp.zeros((D,), jnp.float32), 'wo': jax.random.normal(ks[5], (D, D), jnp.float32) * s, 'bo': jnp.zeros((D,), jnp.float32), 'wt_attn': jax.random.normal(ks[6], (D, 2 * D), jnp.float32) * s, 'bt_attn': jnp.zeros((2 * D,), jnp.float32), 'wt_ffn': jax.random.normal(ks[7], (D, 2 * D), jnp.float32) * s, 'bt_ffn': jnp.zeros((2 * D,), jnp.float32), 'w1': jax.random.normal(ks[8], (D, F), jnp.float32) * s, 'b1': jnp.zeros((F,), jnp.float32), 'w2': jax.random.normal(ks[9], (F, D), jnp.float32) * s, 'b2': jnp.zeros((D,), jnp.float32)}
    _L1_cond_all = _L1_cond_setup()
    _L1_cond_in = {k: v for k, v in _L1_cond_all.items() if k in ('ln1_w', 'ln1_b', 'ln2_w', 'ln2_b', 'wq', 'bq', 'wk', 'bk', 'wv', 'bv', 'wo', 'bo', 'wt_attn', 'bt_attn', 'wt_ffn', 'bt_ffn', 'w1', 'b1', 'w2', 'b2')}
    del _L1_cond_all
    return {'x': x, 'cond_1024': cond_1024, 'mask_BxS_bk0': mask_BxS_bk0, 'L0_cond_ada_w': _L0_cond_in['ada_w'], 'L0_cond_ada_b': _L0_cond_in['ada_b'], 'L0_cond_ssm_w1': _L0_cond_in['ssm_w1'], 'L0_cond_ssm_b1': _L0_cond_in['ssm_b1'], 'L0_cond_ssm_w2': _L0_cond_in['ssm_w2'], 'L0_cond_ssm_b2': _L0_cond_in['ssm_b2'], 'L0_cond_bwd_w1': _L0_cond_in['bwd_w1'], 'L0_cond_bwd_b1': _L0_cond_in['bwd_b1'], 'L0_cond_bwd_w2': _L0_cond_in['bwd_w2'], 'L0_cond_bwd_b2': _L0_cond_in['bwd_b2'], 'L0_cond_ffada_w': _L0_cond_in['ffada_w'], 'L0_cond_ffada_b': _L0_cond_in['ffada_b'], 'L0_cond_ff_w1': _L0_cond_in['ff_w1'], 'L0_cond_ff_b1': _L0_cond_in['ff_b1'], 'L0_cond_ff_w2': _L0_cond_in['ff_w2'], 'L0_cond_ff_b2': _L0_cond_in['ff_b2'], 'L1_cond_ln1_w': _L1_cond_in['ln1_w'], 'L1_cond_ln1_b': _L1_cond_in['ln1_b'], 'L1_cond_ln2_w': _L1_cond_in['ln2_w'], 'L1_cond_ln2_b': _L1_cond_in['ln2_b'], 'L1_cond_wq': _L1_cond_in['wq'], 'L1_cond_bq': _L1_cond_in['bq'], 'L1_cond_wk': _L1_cond_in['wk'], 'L1_cond_bk': _L1_cond_in['bk'], 'L1_cond_wv': _L1_cond_in['wv'], 'L1_cond_bv': _L1_cond_in['bv'], 'L1_cond_wo': _L1_cond_in['wo'], 'L1_cond_bo': _L1_cond_in['bo'], 'L1_cond_wt_attn': _L1_cond_in['wt_attn'], 'L1_cond_bt_attn': _L1_cond_in['bt_attn'], 'L1_cond_wt_ffn': _L1_cond_in['wt_ffn'], 'L1_cond_bt_ffn': _L1_cond_in['bt_ffn'], 'L1_cond_w1': _L1_cond_in['w1'], 'L1_cond_b1': _L1_cond_in['b1'], 'L1_cond_w2': _L1_cond_in['w2'], 'L1_cond_b2': _L1_cond_in['b2']}

def reference(x, cond_1024, mask_BxS_bk0, L0_cond_ada_w, L0_cond_ada_b, L0_cond_ssm_w1, L0_cond_ssm_b1, L0_cond_ssm_w2, L0_cond_ssm_b2, L0_cond_bwd_w1, L0_cond_bwd_b1, L0_cond_bwd_w2, L0_cond_bwd_b2, L0_cond_ffada_w, L0_cond_ffada_b, L0_cond_ff_w1, L0_cond_ff_b1, L0_cond_ff_w2, L0_cond_ff_b2, L1_cond_ln1_w, L1_cond_ln1_b, L1_cond_ln2_w, L1_cond_ln2_b, L1_cond_wq, L1_cond_bq, L1_cond_wk, L1_cond_bk, L1_cond_wv, L1_cond_bv, L1_cond_wo, L1_cond_bo, L1_cond_wt_attn, L1_cond_bt_attn, L1_cond_wt_ffn, L1_cond_bt_ffn, L1_cond_w1, L1_cond_b1, L1_cond_w2, L1_cond_b2):
    import jax
    import jax.numpy as jnp

    def _L0_cond_ref(x, t, mask, ada_w, ada_b, ssm_w1, ssm_b1, ssm_w2, ssm_b2, bwd_w1, bwd_b1, bwd_w2, bwd_b2, ffada_w, ffada_b, ff_w1, ff_b1, ff_w2, ff_b2):
        import jax, jax.numpy as jnp
        import numpy as np
        B, L, D = (8, 1024, 512)
        FF_MULT = 2
        EPS = 1e-06

        def _layernorm(x):
            mu = jnp.mean(x, axis=-1, keepdims=True)
            var = jnp.mean(jnp.square(x - mu), axis=-1, keepdims=True)
            return (x - mu) / jnp.sqrt(var + EPS)

        def _ssm_fallback(u, w1, b1, w2, b2):
            h = jax.nn.gelu(u @ w1 + b1, approximate=False)
            return h @ w2 + b2
        m = mask[:, :, None]
        emb = jax.nn.silu(t) @ ada_w + ada_b
        shift, scale, gate_msa = jnp.split(emb, 3, axis=1)
        norm = _layernorm(x) * (1.0 + scale[:, None]) + shift[:, None]
        norm = jnp.where(m, norm, 0.0)
        fwd = _ssm_fallback(norm, ssm_w1, ssm_b1, ssm_w2, ssm_b2)
        bwd = jnp.flip(_ssm_fallback(jnp.flip(norm, axis=1), bwd_w1, bwd_b1, bwd_w2, bwd_b2), axis=1)
        ssm_out = jnp.where(m, fwd + bwd, 0.0)
        x = x + gate_msa[:, None] * ssm_out
        ff_ada = jax.nn.silu(t) @ ffada_w + ffada_b
        shift_mlp, scale_mlp, gate_mlp = jnp.split(ff_ada, 3, axis=1)
        ff_norm = _layernorm(x) * (1.0 + scale_mlp[:, None]) + shift_mlp[:, None]
        h = jax.nn.gelu(ff_norm @ ff_w1 + ff_b1, approximate=True)
        ff_out = h @ ff_w2 + ff_b2
        return x + gate_mlp[:, None] * ff_out

    def _L1_cond_ref(x, t_emb, ln1_w, ln1_b, ln2_w, ln2_b, wq, bq, wk, bk, wv, bv, wo, bo, wt_attn, bt_attn, wt_ffn, bt_ffn, w1, b1, w2, b2):
        import math
        import jax, jax.numpy as jnp
        import numpy as np
        D_MODEL = 512
        N_HEADS = 16
        FFN_DIM = 2048
        EPS = 1e-05

        def _layernorm(x, w, b):
            mu = jnp.mean(x, axis=-1, keepdims=True)
            var = jnp.var(x, axis=-1, keepdims=True)
            return (x - mu) * jax.lax.rsqrt(var + EPS) * w + b

        def _modulate(x, shift, scale):
            return x * (1.0 + scale[:, None, :]) + shift[:, None, :]
        B, S, D = x.shape
        H = N_HEADS
        hd = D // H
        residual = x
        xn = _layernorm(x, ln1_w, ln1_b)
        t_attn = t_emb @ wt_attn + bt_attn
        shift_a, scale_a = jnp.split(t_attn, 2, axis=-1)
        xn = _modulate(xn, shift_a, scale_a)
        q = (xn @ wq + bq).reshape(B, S, H, hd).transpose(0, 2, 1, 3)
        k = (xn @ wk + bk).reshape(B, S, H, hd).transpose(0, 2, 1, 3)
        v = (xn @ wv + bv).reshape(B, S, H, hd).transpose(0, 2, 1, 3)
        scores = jnp.einsum('bhqd,bhkd->bhqk', q, k) / math.sqrt(hd)
        attn = jax.nn.softmax(scores, axis=-1)
        out = jnp.einsum('bhqk,bhkd->bhqd', attn, v)
        out = out.transpose(0, 2, 1, 3).reshape(B, S, D)
        x = residual + (out @ wo + bo)
        residual = x
        xn = _layernorm(x, ln2_w, ln2_b)
        t_ffn = t_emb @ wt_ffn + bt_ffn
        shift_f, scale_f = jnp.split(t_ffn, 2, axis=-1)
        xn = _modulate(xn, shift_f, scale_f)
        h = jax.nn.gelu(xn @ w1 + b1, approximate=False)
        x = residual + (h @ w2 + b2)
        return x
    x = _L0_cond_ref(x, cond_1024, mask_BxS_bk0, L0_cond_ada_w, L0_cond_ada_b, L0_cond_ssm_w1, L0_cond_ssm_b1, L0_cond_ssm_w2, L0_cond_ssm_b2, L0_cond_bwd_w1, L0_cond_bwd_b1, L0_cond_bwd_w2, L0_cond_bwd_b2, L0_cond_ffada_w, L0_cond_ffada_b, L0_cond_ff_w1, L0_cond_ff_b1, L0_cond_ff_w2, L0_cond_ff_b2)
    x = _L1_cond_ref(x, cond_1024, L1_cond_ln1_w, L1_cond_ln1_b, L1_cond_ln2_w, L1_cond_ln2_b, L1_cond_wq, L1_cond_bq, L1_cond_wk, L1_cond_bk, L1_cond_wv, L1_cond_bv, L1_cond_wo, L1_cond_bo, L1_cond_wt_attn, L1_cond_bt_attn, L1_cond_wt_ffn, L1_cond_bt_ffn, L1_cond_w1, L1_cond_b1, L1_cond_w2, L1_cond_b2)
    return x

_drawn_inputs = setup_inputs


def setup_inputs(seed=0):
    import zlib

    import numpy as np

    out = dict(_drawn_inputs(seed))
    spreads = {'L0_cond_ada_b': (0.0, 0.8),
     'L0_cond_ssm_b1': (0.0, 0.8),
     'L0_cond_ssm_b2': (0.0, 0.8),
     'L0_cond_bwd_b1': (0.0, 0.8),
     'L0_cond_bwd_b2': (0.0, 0.784),
     'L0_cond_ffada_b': (0.0, 0.38),
     'L0_cond_ff_b1': (0.0, 0.697),
     'L0_cond_ff_b2': (0.0, 0.289),
     'L1_cond_ln1_w': (1.0, 0.6),
     'L1_cond_ln1_b': (0.0, 0.343),
     'L1_cond_ln2_w': (1.0, 0.6),
     'L1_cond_ln2_b': (0.0, 0.319),
     'L1_cond_bq': (0.0, 0.8),
     'L1_cond_bk': (0.0, 2.0),
     'L1_cond_bv': (0.0, 0.424),
     'L1_cond_bo': (0.0, 0.1),
     'L1_cond_bt_attn': (0.0, 0.401),
     'L1_cond_bt_ffn': (0.0, 0.497),
     'L1_cond_b1': (0.0, 0.335),
     'L1_cond_b2': (0.0, 0.1)}
    factors = {'L0_cond_ssm_w1': 4.604,
     'L0_cond_ssm_w2': 4.288,
     'L0_cond_bwd_w1': 4.605,
     'L0_cond_bwd_w2': 4.278,
     'L1_cond_wq': 7.845,
     'L1_cond_wk': 7.732}
    for name, (base, spread) in spreads.items():
        noise = np.random.default_rng([zlib.crc32(name.encode()), seed]).standard_normal(out[name].shape)
        drawn = base * np.exp(spread * noise) if base else spread * noise
        out[name] = jnp.asarray(drawn.astype(out[name].dtype))
    for name, factor in factors.items():
        out[name] = (out[name] * factor).astype(out[name].dtype)
    return out
```

```python
from contextlib import ExitStack

import concourse.bass as bass
from concourse import mybir

ALU = mybir.AluOpType
ACT = mybir.ActivationFunctionType
AX = mybir.AxisListType
F32 = mybir.dt.float32
F32R = mybir.dt.float32r
U8 = mybir.dt.uint8

P = 128
B = 32
D = 512
KC = D // P
HEADS = 16
HD = D // HEADS
HPC = P // HD
HI, LO = 0, 1
REGION = 2 * KC * D * 2
HID = 1024
PIECE = 512
MUL_HI_LO = ((HI, HI), (HI, LO), (LO, HI))

VEC_ROWS = {}
for _name, _rows in (("ssm_b1", 4), ("bwd_b1", 4), ("ff_b1", 8), ("b1", 16), ("bq", 4), ("bk", 4), ("bv", 4),
                     ("ada_b", 8), ("ffada_b", 8), ("bt_attn", 8), ("bt_ffn", 8),
                     ("ln1_w", 4), ("ln1_b", 4), ("ln2_w", 4), ("ln2_b", 4)):
    VEC_ROWS[_name] = (sum(r for _, r in VEC_ROWS.values()), _rows)
N_VEC = sum(r for _, r in VEC_ROWS.values())


def f32(ap):
    return ap.bitcast(F32)


def w1_view(region, part):
    return region[:, part, 0:KC * HID].rearrange("p (k h) -> p k h", k=KC)


def w2_view(region, part):
    return region[:, part, KC * HID:].rearrange("p (c n) -> p c n", n=D)


def mlp_pieces(w1_halves, w2_halves):
    pieces = []
    for k in range(KC):
        for half in range(2):
            pieces.append((w1_halves[half][k * P:(k + 1) * P, :], k * HID + half * PIECE))
    for c in range(HID // P):
        pieces.append((w2_halves[c // KC][(c % KC) * P:(c % KC + 1) * P, :], KC * HID + c * D))
    return pieces


def attention_pieces(matrices):
    return [(w[k * P:(k + 1) * P, :], (n * KC + k) * D) for n, w in enumerate(matrices) for k in range(KC)]




class Shared:

    def __init__(self):
        self.semaphores = []

    def semaphore(self, nc, name):
        self.semaphores.append(nc.alloc_semaphore(name=name))
        return self.semaphores[-1]

    def end_phase(self, nc):
        nc.clear_and_free_semaphores(self.semaphores)
        nc.all_engine_barrier()
        self.semaphores = []




def prologue(nc, sh, t):
    sem = lambda name: sh.semaphore(nc, "pro_" + name)
    cond_loaded, vec_loaded, mask_loaded, row_loaded = sem("cond_loaded"), sem("vec_loaded"), sem("mask_loaded"), sem("row_loaded")
    zeroed, ident_done, mask_f_done = sem("zeroed"), sem("ident_done"), sem("mask_f_done")
    cond_turned, vec_turned, mask_turned, cond_copied, silu_done = (
        sem("cond_turned"), sem("vec_turned"), sem("mask_turned"), sem("cond_copied"), sem("silu_done"))
    ADA_RING = 3
    ada_loaded = [sem(f"ada_loaded{r}") for r in range(ADA_RING)]
    ada_done, rows_copied, item_turned, item_read = sem("ada_done"), sem("rows_copied"), sem("item_turned"), sem("item_read")
    table_done, gate_done, scratch_done = sem("table_done"), sem("gate_done"), sem("scratch_done")
    PIECE_RING = 8
    piece_loaded = [sem(f"piece_loaded{r}") for r in range(PIECE_RING)]
    piece_hi, piece_lo_dve, piece_lo_pool = sem("piece_hi"), sem("piece_lo_dve"), sem("piece_lo_pool")
    chain = sem("chain")

    items = []
    for s, (w, kinds) in enumerate(((t["ada_w"], ("shift", "scale", "gate")), (t["ffada_w"], ("shift", "scale", "gate")),
                                    (t["wt_attn"], ("shift", "scale")), (t["wt_ffn"], ("shift", "scale")))):
        items += [(s, kind, w[:, n * D:(n + 1) * D]) for n, kind in enumerate(kinds)]
    BIAS = ("ada_b", "ffada_b", "bt_attn", "bt_ffn")
    pieces = mlp_pieces((t["ssm_w1"], t["bwd_w1"]), (t["ssm_w2"], t["bwd_w2"]))
    turned_before = [sum(kind != "gate" for _, kind, _ in items[:n]) for n in range(len(items) + 1)]
    row_vectors = (t["ada_b"][2 * D:3 * D], t["ffada_b"][2 * D:3 * D], t["ssm_b2"], t["bwd_b2"], t["ff_b2"])

    with ExitStack() as local:
        sb = lambda name, shape, dt: local.enter_context(nc.sbuf_tensor("pro_" + name, shape, dt))
        ps = lambda name, shape: local.enter_context(nc.psum_tensor("pro_" + name, shape, F32))
        cond = sb("cond", [B, D], F32)
        vec_rows = sb("vec_rows", [P, P], F32)
        mask_u8 = sb("mask_u8", [B, P], U8)
        mask_f = sb("mask_f", [B, P], F32)
        condT = sb("condT", [P, KC, B], F32)
        siluT = sb("siluT", [P, KC, B], F32)
        ada = sb("ada", [P, ADA_RING, KC, D], F32)
        stage = sb("stage", [P, PIECE_RING, PIECE], F32)
        tables = sb("tables", [P, 4, 2, KC, B], F32)
        result = sb("result", [P, len(items), KC, B], F32)
        scratch = sb("scratch", [P, 2, 2, KC, B], F32)
        rows = sb("rows", [B, 2, D], F32)
        row_sb = sb("row_sb", [B, len(row_vectors), D], F32)
        gates = sb("gates", [B, 2, 2, D], F32)
        cond_ps = ps("cond_ps", [P, 512])
        vec_ps = ps("vec_ps", [P, 512])
        item_ps = ps("item_ps", [P, 2, 512])
        turn_ps = ps("turn_ps", [P, 2, 512])

        block = local.enter_context(nc.Block())

        @block.sync
        def _(sp):
            sp.dma_start(cond[:, :], t["cond"]).then_inc(cond_loaded, 16)

            def load_item(n):
                if n >= ADA_RING:
                    sp.wait_ge(ada_done, n - ADA_RING + 1)
                source = items[n][2].rearrange("(k p) n -> p k n", p=P)
                sp.dma_start(ada[:, n % ADA_RING, :, :], source).then_inc(ada_loaded[n % ADA_RING], 16)

            def load_piece(q):
                if q >= PIECE_RING:
                    sp.wait_ge(piece_lo_pool if q % 2 else piece_lo_dve, (q - PIECE_RING) // 2 + 1)
                sp.dma_start(stage[:, q % PIECE_RING, :], pieces[q][0]).then_inc(piece_loaded[q % PIECE_RING], 16)

            for n in range(len(items)):
                load_item(n)
                for q in range(2 * n, min(2 * n + 2, len(pieces))):
                    load_piece(q)
            sp.wait_ge(table_done, 4)
            sp.dma_start(sh.tables_dram, tables[:, :, :, :, :].rearrange("p s a k b -> p (s a k b)")).then_inc(scratch_done, 16)
            sp.wait_ge(gate_done, 2)
            for s in range(2):
                sp.dma_start(sh.gates_dram[s], gates[:, s, 0, :]).then_inc(scratch_done, 16)
                sp.dma_start(sh.gate_bias_dram[s], gates[:, s, 1, :]).then_inc(scratch_done, 16)
            sp.wait_ge(scratch_done, 80)

        @block.gpsimd
        def _(pool):
            nc.gpsimd.memset(sh.ident[:, :], 0.0).then_inc(zeroed, 1)
            pool.wait_ge(zeroed, 1)
            nc.gpsimd.affine_select(out=sh.ident[:, :], in_=sh.ident[:, :], compare_op=ALU.not_equal, fill=1.0,
                                    base=0, pattern=[[-1, P]], channel_multiplier=1).then_inc(ident_done, 1)
            nc.gpsimd.memset(sh.neg_half[:, :], -0.5)
            pool.dma_start(mask_u8[:, :], t["mask"]).then_inc(mask_loaded, 16)
            for r, vector in enumerate(row_vectors):
                pool.dma_start(row_sb[:, r, :], vector.rearrange("(a n) -> a n", a=1).to_broadcast([B, D])).then_inc(row_loaded, 16)
            for q in range(1, len(pieces), 2):
                at = pieces[q][1]
                pool.wait_ge(piece_hi, q + 1)
                nc.gpsimd.tensor_tensor(sh.w[0][:, LO, at:at + PIECE], stage[:, q % PIECE_RING, :],
                                        f32(sh.w[0][:, HI, at:at + PIECE]), ALU.subtract).then_inc(piece_lo_pool, 1)

        @block.scalar
        def _(act):
            for name, (row, count) in VEC_ROWS.items():
                vector = t[name][0:count * P].rearrange("(c p) -> c p", p=P)
                act.dma_start(vec_rows[row:row + count, :], vector).then_inc(vec_loaded, 16)
            act.wait_ge(cond_copied, 1)
            nc.scalar.activation(siluT[:, :, :], condT[:, :, :], ACT.Silu).then_inc(silu_done, 1)
            for q in range(len(pieces)):
                at = pieces[q][1]
                act.wait_ge(piece_loaded[q % PIECE_RING], 16 * (q // PIECE_RING + 1))
                nc.scalar.activation(sh.w[0][:, HI, at:at + PIECE], stage[:, q % PIECE_RING, :], ACT.Copy).then_inc(piece_hi, 1)

        @block.tensor
        def _(pe):
            def item_product(n):
                cond_in = siluT if items[n][0] < 2 else condT
                if n >= 2:
                    pe.wait_ge(rows_copied, n - 1)
                pe.wait_ge(ada_loaded[n % ADA_RING], 16 * (n // ADA_RING + 1))
                for k in range(KC):
                    last = nc.tensor.matmul(item_ps[0:B, n % 2, :], cond_in[:, k, :], ada[:, n % ADA_RING, k, :], start=k == 0, stop=k == KC - 1)
                last.then_inc(ada_done, 1)

            def item_turn(n):
                if items[n][1] == "gate":
                    return
                turn = turned_before[n]
                pe.wait_ge(rows_copied, n + 1)
                if turn >= 2:
                    pe.wait_ge(item_read, turn - 1)
                for k in range(KC):
                    last = nc.tensor.transpose(turn_ps[:, turn % 2, k * B:(k + 1) * B], rows[:, n % 2, k * P:(k + 1) * P], sh.ident[0:B, 0:B])
                last.then_inc(item_turned, 1)

            pe.wait_ge(ident_done, 1)
            pe.wait_ge(cond_loaded, 16)
            for k in range(KC):
                last = nc.tensor.transpose(cond_ps[:, k * B:(k + 1) * B], cond[:, k * P:(k + 1) * P], sh.ident[0:B, 0:B])
            last.then_inc(cond_turned, 1)
            pe.wait_ge(vec_loaded, 16 * len(VEC_ROWS))
            nc.tensor.transpose(vec_ps[:, 0:N_VEC], vec_rows[0:N_VEC, :], sh.ident[0:N_VEC, 0:N_VEC]).then_inc(vec_turned, 1)
            pe.wait_ge(silu_done, 1)
            item_product(0)
            for n in range(1, len(items)):
                item_product(n)
                item_turn(n - 1)
            item_turn(len(items) - 1)
            pe.wait_ge(mask_f_done, 1)
            nc.tensor.transpose(vec_ps[:, P:P + B], mask_f[:, :], sh.ident[0:B, 0:B]).then_inc(mask_turned, 1)

        @block.vector
        def _(dve):
            done = [0]

            def link(ins):
                done[0] += 1
                ins.then_inc(chain, 1)
                dve.wait_ge(chain, done[0])

            def vec(name, part=0):
                row = VEC_ROWS[name][0] + KC * part
                return sh.vecs[:, row:row + KC].unsqueeze(2).to_broadcast([P, KC, B])

            def split_piece(q):
                at = pieces[q][1]
                dve.wait_ge(piece_hi, q + 1)
                nc.vector.tensor_tensor(sh.w[0][:, LO, at:at + PIECE], stage[:, q % PIECE_RING, :],
                                        f32(sh.w[0][:, HI, at:at + PIECE]), ALU.subtract).then_inc(piece_lo_dve, 1)

            def copy_rows(n):
                s, kind, _ = items[n]
                dve.wait_ge(ada_done, n + 1)
                if kind == "gate":
                    gate = gates[:, s, 0, :]
                    nc.vector.tensor_tensor(gate, item_ps[0:B, n % 2, :], row_sb[:, s, :], ALU.add).then_inc(rows_copied, 1)
                    dve.wait_ge(rows_copied, n + 1)
                    nc.vector.tensor_tensor(gates[:, s, 1, :], gate, row_sb[:, 2 + 2 * s, :], ALU.mult).then_inc(gate_done, 1)
                    return
                if turned_before[n] >= 2:
                    dve.wait_ge(item_turned, turned_before[n] - 1)
                nc.vector.tensor_copy(rows[:, n % 2, :], item_ps[0:B, n % 2, :]).then_inc(rows_copied, 1)

            def finish_item(n):
                s, kind, _ = items[n]
                if kind == "gate":
                    return
                turn = turned_before[n]
                raw = result[:, n, :, :]
                dve.wait_ge(item_turned, turn + 1)
                nc.vector.tensor_copy(raw, turn_ps[:, turn % 2, 0:KC * B].rearrange("p (m b) -> p m b", m=KC)).then_inc(item_read, 1)
                dve.wait_ge(item_read, turn + 1)
                scale_tab, shift_tab = tables[:, s, 0, :, :], tables[:, s, 1, :, :]
                if kind == "shift":
                    link(nc.vector.tensor_tensor(shift_tab, raw, vec(BIAS[s], 0), ALU.add))
                elif s < 2:
                    nc.vector.scalar_tensor_tensor(out=scale_tab, in0=raw, scalar=1.0, in1=vec(BIAS[s], 1),
                                                   op0=ALU.add, op1=ALU.add).then_inc(table_done, 1)
                else:
                    ln = ("ln1", "ln2")[s - 2]
                    scaled, shifted = scratch[:, s - 2, 0, :, :], scratch[:, s - 2, 1, :, :]
                    link(nc.vector.scalar_tensor_tensor(out=scaled, in0=raw, scalar=1.0, in1=vec(BIAS[s], 1), op0=ALU.add, op1=ALU.add))
                    link(nc.vector.tensor_tensor(scale_tab, scaled, vec(ln + "_w"), ALU.mult))
                    link(nc.vector.tensor_tensor(shifted, scaled, vec(ln + "_b"), ALU.mult))
                    nc.vector.tensor_tensor(shift_tab, shift_tab, shifted, ALU.add).then_inc(table_done, 1)

            dve.wait_ge(cond_turned, 1)
            nc.vector.tensor_copy(condT[:, :, :], cond_ps[:, 0:KC * B].rearrange("p (k b) -> p k b", k=KC)).then_inc(cond_copied, 1)
            dve.wait_ge(mask_loaded, 16)
            nc.vector.tensor_scalar(mask_f[:, :], mask_u8[:, :], 0.0, None, ALU.not_equal).then_inc(mask_f_done, 1)
            dve.wait_ge(vec_turned, 1)
            link(nc.vector.tensor_copy(sh.vecs[:, :], vec_ps[:, 0:N_VEC]))
            dve.wait_ge(row_loaded, 16 * len(row_vectors))
            link(nc.vector.tensor_tensor(row_sb[:, 2, :], row_sb[:, 2, :], row_sb[:, 3, :], ALU.add))
            for n in range(len(items)):
                copy_rows(n)
                if n:
                    finish_item(n - 1)
                if 2 * n < len(pieces):
                    split_piece(2 * n)
            finish_item(len(items) - 1)
            dve.wait_ge(mask_turned, 1)
            nc.vector.tensor_copy(sh.mask[:, :], vec_ps[:, P:P + B])



TPB = 4
NBLK = B // TPB
TOK = TPB * P


class Stage:

    def __init__(self, source, target, tiles, bias1, func, eps, table, gate=None, bias2=None, masked=False,
                 prefetch=(), prefetch_region=0):
        self.source = source.rearrange("(n p) d -> n p d", p=P)
        self.target = target.rearrange("(n p) d -> n p d", p=P)
        self.tiles, self.bias1, self.func, self.eps, self.table = tiles, bias1, func, eps, table
        self.gate, self.bias2, self.masked = gate, bias2, masked
        self.prefetch, self.prefetch_region = prefetch, prefetch_region


def mlp_phase(nc, sh, name, stages, *, chunks, second_half_first=False):
    sem = lambda what: sh.semaphore(nc, f"{name}_{what}")
    gated = stages[0].gate is not None
    x_loaded = [sem(f"x_loaded{tile}") for tile in range(TPB)]
    stored = [sem(f"stored{tile}") for tile in range(TPB)]
    gate_loaded, table_loaded, bias_loaded = sem("gate_loaded"), sem("table_loaded"), sem("bias_loaded")
    passed = sem("passed")
    raw_stats, stats_done, var_done, rstd_done, rstd_masked = (
        sem("raw_stats"), sem("stats_done"), sem("var_done"), sem("rstd_done"), sem("rstd_masked"))
    xhat_ready, turned, modulated, xhi_done, xn_ready = (
        sem("xhat_ready"), sem("turned"), sem("modulated"), sem("xhi_done"), sem("xn_ready"))
    m1_done, act_done, hhi_done, h_ready, m2_done = (
        sem("m1_done"), sem("act_done"), sem("hhi_done"), sem("h_ready"), sem("m2_done"))
    y_done, x_final, y_scaled, bias_masked, bias_added = (
        sem("y_done"), sem("x_final"), sem("y_scaled"), sem("bias_masked"), sem("bias_added"))
    STAGE_RING = 4 if second_half_first else 1
    piece_loaded = [sem(f"piece_loaded{r}") for r in range(STAGE_RING)]
    piece_hi, piece_done = sem("piece_hi"), sem("piece_done")
    total = NBLK * len(stages)

    with ExitStack() as local:
        sb = lambda what, shape, dt: local.enter_context(nc.sbuf_tensor(f"{name}_{what}", shape, dt))
        ps = lambda what, shape: local.enter_context(nc.psum_tensor(f"{name}_{what}", shape, F32))
        x = sb("x", [P, 2, TPB, D], F32)
        xhat = sb("xhat", [P, D], F32)
        xmod = sb("xmod", [P, KC, P], F32)
        xn = sb("xn", [P, 2, 2, KC, TOK], F32R)
        g = sb("g", [P, TOK], F32)
        h = sb("h", [P, 2, 2, TOK], F32R)
        bias = sb("bias", [P, D], F32)
        if gated:
            tmp = sb("tmp", [P, D], F32)
            gate_bc = sb("gate", [P, TPB, D], F32)
        table_sb = sb("table", [P, 2, KC, B], F32)
        bn = sb("bn", [P, TPB, 6], F32)
        mv = sb("mv", [P, TPB, 2], F32)
        var_eps = sb("var_eps", [P, TPB], F32)
        rstd = sb("rstd", [P, TPB], F32)
        rstd_m = sb("rstd_m", [P, TPB], F32)
        stage = sb("stage", [P, STAGE_RING, PIECE], F32)
        y_ps = ps("y", [P, TPB, D])
        m1_ps = ps("m1", [P, 2, TOK])
        turn_ps = ps("turn", [P, 2, KC * P])

        def schedule(eng, first, block_step):
            first()
            for s, st in enumerate(stages):
                base = NBLK * s
                block_step(base, 0, stages[max(s - 1, 0)], st, st)
                with eng.Fori(0, NBLK // 2 - 1) as i:
                    block_step(2 * i + (base + 1), 1, st, st, st)
                    block_step(2 * i + (base + 2), 0, st, st, st)
                block_step(base + NBLK - 1, 1, st, st, stages[s + 1] if s + 1 < len(stages) else None)

        def batch_row(st, n, tile):
            return TPB * n + tile - B * stages.index(st)

        TURN_STEP = 2

        block = local.enter_context(nc.Block())

        @block.sync
        def _(sp):
            def load_x(st, n, parity, tile):
                sp.dma_start(x[:, parity, tile, :], st.source[batch_row(st, n, tile)]).then_inc(x_loaded[tile], 16)

            def store(st, n, parity, tile):
                sp.wait_ge(x_final, TPB * n + tile + 1)
                sp.sem_inc(passed, 1)
                sp.dma_start(st.target[batch_row(st, n, tile)], x[:, parity, tile, :]).then_inc(stored[tile], 16)

            def load_gate(st, n):
                row = sh.gates_dram[st.gate].rearrange("(n t) d -> n (t d)", t=TPB)[bass.ds(n - NBLK * stages.index(st), 1), :]
                sp.dma_start(gate_bc[:, :, :].rearrange("p t d -> p (t d)"), row.to_broadcast([P, TPB * D])).then_inc(gate_loaded, 16)

            def load_table(st):
                sp.dma_start(table_sb[:, :, :, :].rearrange("p a k b -> p (a k b)"),
                             sh.tables_dram[:, st.table * 2 * KC * B:(st.table + 1) * 2 * KC * B]).then_inc(table_loaded, 16)

            def first():
                for tile in range(TPB):
                    load_x(stages[0], 0, 0, tile)
                load_table(stages[0])
                if gated:
                    load_gate(stages[0], 0)

            def block_step(n, parity, before, st, after):
                if isinstance(n, int) and n == 0:
                    for tile in range(TPB):
                        sp.wait_ge(stats_done, tile + 1)
                        load_x(after, 1, 1, tile)
                    return
                if after is not None and after is not st:
                    sp.wait_ge(modulated, TPB * (n + 1))
                    load_table(after)

                def load_next(tile):
                    if after is not None:
                        sp.wait_ge(stored[tile], 16 * n)
                        sp.sem_inc(passed, 1)
                        load_x(after, n + 1, 1 - parity, tile)

                store(before, n - 1, 1 - parity, 0)
                store(before, n - 1, 1 - parity, 1)
                load_next(0)
                store(before, n - 1, 1 - parity, 2)
                load_next(1)
                store(before, n - 1, 1 - parity, 3)
                if gated:
                    load_gate(st, n)
                load_next(2)
                load_next(3)

            schedule(sp, first, block_step)
            for tile in range(TPB):
                store(stages[-1], total - 1, 1, tile)
            for tile in range(TPB):
                sp.wait_ge(stored[tile], 16 * total)

        @block.gpsimd
        def _(pool):
            def rstd_of(n, tile):
                pool.wait_ge(var_done, TPB * n + tile + 1)
                if n:
                    pool.wait_ge(xhat_ready, TPB * (n - 1) + tile + 1)
                nc.gpsimd.tensor_tensor(rstd[:, tile:tile + 1], var_eps[:, tile:tile + 1], sh.neg_half[:, 0:1], ALU.pow).then_inc(rstd_done, 1)

            def add_bias(st, n, tile):
                row, added = batch_row(st, n, tile), TPB * n + tile
                xt = x[:, n % 2, tile, :]
                if not gated:
                    nc.gpsimd.tensor_tensor(xt, xt, bias[:, :], ALU.add).then_inc(bias_added, 1)
                    return
                if added:
                    pool.wait_ge(bias_added, added)
                pool.dma_start(bias[:, :], sh.gate_bias_dram[st.gate][row:row + 1, :].to_broadcast([P, D])).then_inc(bias_loaded, 16)
                pool.wait_ge(bias_loaded, 16 * (added + 1))
                if st.masked:
                    nc.gpsimd.tensor_scalar(bias[:, :], bias[:, :], sh.mask[:, row:row + 1], 1.0, ALU.mult, ALU.mult).then_inc(bias_masked, 1)
                    pool.wait_ge(bias_masked, added + 1)
                nc.gpsimd.tensor_tensor(xt, xt, bias[:, :], ALU.add).then_inc(bias_added, 1)

            def load_piece(st, q):
                if q >= STAGE_RING:
                    pool.wait_ge(piece_done, q - STAGE_RING + 1)
                pool.dma_start(stage[:, q % STAGE_RING, :], st.prefetch[q % len(st.prefetch)][0]).then_inc(piece_loaded[q % STAGE_RING], 16)

            for tile in range(TPB):
                rstd_of(0, tile)
            if not gated:
                pool.dma_start(bias[:, :], stages[0].bias2.rearrange("(a n) -> a n", a=1).to_broadcast([P, D])).then_inc(bias_loaded, 16)
                pool.wait_ge(bias_loaded, 16)
            for q in range(STAGE_RING):
                load_piece(stages[0], q)
            for n in range(total):
                st = stages[n // NBLK]
                pool.wait_ge(xhat_ready, TPB * (n + 1))
                if not second_half_first:
                    load_piece(st, 2 * n + 1)
                for tile in range(TPB):
                    if second_half_first and n == 0:
                        load_piece(st, STAGE_RING + 2 * tile)
                        load_piece(st, STAGE_RING + 2 * tile + 1)
                    if n + 1 < total:
                        rstd_of(n + 1, tile)
                    add_bias(st, n, tile)
                if not second_half_first and n + 1 < total:
                    load_piece(stages[(n + 1) // NBLK], 2 * n + 2)
                if second_half_first and n == 0:
                    for q in range(STAGE_RING + 2 * TPB, len(st.prefetch)):
                        load_piece(st, q)

        @block.tensor
        def _(pe):
            def turn(n, tile):
                pe.wait_ge(xhat_ready, TPB * n + tile + 1)
                if not (isinstance(n, int) and n == 0 and tile < 2):
                    pe.wait_ge(modulated, TPB * n + tile - 1)
                for k in range(KC):
                    last = nc.tensor.transpose(turn_ps[:, tile % 2, k * P:(k + 1) * P], xhat[:, k * P:(k + 1) * P], sh.ident[:, :])
                last.then_inc(turned, 1)

            def first_product(st, n, parity, c):
                if c == 0:
                    pe.wait_ge(xn_ready, TPB * (n + 1))
                if not (isinstance(n, int) and n == 0 and c < 2):
                    pe.wait_ge(act_done, chunks * n + c - 1)
                if second_half_first and isinstance(n, int) and n == 0 and c == HID // P:
                    pe.wait_ge(piece_done, 2 * KC)
                if not second_half_first and isinstance(n, int) and n == NBLK * stages.index(st) and n and c == 0:
                    pe.wait_ge(piece_done, 2 * n)
                steps = [(k, a, b) for k in range(KC) for a, b in MUL_HI_LO]
                for s, (k, a, b) in enumerate(steps):
                    last = nc.tensor.matmul(m1_ps[:, c % 2, :], st.tiles[0](a, k, c), xn[:, parity, b, k, :],
                                            start=s == 0, stop=s == len(steps) - 1)
                last.then_inc(m1_done, 1)

            def second_product(st, n, c):
                if second_half_first and isinstance(n, int) and n == 0 and c >= HID // P:
                    pe.wait_ge(piece_done, 2 * KC + c - HID // P + 1)
                pe.wait_ge(h_ready, chunks * n + c + 1)
                for tile in range(TPB):
                    if c == 0 and not (isinstance(n, int) and n == 0):
                        if gated:
                            pe.wait_ge(y_scaled, TPB * (n - 1) + tile + 1)
                        else:
                            pe.wait_ge(x_final, TPB * (n - 1) + tile + 1)
                    for s, (a, b) in enumerate(MUL_HI_LO):
                        last = nc.tensor.matmul(y_ps[:, tile, :], h[:, c % 2, a, tile * P:(tile + 1) * P], st.tiles[1](b, c),
                                                start=c == 0 and s == 0, stop=c == chunks - 1 and s == 2)
                    if c == chunks - 1:
                        last.then_inc(y_done, 1)
                if c < chunks - 1:
                    last.then_inc(m2_done, 1)

            def first():
                for tile in range(TPB):
                    turn(0, tile)

            def block_step(n, parity, before, st, after):
                first_product(st, n, parity, 0)
                for c in range(chunks):
                    if c + 1 < chunks:
                        first_product(st, n, parity, c + 1)
                    second_product(st, n, c)
                    if after is not None and TURN_STEP <= c < TURN_STEP + TPB:
                        turn(n + 1, c - TURN_STEP)

            schedule(pe, first, block_step)

        @block.scalar
        def _(act):
            def modulate(st, n, tile):
                row = batch_row(st, n, tile)
                act.wait_ge(turned, TPB * n + tile + 1)
                if isinstance(n, int) and row == 0:
                    act.wait_ge(table_loaded, 16 * (stages.index(st) + 1))
                if not (isinstance(n, int) and n == 0 and tile == 0):
                    act.wait_ge(xn_ready, TPB * n + tile)
                for k in range(KC):
                    last = nc.scalar.activation(xmod[:, k, :], turn_ps[:, tile % 2, k * P:(k + 1) * P], ACT.Identity,
                                                bias=table_sb[:, 1, k, bass.ds(row, 1)], scale=table_sb[:, 0, k, bass.ds(row, 1)])
                last.then_inc(modulated, 1)

            def activate(st, n, c):
                act.wait_ge(m1_done, chunks * n + c + 1)
                if not (isinstance(n, int) and n == 0 and c == 0):
                    act.wait_ge(h_ready, chunks * n + c)
                nc.scalar.activation(g[:, :], m1_ps[:, c % 2, :], st.func, bias=st.bias1(c)).then_inc(act_done, 1)

            def piece_high(st, q, at, slot, turns):
                act.wait_ge(piece_loaded[slot], 16 * (turns + 1))
                nc.scalar.activation(sh.w[st.prefetch_region][:, HI, bass.ds(at, PIECE)], stage[:, slot, :], ACT.Copy).then_inc(piece_hi, 1)

            def first():
                for tile in range(TPB):
                    modulate(stages[0], 0, tile)

            def block_step(n, parity, before, st, after):
                activate(st, n, 0)
                for c in range(chunks):
                    if c + 1 < chunks:
                        activate(st, n, c + 1)
                    if after is not None and TURN_STEP <= c < TURN_STEP + TPB:
                        modulate(after, n + 1, c - TURN_STEP)
                    if second_half_first and isinstance(n, int) and n == 0 and 2 * c < len(st.prefetch):
                        for q in (2 * c, 2 * c + 1):
                            piece_high(st, q, st.prefetch[q][1], q % STAGE_RING, q // STAGE_RING)
                    if not second_half_first and c in (0, chunks - 1):
                        q = 2 * n + (c > 0)
                        local_n = n - NBLK * stages.index(st)
                        piece_high(st, q, (2 * local_n + (c > 0)) * PIECE, 0, q)

            schedule(act, first, block_step)

        @block.vector
        def _(dve):
            def stats(st, n, parity, tile):
                row = TPB * n + tile
                dve.wait_ge(x_loaded[tile], 16 * (n + 1))
                nc.vector.bn_stats(bn[:, tile, :], x[:, parity, tile, :]).then_inc(raw_stats, 1)
                dve.wait_ge(raw_stats, row + 1)
                dve.sem_inc(passed, 1)
                nc.vector.bn_aggr(mv[:, tile, :], bn[:, tile, :]).then_inc(stats_done, 1)
                dve.wait_ge(stats_done, row + 1)
                nc.vector.tensor_scalar(var_eps[:, tile:tile + 1], mv[:, tile, 1:2], st.eps, None, ALU.add).then_inc(var_done, 1)

            def normalise(st, n, parity, tile):
                row = TPB * n + tile
                dve.wait_ge(rstd_done, row + 1)
                r = rstd[:, tile:tile + 1]
                if st.masked:
                    nc.vector.tensor_tensor(rstd_m[:, tile:tile + 1], r, sh.mask[:, bass.ds(row, 1)], ALU.mult).then_inc(rstd_masked, 1)
                    dve.wait_ge(rstd_masked, row + 1)
                    r = rstd_m[:, tile:tile + 1]
                if not (isinstance(n, int) and row == 0):
                    dve.wait_ge(turned, row)
                nc.vector.tensor_scalar(xhat[:, :], x[:, parity, tile, :], mv[:, tile, 0:1], r,
                                        ALU.subtract, ALU.mult).then_inc(xhat_ready, 1)

            def split_xn(n, parity, tile):
                dve.wait_ge(modulated, TPB * n + tile + 1)
                hi = xn[:, parity, HI, :, tile * P:(tile + 1) * P]
                nc.vector.tensor_copy(hi, xmod[:, :, :]).then_inc(xhi_done, 1)
                dve.wait_ge(xhi_done, TPB * n + tile + 1)
                nc.vector.tensor_tensor(xn[:, parity, LO, :, tile * P:(tile + 1) * P], xmod[:, :, :], f32(hi),
                                        ALU.subtract).then_inc(xn_ready, 1)

            def split_h(n, c):
                dve.wait_ge(act_done, chunks * n + c + 1)
                if c >= 2 or (c == 0 and not (isinstance(n, int) and n == 0)):
                    dve.wait_ge(m2_done, (chunks - 1) * n + max(c - 1, 0))
                elif not (isinstance(n, int) and n == 0):
                    dve.wait_ge(y_done, TPB * n)
                nc.vector.tensor_copy(h[:, c % 2, HI, :], g[:, :]).then_inc(hhi_done, 1)
                dve.wait_ge(hhi_done, chunks * n + c + 1)
                nc.vector.tensor_tensor(h[:, c % 2, LO, :], g[:, :], f32(h[:, c % 2, HI, :]), ALU.subtract).then_inc(h_ready, 1)

            def finish(st, n, parity, tile):
                row = TPB * n + tile
                xt = x[:, parity, tile, :]
                dve.wait_ge(y_done, row + 1)
                if tile == 0 and gated:
                    dve.wait_ge(gate_loaded, 16 * (n + 1))
                if not gated:
                    dve.wait_ge(bias_added, row + 1)
                    nc.vector.tensor_tensor(xt, y_ps[:, tile, :], xt, ALU.add).then_inc(x_final, 1)
                    return
                if not (isinstance(n, int) and row == 0):
                    dve.wait_ge(x_final, row)
                if st.masked:
                    nc.vector.scalar_tensor_tensor(out=tmp[:, :], in0=y_ps[:, tile, :], scalar=sh.mask[:, bass.ds(row, 1)],
                                                   in1=gate_bc[:, tile, :], op0=ALU.mult, op1=ALU.mult).then_inc(y_scaled, 1)
                else:
                    nc.vector.tensor_tensor(tmp[:, :], y_ps[:, tile, :], gate_bc[:, tile, :], ALU.mult).then_inc(y_scaled, 1)
                dve.wait_ge(y_scaled, row + 1)
                dve.wait_ge(bias_added, row + 1)
                nc.vector.tensor_tensor(xt, xt, tmp[:, :], ALU.add).then_inc(x_final, 1)

            def piece_low(st, q, at, slot):
                w = sh.w[st.prefetch_region]
                dve.wait_ge(piece_hi, q + 1)
                nc.vector.tensor_tensor(w[:, LO, bass.ds(at, PIECE)], stage[:, slot, :],
                                        f32(w[:, HI, bass.ds(at, PIECE)]), ALU.subtract).then_inc(piece_done, 1)

            def first():
                for tile in range(TPB):
                    stats(stages[0], 0, 0, tile)
                for tile in range(TPB):
                    normalise(stages[0], 0, 0, tile)
                    if tile:
                        split_xn(0, 0, tile - 1)
                split_xn(0, 0, TPB - 1)

            def block_step(n, parity, before, st, after):
                for c in range(chunks):
                    split_h(n, c)
                    if c == 0 and not (isinstance(n, int) and n == 0):
                        finish(before, n - 1, 1 - parity, TPB - 1)
                    if after is not None:
                        if TURN_STEP + 1 <= c <= TURN_STEP + TPB:
                            split_xn(n + 1, 1 - parity, c - TURN_STEP - 1)
                        if TURN_STEP - 1 <= c < TURN_STEP - 1 + TPB:
                            stats(after, n + 1, 1 - parity, c - TURN_STEP + 1)
                        if TURN_STEP <= c < TURN_STEP + TPB:
                            normalise(after, n + 1, 1 - parity, c - TURN_STEP)
                    if second_half_first and isinstance(n, int) and n == 0 and 2 * c < len(st.prefetch):
                        for q in (2 * c, 2 * c + 1):
                            piece_low(st, q, st.prefetch[q][1], q % STAGE_RING)
                    if not second_half_first and c in (0, chunks - 1):
                        piece_low(st, 2 * n + (c > 0), (2 * (n - NBLK * stages.index(st)) + (c > 0)) * PIECE, 0)
                for tile in range(TPB - 1):
                    finish(st, n, parity, tile)

            schedule(dve, first, block_step)
            finish(stages[-1], total - 1, 1, TPB - 1)



TPP = 2
NPAIR = B // TPP
PT = TPP * P
HALF = HEADS // 2


def attention_phase(nc, sh, *, source, target, bo, eps, table, prefetch, prefetch_region):
    sem = lambda what: sh.semaphore(nc, "att_" + what)
    x_loaded = [sem(f"x_loaded{tile}") for tile in range(TPP)]
    residual_loaded = [sem(f"residual_loaded{tile}") for tile in range(TPP)]
    stored = [sem(f"stored{tile}") for tile in range(TPP)]
    const_loaded = sem("const_loaded")
    passed = sem("passed")
    bv_hi, bv_ready, bvo_done, bo_ready = sem("bv_hi"), sem("bv_ready"), sem("bvo_done"), sem("bo_ready")
    raw_stats, stats_done, var_done, rstd_done = sem("raw_stats"), sem("stats_done"), sem("var_done"), sem("rstd_done")
    xhat_ready, turned, modulated, xhi_done, xn_ready = (
        sem("xhat_ready"), sem("turned"), sem("modulated"), sem("xhi_done"), sem("xn_ready"))
    kq_done, kq_hi, kq_ready, v_done, v_ready = sem("kq_done"), sem("kq_hi"), sem("kq_ready"), sem("v_done"), sem("v_ready")
    diag_zeroed, diag_loaded = sem("diag_zeroed"), sem("diag_loaded")
    scores_done, max_done, negmax_done, exp_done, inv_done, probs_ready = (
        sem("scores_done"), sem("max_done"), sem("negmax_done"), sem("exp_done"), sem("inv_done"), sem("probs_ready"))
    probs_turned, probsT_ready, out_part = sem("probs_turned"), sem("probsT_ready"), sem("out_part")
    out_hi, out_ready = sem("out_hi"), sem("out_ready")
    proj_done, x_final, bias_added = sem("proj_done"), sem("x_final"), sem("bias_added")
    piece_loaded, piece_hi, piece_done = sem("piece_loaded"), sem("piece_hi"), sem("piece_done")
    scale = float(HD) ** -0.5
    W = sh.w[0]

    def weight(part, matrix, k):
        at = (matrix * KC + k) * D
        return W[:, part, at:at + D]

    WK, WQ, WV, WO = range(4)

    with ExitStack() as local:
        sb = lambda what, shape, dt: local.enter_context(nc.sbuf_tensor("att_" + what, shape, dt))
        x = sb("x", [P, TPP, D], F32)
        residual = sb("residual", [P, TPP, D], F32)
        xmod = sb("xmod", [P, TPP, KC, P], F32)
        xn = sb("xn", [P, 2, KC, PT], F32R)
        q = sb("q", [P, 2, KC, PT], F32R)
        kst = sb("kst", [P, 2, KC, PT], F32R)
        kdiag = sb("kdiag", [P, 2, KC, HPC * P], F32R)
        v = sb("v", [P, TPP, D], F32)
        probs = sb("probs", [P, HEADS, P], F32)
        probsT = sb("probsT", [P, 2, HPC * P], F32)
        oT = sb("oT", [P, 2, KC, P], F32R)
        bo_bc = sb("bo", [P, D], F32)
        table_sb = sb("table", [P, 2, KC, B], F32)
        bn = sb("bn", [P, 6], F32)
        mv = sb("mv", [P, TPP, 2], F32)
        var_eps = sb("var_eps", [P, TPP], F32)
        rstd = sb("rstd", [P, TPP], F32)
        smax = sb("smax", [P, HEADS], F32)
        negmax = sb("negmax", [P, HEADS], F32)
        rowsum = sb("rowsum", [P, HEADS], F32)
        inv = sb("inv", [P, HEADS], F32)
        stage = sb("stage", [P, PIECE], F32)
        s_ps = local.enter_context(nc.psum_tensor("att_s", [P, HEADS, P], F32))
        bank_ps = local.enter_context(nc.psum_tensor("att_banks", [P, 3, 512], F32))
        o_ps = local.enter_context(nc.psum_tensor("att_o", [P, KC, P], F32))
        bank = lambda n: bank_ps[:, n - 4, :]

        source_t = source.rearrange("(n p) d -> n p d", p=P)
        target_t = target.rearrange("(n p) d -> n p d", p=P)

        def schedule(eng, first, pair_step, last_tail):
            first()
            pair_step(0, False, True)
            with eng.Fori(0, NPAIR - 2) as i:
                pair_step(i + 1, True, True)
            pair_step(NPAIR - 1, True, False)
            last_tail()

        def probs_bank(tile, m):
            return 6 if m % 2 == 0 else 4 + tile

        def is_first(row):
            return isinstance(row, int) and row == 0

        block = local.enter_context(nc.Block())

        @block.sync
        def _(sp):
            def load_x(n, tile):
                sp.dma_start(x[:, tile, :], source_t[TPP * n + tile]).then_inc(x_loaded[tile], 16)

            def load_residual(n, tile):
                sp.dma_start(residual[:, tile, :], source_t[TPP * n + tile]).then_inc(residual_loaded[tile], 16)

            def diag(n, tile):
                sp.wait_ge(kq_ready, 2 * KC * n + KC)
                sp.sem_inc(passed, 1)
                if is_first(TPP * n + tile):
                    sp.wait_ge(diag_zeroed, 1)
                else:
                    sp.wait_ge(scores_done, 2 * (TPP * n + tile))
                    sp.sem_inc(passed, 1)
                for j in range(HPC):
                    rows = slice(j * HD, (j + 1) * HD)
                    sp.dma_start(f32(kdiag[rows, :, :, j * P:(j + 1) * P]), f32(kst[rows, :, :, tile * P:(tile + 1) * P])).then_inc(diag_loaded, 16)

            def store(n, tile):
                sp.wait_ge(x_final, TPP * n + tile + 1)
                sp.sem_inc(passed, 1)
                sp.dma_start(target_t[TPP * n + tile], residual[:, tile, :]).then_inc(stored[tile], 16)

            def first():
                load_x(0, 0)
                load_x(0, 1)
                sp.dma_start(table_sb[:, :, :, :].rearrange("p a k b -> p (a k b)"),
                             sh.tables_dram[:, table * 2 * KC * B:(table + 1) * 2 * KC * B]).then_inc(const_loaded, 16)
                sp.dma_start(bo_bc[:, :], bo.rearrange("(a n) -> a n", a=1).to_broadcast([P, D])).then_inc(const_loaded, 16)

            def pair_step(n, before, more):
                if more:
                    for tile in range(TPP):
                        sp.wait_ge(turned, TPP * n + tile + 1)
                        sp.sem_inc(passed, 1)
                        load_x(n + 1, tile)
                diag(n, 0)
                if before:
                    store(n - 1, 0)
                    sp.wait_ge(stored[0], 16 * n)
                    sp.sem_inc(passed, 1)
                load_residual(n, 0)
                diag(n, 1)
                if before:
                    store(n - 1, 1)
                    sp.wait_ge(stored[1], 16 * n)
                    sp.sem_inc(passed, 1)
                load_residual(n, 1)

            def last_tail():
                store(NPAIR - 1, 0)
                store(NPAIR - 1, 1)

            schedule(sp, first, pair_step, last_tail)
            for tile in range(TPP):
                sp.wait_ge(stored[tile], 16 * NPAIR)

        @block.gpsimd
        def _(pool):
            def rstd_of(row):
                at = row % TPP
                pool.wait_ge(var_done, row + 1)
                if row >= TPP:
                    pool.wait_ge(xhat_ready, row - TPP + 1)
                nc.gpsimd.tensor_tensor(rstd[:, at:at + 1], var_eps[:, at:at + 1], sh.neg_half[:, 0:1], ALU.pow).then_inc(rstd_done, 1)

            def add_bias(row):
                xt = residual[:, row % TPP, :]
                pool.wait_ge(residual_loaded[row % TPP], 16 * (row // TPP + 1))
                nc.gpsimd.tensor_tensor(xt, xt, bo_bc[:, :], ALU.add).then_inc(bias_added, 1)

            rstd_of(0)
            rstd_of(1)
            nc.gpsimd.memset(f32(kdiag[:, :, :, :]).rearrange("p a k c -> p (a k c)"), 0.0).then_inc(diag_zeroed, 1)
            pool.wait_ge(bo_ready, 1)
            for n in range(NPAIR):
                if n:
                    pool.wait_ge(piece_done, n)
                pool.dma_start(stage[:, :], prefetch[n][0]).then_inc(piece_loaded, 16)
                add_bias(TPP * n)
                if n + 1 < NPAIR:
                    rstd_of(TPP * n + 2)
                    rstd_of(TPP * n + 3)
                add_bias(TPP * n + 1)

        @block.tensor
        def _(pe):
            def product(out, steps):
                for s, (lhs, rhs) in enumerate(steps):
                    last = nc.tensor.matmul(out, lhs, rhs, start=s == 0, stop=s == len(steps) - 1)
                return last

            def turn(n, tile):
                pe.wait_ge(xhat_ready, TPP * n + tile + 1)
                if not is_first(n):
                    pe.wait_ge(v_ready, TPP * (n - 1) + tile + 1)
                for k in range(KC):
                    last = nc.tensor.transpose(bank(4 + tile)[:, k * P:(k + 1) * P], x[:, tile, k * P:(k + 1) * P], sh.ident[:, :])
                last.then_inc(turned, 1)

            def keys_queries(n, u):
                m, matrix = u % KC, (WK, WQ)[u // KC]
                product(bank(5 - u % 2)[:, 0:PT], [(weight(a, matrix, k)[:, m * P:(m + 1) * P], xn[:, b, k, :])
                                                   for k in range(KC) for a, b in MUL_HI_LO]).then_inc(kq_done, 1)

            def scores(n, tile, e):
                row = TPP * n + tile
                if e == 0:
                    pe.wait_ge(diag_loaded, 16 * HPC * (row + 1))
                if tile == 0:
                    pe.wait_ge(kq_ready, 2 * KC * n + KC + 2 * e + 2)
                if not is_first(row):
                    pe.wait_ge(exp_done, 2 * row - 1 + e)
                elif e == 0:
                    pe.wait_ge(bo_ready, 1)
                for m in (2 * e, 2 * e + 1):
                    last = product(s_ps[:, m * HPC:(m + 1) * HPC, :].rearrange("p h k -> p (h k)"),
                                   [(q[:, a, m, tile * P:(tile + 1) * P], kdiag[:, b, m, :]) for a, b in MUL_HI_LO])
                last.then_inc(scores_done, 1)

            def values(n, tile):
                product(bank(4 + tile), [(xn[:, a, k, tile * P:(tile + 1) * P], weight(b, WV, k))
                                         for k in range(KC) for a, b in MUL_HI_LO]).then_inc(v_done, 1)

            def turn_probs(row, tile, m):
                if m % 2 == 0:
                    pe.wait_ge(probs_ready, 2 * row + m // 2 + 1)
                if m >= 2:
                    pe.wait_ge(probsT_ready, KC * row + m - 1)
                for j in range(HPC):
                    last = nc.tensor.transpose(bank(probs_bank(tile, m))[:, j * P:(j + 1) * P], probs[:, m * HPC + j, :], sh.ident[:, :])
                last.then_inc(probs_turned, 1)

            def weigh(row, tile, m):
                if m == 0:
                    pe.wait_ge(v_ready, row + 1)
                    if not is_first(row):
                        pe.wait_ge(out_ready, row)
                pe.wait_ge(probsT_ready, KC * row + m + 1)
                for j in range(HPC):
                    head = m * HPC + j
                    last = nc.tensor.matmul(o_ps[j * HD:(j + 1) * HD, m, :], v[:, tile, head * HD:(head + 1) * HD],
                                            probsT[:, m % 2, j * P:(j + 1) * P], start=True, stop=True)
                last.then_inc(out_part, 1)

            def project(row):
                pe.wait_ge(out_ready, row + 1)
                product(bank(6), [(oT[:, a, k, :], weight(b, WO, k)) for k in range(KC) for a, b in MUL_HI_LO]).then_inc(proj_done, 1)

            def first():
                turn(0, 0)
                turn(0, 1)
                pe.wait_ge(bv_ready, 1)
                product(s_ps[:, 0:HPC, :].rearrange("p h k -> p (h k)"),
                        [(q[:, a, k, 0:P], weight(b, WO, k)) for k in range(KC) for a, b in MUL_HI_LO]).then_inc(bvo_done, 1)

            def pair_step(n, before, more):
                row = TPP * n
                pe.wait_ge(xn_ready, TPP * (n + 1))
                pe.wait_ge(modulated, TPP * (n + 1))
                keys_queries(n, 0)
                if before:
                    pe.wait_ge(probsT_ready, KC * (row - 1))
                else:
                    pe.wait_ge(modulated, 1)
                keys_queries(n, 1)
                for u in range(2, 2 * KC):
                    if u == KC and before:
                        project(row - 2)
                    pe.wait_ge(kq_ready, 2 * KC * n + u - 1)
                    keys_queries(n, u)
                scores(n, 0, 0)
                if before:
                    pe.wait_ge(x_final, row - 1)
                    turn_probs(row - 1, 1, 0)
                    pe.wait_ge(kq_ready, 2 * KC * n + 2 * KC - 1)
                    turn_probs(row - 1, 1, 1)
                scores(n, 0, 1)
                if before:
                    weigh(row - 1, 1, 0)
                    turn_probs(row - 1, 1, 2)
                    weigh(row - 1, 1, 1)
                    turn_probs(row - 1, 1, 3)
                pe.wait_ge(kq_ready, 2 * KC * (n + 1))
                values(n, 0)
                if before:
                    weigh(row - 1, 1, 2)
                    weigh(row - 1, 1, 3)
                values(n, 1)
                if before:
                    project(row - 1)
                if more:
                    turn(n + 1, 0)
                    turn(n + 1, 1)
                scores(n, 1, 0)
                if before:
                    pe.wait_ge(x_final, row)
                turn_probs(row, 0, 0)
                if more:
                    pe.wait_ge(modulated, row + 3)
                else:
                    pe.wait_ge(v_ready, row + 1)
                turn_probs(row, 0, 1)
                scores(n, 1, 1)
                weigh(row, 0, 0)
                turn_probs(row, 0, 2)
                weigh(row, 0, 1)
                turn_probs(row, 0, 3)
                weigh(row, 0, 2)
                weigh(row, 0, 3)

            def last_tail():
                row = B - 1
                project(row - 1)
                pe.wait_ge(x_final, row)
                turn_probs(row, 1, 0)
                pe.wait_ge(v_ready, B)
                turn_probs(row, 1, 1)
                weigh(row, 1, 0)
                turn_probs(row, 1, 2)
                weigh(row, 1, 1)
                turn_probs(row, 1, 3)
                weigh(row, 1, 2)
                weigh(row, 1, 3)
                project(row)

            schedule(pe, first, pair_step, last_tail)

        @block.scalar
        def _(act):
            def modulate(n, tile):
                row = TPP * n + tile
                act.wait_ge(turned, row + 1)
                if not is_first(n):
                    act.wait_ge(xn_ready, row - 1)
                for k in range(KC):
                    last = nc.scalar.activation(xmod[:, tile, k, :], bank(4 + tile)[:, k * P:(k + 1) * P], ACT.Identity,
                                                bias=table_sb[:, 1, k, bass.ds(row, 1)], scale=table_sb[:, 0, k, bass.ds(row, 1)])
                last.then_inc(modulated, 1)

            def copy_probsT(row, tile):
                for m in range(KC):
                    act.wait_ge(probs_turned, KC * row + m + 1)
                    if m >= 2 or not is_first(row):
                        act.wait_ge(out_part, KC * row + m - 1)
                    nc.scalar.activation(probsT[:, m % 2, :], bank(probs_bank(tile, m)), ACT.Copy).then_inc(probsT_ready, 1)

            def exponentials(row):
                for e in range(2):
                    act.wait_ge(negmax_done, 2 * row + e + 1)
                    if not is_first(row):
                        act.wait_ge(probs_turned, KC * row - 2 + 2 * e)
                    for head in range(HALF * e, HALF * (e + 1)):
                        last = nc.scalar.activation(probs[:, head, :], s_ps[:, head, :], ACT.Exp, bias=negmax[:, head:head + 1],
                                                    scale=scale, accum_out=rowsum[:, head:head + 1])
                    last.then_inc(exp_done, 1)

            def first():
                act.wait_ge(const_loaded, 32)
                modulate(0, 0)
                modulate(0, 1)

            def pair_step(n, before, more):
                row = TPP * n
                if before:
                    copy_probsT(row - 1, 1)
                exponentials(row)
                act.wait_ge(piece_loaded, 16 * (n + 1))
                nc.scalar.activation(sh.w[prefetch_region][:, HI, bass.ds(n * PIECE, PIECE)], stage[:, :], ACT.Copy).then_inc(piece_hi, 1)
                if more:
                    modulate(n + 1, 0)
                    modulate(n + 1, 1)
                copy_probsT(row, 0)
                exponentials(row + 1)

            schedule(act, first, pair_step, lambda: copy_probsT(B - 1, 1))

        @block.vector
        def _(dve):
            def vec(name, m):
                row = VEC_ROWS[name][0] + m
                return sh.vecs[:, row:row + 1]

            def stats(n, tile):
                row = TPP * n + tile
                dve.wait_ge(x_loaded[tile], 16 * (n + 1))
                nc.vector.bn_stats(bn[:, :], x[:, tile, :]).then_inc(raw_stats, 1)
                dve.wait_ge(raw_stats, row + 1)
                dve.sem_inc(passed, 1)
                nc.vector.bn_aggr(mv[:, tile, :], bn[:, :]).then_inc(stats_done, 1)
                dve.wait_ge(stats_done, row + 1)
                nc.vector.tensor_scalar(var_eps[:, tile:tile + 1], mv[:, tile, 1:2], eps, None, ALU.add).then_inc(var_done, 1)

            def normalise(n, tile):
                row = TPP * n + tile
                dve.wait_ge(rstd_done, row + 1)
                nc.vector.tensor_scalar(x[:, tile, :], x[:, tile, :], mv[:, tile, 0:1], rstd[:, tile:tile + 1],
                                        ALU.subtract, ALU.mult).then_inc(xhat_ready, 1)

            def split_xn(n, tile):
                row = TPP * n + tile
                dve.wait_ge(modulated, row + 1)
                hi = xn[:, HI, :, tile * P:(tile + 1) * P]
                nc.vector.tensor_copy(hi, xmod[:, tile, :, :]).then_inc(xhi_done, 1)
                dve.wait_ge(xhi_done, row + 1)
                nc.vector.tensor_tensor(xn[:, LO, :, tile * P:(tile + 1) * P], xmod[:, tile, :, :], f32(hi),
                                        ALU.subtract).then_inc(xn_ready, 1)

            def split_kq(n, u):
                m, dst, bias = u % KC, (kst, q)[u // KC], ("bk", "bq")[u // KC]
                src = bank(5 - u % 2)[:, 0:PT]
                dve.wait_ge(kq_done, 2 * KC * n + u + 1)
                if u == 0 and not is_first(n):
                    dve.wait_ge(diag_loaded, 16 * HPC * TPP * n)
                nc.vector.tensor_scalar(dst[:, HI, m, :], src, vec(bias, m), None, ALU.add).then_inc(kq_hi, 1)
                dve.wait_ge(kq_hi, 2 * KC * n + u + 1)
                nc.vector.scalar_tensor_tensor(out=dst[:, LO, m, :], in0=src, scalar=vec(bias, m), in1=f32(dst[:, HI, m, :]),
                                               op0=ALU.add, op1=ALU.subtract).then_inc(kq_ready, 1)

            def row_max(row, e):
                heads = slice(HALF * e, HALF * (e + 1))
                dve.wait_ge(scores_done, 2 * row + e + 1)
                nc.vector.tensor_reduce(smax[:, heads], s_ps[:, heads, :], AX.X, ALU.max).then_inc(max_done, 1)
                dve.wait_ge(max_done, 2 * row + e + 1)
                nc.vector.tensor_scalar(negmax[:, heads], smax[:, heads], -scale, None, ALU.mult).then_inc(negmax_done, 1)

            def divide(row, e):
                heads = slice(HALF * e, HALF * (e + 1))
                dve.wait_ge(exp_done, 2 * row + e + 1)
                nc.vector.reciprocal(inv[:, heads], rowsum[:, heads]).then_inc(inv_done, 1)
                dve.wait_ge(inv_done, 2 * row + e + 1)
                nc.vector.tensor_tensor(probs[:, heads, :], probs[:, heads, :], inv[:, heads].unsqueeze(2).to_broadcast([P, HALF, P]),
                                        ALU.mult).then_inc(probs_ready, 1)

            def copy_values(n, tile):
                dve.wait_ge(v_done, TPP * n + tile + 1)
                nc.vector.tensor_copy(v[:, tile, :], bank(4 + tile)).then_inc(v_ready, 1)

            def split_out(row):
                dve.wait_ge(out_part, KC * (row + 1))
                nc.vector.tensor_copy(oT[:, HI, :, :], o_ps[:, :, :]).then_inc(out_hi, 1)
                dve.wait_ge(out_hi, row + 1)
                nc.vector.tensor_tensor(oT[:, LO, :, :], o_ps[:, :, :], f32(oT[:, HI, :, :]), ALU.subtract).then_inc(out_ready, 1)

            def finish(row, tile):
                xt = residual[:, tile, :]
                dve.wait_ge(proj_done, row + 1)
                dve.wait_ge(bias_added, row + 1)
                nc.vector.tensor_tensor(xt, bank(6), xt, ALU.add).then_inc(x_final, 1)

            def first():
                for tile in range(TPP):
                    stats(0, tile)
                row = VEC_ROWS["bv"][0]
                bv = sh.vecs[:, row:row + KC].unsqueeze(2).to_broadcast([P, KC, P])
                nc.vector.tensor_copy(q[:, HI, :, 0:P], bv).then_inc(bv_hi, 1)
                dve.wait_ge(bv_hi, 1)
                nc.vector.tensor_tensor(q[:, LO, :, 0:P], bv, f32(q[:, HI, :, 0:P]), ALU.subtract).then_inc(bv_ready, 1)
                normalise(0, 0)
                normalise(0, 1)
                split_xn(0, 0)
                split_xn(0, 1)
                dve.wait_ge(const_loaded, 32)
                dve.wait_ge(bvo_done, 1)
                nc.vector.tensor_tensor(bo_bc[:, :], s_ps[:, 0:HPC, :].rearrange("p h k -> p (h k)"), bo_bc[:, :], ALU.add).then_inc(bo_ready, 1)

            def pair_step(n, before, more):
                row = TPP * n
                for u in range(KC):
                    split_kq(n, u)
                if before:
                    divide(row - 1, 0)
                    divide(row - 1, 1)
                split_kq(n, KC)
                if before:
                    finish(row - 2, 0)
                for u in range(KC + 1, 2 * KC):
                    split_kq(n, u)
                row_max(row, 0)
                row_max(row, 1)
                if more:
                    stats(n + 1, 0)
                    stats(n + 1, 1)
                copy_values(n, 0)
                if before:
                    split_out(row - 1)
                if more:
                    normalise(n + 1, 0)
                    normalise(n + 1, 1)
                divide(row, 0)
                copy_values(n, 1)
                divide(row, 1)
                if before:
                    finish(row - 1, 1)
                if more:
                    split_xn(n + 1, 0)
                row_max(row + 1, 0)
                if more:
                    split_xn(n + 1, 1)
                row_max(row + 1, 1)
                dve.wait_ge(piece_hi, n + 1)
                nc.vector.tensor_tensor(sh.w[prefetch_region][:, LO, bass.ds(n * PIECE, PIECE)], stage[:, :],
                                        f32(sh.w[prefetch_region][:, HI, bass.ds(n * PIECE, PIECE)]), ALU.subtract).then_inc(piece_done, 1)
                split_out(row)

            def last_tail():
                finish(B - 2, 0)
                divide(B - 1, 0)
                divide(B - 1, 1)
                split_out(B - 1)
                finish(B - 1, 1)

            schedule(dve, first, pair_step, last_tail)




def cond_seq_kernel(nc, t, out):
    with ExitStack() as ctx:
        sh = Shared()
        sh.w = [ctx.enter_context(nc.sbuf_tensor(f"weights{r}", [P, 2, REGION], F32R)) for r in range(2)]
        sh.ident = ctx.enter_context(nc.sbuf_tensor("ident", [P, P], F32))
        sh.vecs = ctx.enter_context(nc.sbuf_tensor("vecs", [P, N_VEC], F32))
        sh.mask = ctx.enter_context(nc.sbuf_tensor("mask", [P, B], F32))
        sh.neg_half = ctx.enter_context(nc.sbuf_tensor("neg_half", [P, 4], F32))
        sh.tables_dram = nc.dram_tensor("mod_tables", (P, 4 * 2 * KC * B), F32, kind="Internal").ap()
        sh.gates_dram = nc.dram_tensor("gate_rows", (2, B, D), F32, kind="Internal").ap()
        sh.gate_bias_dram = nc.dram_tensor("gate_bias_rows", (2, B, D), F32, kind="Internal").ap()
        x0 = t["x"].rearrange("b s d -> (b s) d")
        x1, x2, x3 = (nc.dram_tensor(f"x{n}", (B * P, D), F32, kind="Internal").ap() for n in (1, 2, 3))
        x4 = out.rearrange("b s d -> (b s) d")

        prologue(nc, sh, t)
        sh.end_phase(nc)

        def vec_column(*names):
            columns = [VEC_ROWS[n][0] + r for n in names for r in range(VEC_ROWS[n][1])]
            return lambda c: sh.vecs[:, columns[c]:columns[c] + 1]

        def tiles(regions):
            first = lambda part, k, c: w1_view(regions[c // 8], part)[:, k, (c % 8) * P:(c % 8 + 1) * P]
            second = lambda part, c: w2_view(regions[c // 8], part)[:, c % 8, :]
            return first, second

        ff = mlp_pieces((t["ff_w1"][:, 0:512], t["ff_w1"][:, 512:1024]), (t["ff_w2"][0:512, :], t["ff_w2"][512:1024, :]))
        att = attention_pieces((t["wk"], t["wq"], t["wv"], t["wo"]))
        ffn = [mlp_pieces((t["w1"][:, h:h + 512], t["w1"][:, h + 512:h + 1024]), (t["w2"][h:h + 512, :], t["w2"][h + 512:h + 1024, :]))
               for h in (0, HID)]

        ssm_stage = Stage(x0, x1, tiles([sh.w[0]]), vec_column("ssm_b1", "bwd_b1"), ACT.Gelu, 1e-6, table=0, gate=0,
                          masked=True, prefetch=ff, prefetch_region=1)
        ff_stage = Stage(x1, x2, tiles([sh.w[1]]), vec_column("ff_b1"), ACT.Gelu_apprx_tanh, 1e-6, table=1, gate=1,
                         prefetch=att, prefetch_region=0)
        mlp_phase(nc, sh, "mlp", [ssm_stage, ff_stage], chunks=HID // P)
        sh.end_phase(nc)
        attention_phase(nc, sh, source=x2, target=x3, bo=t["bo"], eps=1e-5, table=2, prefetch=ffn[0], prefetch_region=1)
        sh.end_phase(nc)
        ffn_stage = Stage(x3, x4, tiles([sh.w[1], sh.w[0]]), vec_column("b1"), ACT.Gelu, 1e-5, table=3, bias2=t["b2"],
                          prefetch=ffn[1], prefetch_region=0)
        mlp_phase(nc, sh, "ffn", [ffn_stage], chunks=2 * HID // P, second_half_first=True)


_INS = ["x", "cond_1024", "mask_BxS_bk0"] + ["L0_cond_" + n for n in (
    "ada_w", "ada_b", "ssm_w1", "ssm_b1", "ssm_w2", "ssm_b2", "bwd_w1", "bwd_b1", "bwd_w2", "bwd_b2",
    "ffada_w", "ffada_b", "ff_w1", "ff_b1", "ff_w2", "ff_b2")] + ["L1_cond_" + n for n in (
    "ln1_w", "ln1_b", "ln2_w", "ln2_b", "wq", "bq", "wk", "bk", "wv", "bv", "wo", "bo",
    "wt_attn", "bt_attn", "wt_ffn", "bt_ffn", "w1", "b1", "w2", "b2")]
_SHORT = {"cond_1024": "cond", "mask_BxS_bk0": "mask"}


def kernel(**inputs):
    import numpy as _np
    import concourse.bacc as _bacc
    from concourse import mybir as _mybir
    from concourse.bass_utils import run_bass_kernel_spmd as _run

    nc = _bacc.Bacc("TRN2", target_bir_lowering=False, num_devices=1)
    arrays, tensors = {}, {}
    for name in _INS:
        a = _np.ascontiguousarray(inputs[name])
        arrays[f"in_{name}_dram"] = a
        ap = nc.dram_tensor(f"in_{name}_dram", a.shape, _mybir.dt.from_np(a.dtype), kind="ExternalInput").ap()
        tensors[_SHORT.get(name, name.removeprefix("L0_cond_").removeprefix("L1_cond_"))] = ap
    out = nc.dram_tensor("out_0_dram", (B, P, D), _mybir.dt.float32, kind="ExternalOutput").ap()
    cond_seq_kernel(nc, tensors, out)
    r = _run(nc, [arrays], core_ids=[0])
    return r.results[0]["out_0_dram"]
```

```python
from contextlib import ExitStack

import concourse.bass as bass
from concourse import mybir

ALU = mybir.AluOpType
ACT = mybir.ActivationFunctionType
AX = mybir.AxisListType
F32 = mybir.dt.float32
F32R = mybir.dt.float32r
U8 = mybir.dt.uint8

P = 128
B = 32
D = 512
KC = D // P
HEADS = 16
HD = D // HEADS
HPC = P // HD
HI, LO = 0, 1
REGION = 2 * KC * D * 2
HID = 1024
PIECE = 512
MUL_HI_LO = ((HI, HI), (HI, LO), (LO, HI))

VEC_ROWS = {}
for _name, _rows in (("ssm_b1", 4), ("bwd_b1", 4), ("ff_b1", 8), ("b1", 16), ("bq", 4), ("bk", 4), ("bv", 4),
                     ("ada_b", 8), ("ffada_b", 8), ("bt_attn", 8), ("bt_ffn", 8),
                     ("ln1_w", 4), ("ln1_b", 4), ("ln2_w", 4), ("ln2_b", 4)):
    VEC_ROWS[_name] = (sum(r for _, r in VEC_ROWS.values()), _rows)
N_VEC = sum(r for _, r in VEC_ROWS.values())


def f32(ap):
    return ap.bitcast(F32)


def w1_view(region, part):
    return region[:, part, 0:KC * HID].rearrange("p (k h) -> p k h", k=KC)


def w2_view(region, part):
    return region[:, part, KC * HID:].rearrange("p (c n) -> p c n", n=D)


def mlp_pieces(w1_halves, w2_halves):
    pieces = []
    for k in range(KC):
        for half in range(2):
            pieces.append((w1_halves[half][k * P:(k + 1) * P, :], k * HID + half * PIECE))
    for c in range(HID // P):
        pieces.append((w2_halves[c // KC][(c % KC) * P:(c % KC + 1) * P, :], KC * HID + c * D))
    return pieces


def attention_pieces(matrices):
    return [(w[k * P:(k + 1) * P, :], (n * KC + k) * D) for n, w in enumerate(matrices) for k in range(KC)]




LATE_ITEMS = ((1, "shift"), (1, "scale"), (2, "shift"), (2, "scale"), (3, "shift"), (3, "scale"))
HALF_D = D // 2
FIRST_RING = 12


class Room:

    def __init__(self, room):
        slots = [half * REGION + 2 * PIECE + n * KC * D for half in range(2) for n in range(3)]
        self.weights = [room[:, at:at + KC * D].rearrange("p (k n) -> p k n", k=KC) for at in slots]
        raw = [half * REGION + n * PIECE for half in range(2) for n in range(2)]
        raw += [slots[n] + k * PIECE for n in (4, 5) for k in range(KC)]
        self.raw = [room[:, at:at + PIECE] for at in raw]
        spare = [slots[2] + KC * D, slots[5] + KC * D]
        size = KC * B
        cut = lambda at, n: room[:, at + n * size:at + (n + 1) * size].rearrange("p (k b) -> p k b", k=KC)
        self.tables = [[cut(spare[0], 2 * n + kind) for kind in range(2)] for n in range(2)]
        self.tables_row = room[:, spare[0]:spare[0] + 4 * size]
        self.scaled = [cut(spare[0], 4 + n) for n in range(2)]
        self.shifted = [cut(spare[0], 6 + n) for n in range(2)]
        self.cond, self.silu = cut(spare[1], 0), cut(spare[1], 1)
        self.rows = [room[:, at:at + HALF_D] for at in (spare[1] + 2 * size, spare[1] + 2 * size + HALF_D)]


class Shared:

    def __init__(self, nc):
        self.semaphores = []
        lasting = lambda name: nc.alloc_semaphore(name=name)
        self.opening_x = {phase: lasting("opening_x_" + phase) for phase in ("att", "ffn")}
        self.table_loaded = {phase: lasting("table_loaded_" + phase) for phase in ("att", "ffn")}
        self.stored = {phase: [lasting(f"stored{tile}_{phase}") for tile in range(4)] for phase in ("mlp", "att", "ffn")}

    def semaphore(self, nc, name):
        self.semaphores.append(nc.alloc_semaphore(name=name))
        return self.semaphores[-1]

    def vec(self, name, part):
        row = VEC_ROWS[name][0] + KC * part
        return self.vecs[:, row:row + KC].unsqueeze(2).to_broadcast([P, KC, B])

    def end_phase(self, nc):
        nc.clear_and_free_semaphores(self.semaphores)
        nc.all_engine_barrier()
        self.semaphores = []



TPB = 4
NBLK = B // TPB
TOK = TPB * P


class Stage:

    def __init__(self, source, target, tiles, bias1, func, eps, table, gate=None, bias2=None, masked=False,
                 prefetch=(), prefetch_region=0, following=None):
        self.following = following
        self.source = source.rearrange("(n p) d -> n p d", p=P)
        self.target = target.rearrange("(n p) d -> n p d", p=P)
        self.tiles, self.bias1, self.func, self.eps, self.table = tiles, bias1, func, eps, table
        self.gate, self.bias2, self.masked = gate, bias2, masked
        self.prefetch, self.prefetch_region = prefetch, prefetch_region


def mlp_phase(nc, sh, name, stages, *, chunks, second_half_first=False, room=None, t=None):
    sem = lambda what: sh.semaphore(nc, f"{name}_{what}")
    gated = stages[0].gate is not None
    x_loaded = [sem(f"x_loaded{tile}") for tile in range(TPB)]
    stored = sh.stored[name]
    opening_x = None if room else sh.opening_x[name]
    first_x = [sem(f"first_x{tile}") for tile in range(TPB)] if room else None
    if room:
        cond_loaded, vec_loaded, mask_loaded, row_loaded = sem("cond_loaded"), sem("vec_loaded"), sem("mask_loaded"), sem("row_loaded")
        zeroed, ident_done, mask_f_done, vecs_done, mask_done = (
            sem("zeroed"), sem("ident_done"), sem("mask_f_done"), sem("vecs_done"), sem("mask_done"))
        cond_turned, vec_turned, mask_turned, cond_copied, silu_done = (
            sem("cond_turned"), sem("vec_turned"), sem("mask_turned"), sem("cond_copied"), sem("silu_done"))
        ada_loaded = [sem(f"ada_loaded{r}") for r in range(4)]
        products_done, rows_copied, rows_turned, first_table = (
            sem("products_done"), sem("rows_copied"), sem("rows_turned"), sem("first_table"))
        b2_added, gate_added, gates_done, gates_stored = sem("b2_added"), sem("gate_added"), sem("gates_done"), sem("gates_stored")
        first_loaded = [sem(f"first_loaded{r}") for r in range(FIRST_RING)]
        first_hi, first_lo_dve, first_lo_pool = sem("first_hi"), sem("first_lo_dve"), sem("first_lo_pool")
        late_loaded = [sem(f"late_loaded{n}") for n in range(len(LATE_ITEMS))]
        ada_items = [t["ada_w"][:, 0:D], t["ada_w"][:, D:2 * D], t["ada_w"][:, 2 * D:3 * D], t["ffada_w"][:, 2 * D:3 * D]]
        late_source = {1: t["ffada_w"], 2: t["wt_attn"], 3: t["wt_ffn"]}
        first_pieces = mlp_pieces((t["ssm_w1"], t["bwd_w1"]), (t["ssm_w2"], t["bwd_w2"]))
        first_pieces = first_pieces[0:8:2] + first_pieces[1:8:2] + first_pieces[8:]
    gate_loaded, bias_loaded = sem("gate_loaded"), sem("bias_loaded")
    late_multiplied, late_copied, late_turned, late_stored, late_chain = (
        sem("late_multiplied"), sem("late_copied"), sem("late_turned"), sem("late_stored"), sem("late_chain"))
    LATE_FIRST = 2
    LATE_DONE = sum(1 if kind == "shift" or s == 1 else 4 for s, kind in LATE_ITEMS)
    passed = sem("passed")
    raw_stats, stats_done, var_done, rstd_done, rstd_masked = (
        sem("raw_stats"), sem("stats_done"), sem("var_done"), sem("rstd_done"), sem("rstd_masked"))
    xhat_ready, turned, modulated, xhi_done, xn_ready = (
        sem("xhat_ready"), sem("turned"), sem("modulated"), sem("xhi_done"), sem("xn_ready"))
    m1_done, act_done, hhi_done, h_ready, m2_done = (
        sem("m1_done"), sem("act_done"), sem("hhi_done"), sem("h_ready"), sem("m2_done"))
    y_done, x_final, y_scaled, bias_masked, bias_added = (
        sem("y_done"), sem("x_final"), sem("y_scaled"), sem("bias_masked"), sem("bias_added"))
    STAGE_RING = 4 if second_half_first else 1
    piece_loaded = [sem(f"piece_loaded{r}") for r in range(STAGE_RING)]
    piece_hi, piece_done = sem("piece_hi"), sem("piece_done")
    total = NBLK * len(stages)

    with ExitStack() as local:
        sb = lambda what, shape, dt: local.enter_context(nc.sbuf_tensor(f"{name}_{what}", shape, dt))
        ps = lambda what, shape: local.enter_context(nc.psum_tensor(f"{name}_{what}", shape, F32))
        x = sh.x
        xhat = sb("xhat", [P, D], F32)
        xmod = sb("xmod", [P, KC, P], F32)
        xn = sb("xn", [P, 2, 2, KC, TOK], F32R)
        g = sb("g", [P, TOK], F32)
        h = sb("h", [P, 2, 2, TOK], F32R)
        bias = sb("bias", [P, D], F32)
        if gated:
            tmp = sb("tmp", [P, D], F32)
            gate_bc = sb("gate", [P, TPB, D], F32)
        second_xmod = bias[:, :].rearrange("p (k q) -> p k q", k=KC) if gated else sb("xmod2", [P, KC, P], F32)
        xhats, xmods = (xhat, g), (xmod, second_xmod)
        bn = sb("bn", [P, TPB, 6], F32)
        mv = sb("mv", [P, TPB, 2], F32)
        var_eps = sb("var_eps", [P, TPB], F32)
        rstd = sb("rstd", [P, TPB], F32)
        rstd_m = sb("rstd_m", [P, TPB], F32)
        stage = sb("stage", [P, STAGE_RING, PIECE], F32)
        y_ps = ps("y", [P, TPB, D])
        m1_ps = ps("m1", [P, 2, TOK])
        turn_ps = ps("turn", [P, 2, KC * P])
        if room:
            mask_u8 = sb("mask_u8", [B, P], U8)
            cond = tmp[0:B, :]
            vec_rows, mask_f = g[:, 0:P], g[0:B, P:2 * P]
            gates = gate_bc[:, 0:2, 0:HALF_D]
            bwd_b2, rows = gate_bc[0:2 * B, 2, 0:HALF_D], gate_bc[:, 3, 0:HALF_D]
            cond_ps, vec_ps, item_ps, rows_ps = (y_ps[:, n, :] for n in range(TPB))

        def schedule(eng, first, block_step):
            first()
            for s, st in enumerate(stages):
                base = NBLK * s
                block_step(base, 0, stages[max(s - 1, 0)], st, st)
                with eng.Fori(0, NBLK // 2 - 1) as i:
                    block_step(2 * i + (base + 1), 1, st, st, st)
                    block_step(2 * i + (base + 2), 0, st, st, st)
                block_step(base + NBLK - 1, 1, st, st, stages[s + 1] if s + 1 < len(stages) else None)

        def batch_row(st, n, tile):
            return TPB * n + tile - B * stages.index(st)

        def piece_steps(n):
            return (TPB if room and isinstance(n, int) and n == 0 else 0, chunks - 1)

        TURN_STEP = 2

        block = local.enter_context(nc.Block())

        @block.sync
        def _(sp):
            def load_x(st, n, parity, tile):
                sp.dma_start(x[:, parity, tile, :], st.source[batch_row(st, n, tile)]).then_inc(x_loaded[tile], 16)

            def store(st, n, parity, tile):
                sp.wait_ge(x_final, TPB * n + tile + 1)
                sp.sem_inc(passed, 1)
                sp.dma_start(st.target[batch_row(st, n, tile)], x[:, parity, tile, :]).then_inc(stored[tile], 16)

            def load_gate(st, n):
                row = sh.gates_dram[st.gate].rearrange("(n t) d -> n (t d)", t=TPB)[bass.ds(n - NBLK * stages.index(st), 1), :]
                sp.dma_start(gate_bc[:, :, :].rearrange("p t d -> p (t d)"), row.to_broadcast([P, TPB * D])).then_inc(gate_loaded, 16)

            def load_raw(q):
                if q >= FIRST_RING:
                    sp.wait_ge(first_lo_pool if q % 2 else first_lo_dve, (q - FIRST_RING) // 2 + 1)
                sp.dma_start(room.raw[q % FIRST_RING], first_pieces[q][0]).then_inc(first_loaded[q % FIRST_RING], 16)

            def load_ada(n):
                sp.dma_start(room.weights[n], ada_items[n].rearrange("(k p) n -> p k n", p=P)).then_inc(ada_loaded[n], 16)

            def load_late(n):
                s, kind = LATE_ITEMS[n]
                at = D * ("shift", "scale").index(kind)
                sp.dma_start(room.weights[n], late_source[s][:, at:at + D].rearrange("(k p) n -> p k n", p=P)).then_inc(late_loaded[n], 16)

            def first():
                if room:
                    sp.dma_start(cond, t["cond"]).then_inc(cond_loaded, 16)
                    load_ada(0)
                    load_ada(1)
                    for tile in range(TPB):
                        sp.dma_start(x[:, 0, tile, :], stages[0].source[tile]).then_inc(first_x[tile], 16)
                    for vec_name, (row, count) in VEC_ROWS.items():
                        vector = t[vec_name][0:count * P].rearrange("(c p) -> c p", p=P)
                        sp.dma_start(vec_rows[row:row + count, :], vector).then_inc(vec_loaded, 16)
                    for q in range(10):
                        load_raw(q)
                    load_ada(2)
                    load_raw(10)
                    load_raw(11)
                    load_ada(3)
                    for q in range(12, len(first_pieces)):
                        load_raw(q)
                else:
                    for tile in range(TPP):
                        sp.wait_ge(sh.stored["att"][tile], 16 * NPAIR)

            def block_step(n, parity, before, st, after):
                if isinstance(n, int) and n == 0:
                    for tile in range(TPB):
                        load_x(after, 1, 1, tile)
                    if room:
                        sp.wait_ge(products_done, 1)
                        load_late(0)
                        load_late(1)
                        sp.wait_ge(gates_done, 1)
                        for s in range(2):
                            for half in range(2):
                                unit, columns = slice((2 * s + half) * B, (2 * s + half + 1) * B), slice(half * HALF_D, (half + 1) * HALF_D)
                                sp.dma_start(sh.gates_dram[s][:, columns], gates[unit, 0, :]).then_inc(gates_stored, 16)
                                sp.dma_start(sh.gate_bias_dram[s][:, columns], gates[unit, 1, :]).then_inc(gates_stored, 16)
                        for item in (2, 3):
                            sp.wait_ge(late_loaded[item - 2], 16)
                            load_late(item)
                        sp.wait_ge(first_lo_dve, len(first_pieces) // 2)
                        sp.wait_ge(first_lo_pool, len(first_pieces) // 2)
                        for item in (4, 5):
                            sp.wait_ge(late_loaded[item - 2], 16)
                            load_late(item)
                        sp.wait_ge(gates_stored, 128)
                        load_gate(stages[0], 0)
                        sp.wait_ge(late_chain, LATE_DONE)
                        sp.dma_start(sh.tables_dram, room.tables_row).then_inc(late_stored, 16)
                    return

                def load_next(tile):
                    if after is not None:
                        sp.wait_ge(stored[tile], 16 * n)
                        sp.sem_inc(passed, 1)
                        load_x(after, n + 1, 1 - parity, tile)

                store(before, n - 1, 1 - parity, 0)
                store(before, n - 1, 1 - parity, 1)
                load_next(0)
                store(before, n - 1, 1 - parity, 2)
                load_next(1)
                store(before, n - 1, 1 - parity, 3)
                if gated:
                    load_gate(st, n)
                load_next(2)
                load_next(3)
                if after is None and st.following:
                    phase, table, place, tiles = st.following
                    sp.wait_ge(late_stored, 16)
                    sp.dma_start(sh.tables[:, place, :, :, :].rearrange("p a k b -> p (a k b)"),
                                 sh.tables_dram[:, table * 2 * KC * B:(table + 1) * 2 * KC * B]).then_inc(sh.table_loaded[phase], 16)
                    for tile in range(tiles):
                        sp.wait_ge(stored[tile], 16 * n)
                        sp.dma_start(x[:, 0, tile, :], st.target[tile]).then_inc(sh.opening_x[phase], 16)

            schedule(sp, first, block_step)
            for tile in range(TPB):
                store(stages[-1], total - 1, 1, tile)
            if not stages[-1].following:
                for tile in range(TPB):
                    sp.wait_ge(stored[tile], 16 * total)

        @block.gpsimd
        def _(pool):
            def rstd_of(n, tile):
                pool.wait_ge(var_done, TPB * n + tile + 1)
                if n:
                    pool.wait_ge(xhat_ready, TPB * (n - 1) + tile + 1)
                nc.gpsimd.tensor_tensor(rstd[:, tile:tile + 1], var_eps[:, tile:tile + 1], sh.neg_half[:, 0:1], ALU.pow).then_inc(rstd_done, 1)

            def add_bias(st, n, tile):
                row, added = batch_row(st, n, tile), TPB * n + tile
                xt = x[:, n % 2, tile, :]
                if not gated:
                    nc.gpsimd.tensor_tensor(xt, xt, bias[:, :], ALU.add).then_inc(bias_added, 1)
                    return
                if added:
                    pool.wait_ge(bias_added, added)
                if not added:
                    pool.wait_ge(gates_stored, 128)
                    pool.wait_ge(xn_ready, TPB)
                pool.dma_start(bias[:, :], sh.gate_bias_dram[st.gate][row:row + 1, :].to_broadcast([P, D])).then_inc(bias_loaded, 16)
                pool.wait_ge(bias_loaded, 16 * (added + 1))
                if st.masked:
                    nc.gpsimd.tensor_scalar(bias[:, :], bias[:, :], sh.mask[:, row:row + 1], 1.0, ALU.mult, ALU.mult).then_inc(bias_masked, 1)
                    pool.wait_ge(bias_masked, added + 1)
                nc.gpsimd.tensor_tensor(xt, xt, bias[:, :], ALU.add).then_inc(bias_added, 1)

            def load_piece(st, q):
                if q >= STAGE_RING:
                    pool.wait_ge(piece_done, q - STAGE_RING + 1)
                pool.dma_start(stage[:, q % STAGE_RING, :], st.prefetch[q % len(st.prefetch)][0]).then_inc(piece_loaded[q % STAGE_RING], 16)

            def first_low(q):
                at = first_pieces[q][1]
                pool.wait_ge(first_hi, q + 1)
                nc.gpsimd.tensor_tensor(sh.w[0][:, LO, at:at + PIECE], room.raw[q % FIRST_RING],
                                        f32(sh.w[0][:, HI, at:at + PIECE]), ALU.subtract).then_inc(first_lo_pool, 1)

            if room:
                nc.gpsimd.memset(sh.ident[:, :], 0.0).then_inc(zeroed, 1)
                pool.wait_ge(zeroed, 1)
                nc.gpsimd.affine_select(out=sh.ident[:, :], in_=sh.ident[:, :], compare_op=ALU.not_equal, fill=1.0,
                                        base=0, pattern=[[-1, P]], channel_multiplier=1).then_inc(ident_done, 1)
                nc.gpsimd.memset(sh.neg_half[:, :], -0.5).then_inc(zeroed, 1)
                for half in range(2):
                    over_rows = lambda vector: vector[half * HALF_D:(half + 1) * HALF_D].rearrange("(a n) -> a n", a=1).to_broadcast([B, HALF_D])
                    ssm, ff = slice(half * B, (half + 1) * B), slice((2 + half) * B, (3 + half) * B)
                    pool.dma_start(gates[ssm, 0, :], over_rows(t["ada_b"][2 * D:3 * D])).then_inc(row_loaded, 16)
                    pool.dma_start(gates[ff, 0, :], over_rows(t["ffada_b"][2 * D:3 * D])).then_inc(row_loaded, 16)
                    pool.dma_start(gates[ssm, 1, :], over_rows(t["ssm_b2"])).then_inc(row_loaded, 16)
                    pool.dma_start(gates[ff, 1, :], over_rows(t["ff_b2"])).then_inc(row_loaded, 16)
                    pool.dma_start(bwd_b2[ssm], over_rows(t["bwd_b2"])).then_inc(row_loaded, 16)
                pool.wait_ge(zeroed, 2)
            rstd_of(0, 0)
            rstd_of(0, 1)
            if room:
                first_low(1)
            rstd_of(0, 2)
            rstd_of(0, 3)
            if room:
                for q in range(3, len(first_pieces), 2):
                    first_low(q)
            if not gated:
                pool.dma_start(bias[:, :], stages[0].bias2.rearrange("(a n) -> a n", a=1).to_broadcast([P, D])).then_inc(bias_loaded, 16)
                pool.wait_ge(bias_loaded, 16)
            for q in range(STAGE_RING):
                load_piece(stages[0], q)
            for n in range(total):
                st = stages[n // NBLK]
                pool.wait_ge(xhat_ready, TPB * (n + 1))
                if not second_half_first and not (room and n == 0):
                    load_piece(st, 2 * n + 1)
                for tile in range(TPB):
                    if second_half_first and n == 0:
                        load_piece(st, STAGE_RING + 2 * tile)
                        load_piece(st, STAGE_RING + 2 * tile + 1)
                    if n + 1 < total:
                        rstd_of(n + 1, tile)
                    if room and n == 0:
                        if tile == 2:
                            add_bias(st, n, 0)
                        if tile == 3:
                            load_piece(st, 1)
                            for late_tile in (1, 2, 3):
                                add_bias(st, n, late_tile)
                    else:
                        add_bias(st, n, tile)
                if not second_half_first:
                    if n + 1 < total:
                        load_piece(stages[(n + 1) // NBLK], 2 * n + 2)
                if second_half_first and n == 0:
                    for q in range(STAGE_RING + 2 * TPB, len(st.prefetch)):
                        load_piece(st, q)

        @block.tensor
        def _(pe):
            def turn(n, tile):
                source = xhats[tile % 2] if isinstance(n, int) and n == 0 else xhat
                pe.wait_ge(xhat_ready, TPB * n + tile + 1)
                if not (isinstance(n, int) and n == 0 and tile < 2):
                    pe.wait_ge(modulated, TPB * n + tile - 1)
                if room and not isinstance(n, int):
                    pe.wait_ge(late_chain, LATE_DONE)
                for k in range(KC):
                    last = nc.tensor.transpose(turn_ps[:, tile % 2, k * P:(k + 1) * P], source[:, k * P:(k + 1) * P], sh.ident[:, :])
                last.then_inc(turned, 1)

            def first_product(st, n, parity, c):
                if c == 0:
                    pe.wait_ge(xn_ready, TPB * (n + 1))
                if not (isinstance(n, int) and n == 0 and c < 2):
                    pe.wait_ge(act_done, chunks * n + c - 1)
                if second_half_first and isinstance(n, int) and n == 0 and c == HID // P:
                    pe.wait_ge(piece_done, 2 * KC)
                if not second_half_first and isinstance(n, int) and n == NBLK * stages.index(st) and n and c == 0:
                    pe.wait_ge(piece_done, 2 * n)
                if room and isinstance(n, int) and n == 0 and c == 0:
                    pe.wait_ge(first_lo_dve, 2)
                    pe.wait_ge(first_lo_pool, 2)
                if room and isinstance(n, int) and n == 0 and c == KC:
                    pe.wait_ge(first_lo_dve, 4)
                    pe.wait_ge(first_lo_pool, 4)
                steps = [(k, a, b) for k in range(KC) for a, b in MUL_HI_LO]
                for s, (k, a, b) in enumerate(steps):
                    last = nc.tensor.matmul(m1_ps[:, c % 2, :], st.tiles[0](a, k, c), xn[:, parity, b, k, :],
                                            start=s == 0, stop=s == len(steps) - 1)
                last.then_inc(m1_done, 1)

            def second_product(st, n, c):
                if room and isinstance(n, int) and n == 0:
                    if c % 2:
                        pe.wait_ge(first_lo_pool, KC + c // 2 + 1)
                    else:
                        pe.wait_ge(first_lo_dve, KC + c // 2 + 1)
                if second_half_first and isinstance(n, int) and n == 0 and c >= HID // P:
                    pe.wait_ge(piece_done, 2 * KC + c - HID // P + 1)
                pe.wait_ge(h_ready, chunks * n + c + 1)
                for tile in range(TPB):
                    if c == 0 and not (isinstance(n, int) and n == 0):
                        if gated:
                            pe.wait_ge(y_scaled, TPB * (n - 1) + tile + 1)
                        else:
                            pe.wait_ge(x_final, TPB * (n - 1) + tile + 1)
                    for s, (a, b) in enumerate(MUL_HI_LO):
                        last = nc.tensor.matmul(y_ps[:, tile, :], h[:, c % 2, a, tile * P:(tile + 1) * P], st.tiles[1](b, c),
                                                start=c == 0 and s == 0, stop=c == chunks - 1 and s == 2)
                    if c == chunks - 1:
                        last.then_inc(y_done, 1)
                if c < chunks - 1:
                    last.then_inc(m2_done, 1)

            def pair_product(out, cond_in, weights):
                for k in range(KC):
                    for unit in range(4):
                        item, half = divmod(unit, 2)
                        last = nc.tensor.matmul(out[unit * B:(unit + 1) * B, 0:HALF_D], cond_in[:, k, :],
                                                weights[item][:, k, half * HALF_D:(half + 1) * HALF_D], start=k == 0, stop=k == KC - 1)
                return last

            def turn_pair(out, rows):
                by_unit = out[:, 0:HALF_D].rearrange("p (u c b) -> p c u b", u=4, c=2)
                for c in range(2):
                    last = nc.tensor.transpose(by_unit[:, c], rows[:, c * P:(c + 1) * P], sh.ident[:, :])
                return last

            def late_product(group):
                pe.wait_ge(late_loaded[2 * group], 16)
                pe.wait_ge(late_loaded[2 * group + 1], 16)
                pair_product(turn_ps[:, group % 2, :], room.cond if group else room.silu,
                             room.weights[2 * group:2 * group + 2]).then_inc(late_multiplied, 1)

            def late_turn(group):
                pe.wait_ge(late_copied, group + 1)
                turn_pair(turn_ps[:, group % 2, :], room.rows[group % 2]).then_inc(late_turned, 1)

            def ada_product(out, pair):
                pe.wait_ge(ada_loaded[2 * pair], 16)
                pe.wait_ge(ada_loaded[2 * pair + 1], 16)
                pair_product(out, room.silu, room.weights[2 * pair:2 * pair + 2]).then_inc(products_done, 1)

            def opening():
                pe.wait_ge(ident_done, 1)
                pe.wait_ge(cond_loaded, 16)
                for k in range(KC):
                    last = nc.tensor.transpose(cond_ps[:, k * B:(k + 1) * B], cond[:, k * P:(k + 1) * P], sh.ident[0:B, 0:B])
                last.then_inc(cond_turned, 1)
                pe.wait_ge(mask_f_done, 1)
                pe.wait_ge(cond_copied, 1)
                nc.tensor.transpose(cond_ps[:, P:P + B], mask_f, sh.ident[0:B, 0:B]).then_inc(mask_turned, 1)
                pe.wait_ge(silu_done, 1)
                ada_product(item_ps, 0)
                pe.wait_ge(vec_loaded, 16 * len(VEC_ROWS))
                nc.tensor.transpose(vec_ps[:, 0:N_VEC], vec_rows[0:N_VEC, :], sh.ident[0:N_VEC, 0:N_VEC]).then_inc(vec_turned, 1)
                pe.wait_ge(rows_copied, 1)
                turn_pair(rows_ps, rows).then_inc(rows_turned, 1)

            def first():
                if room:
                    opening()
                for tile in range(TPB):
                    turn(0, tile)

            def block_step(n, parity, before, st, after):
                first_product(st, n, parity, 0)
                for c in range(chunks):
                    if c + 1 < chunks:
                        first_product(st, n, parity, c + 1)
                    second_product(st, n, c)
                    if room and isinstance(n, int) and n == 0 and c == 0:
                        pe.wait_ge(modulated, TPB)
                        ada_product(turn_ps[:, 1, :], 1)
                    if room and isinstance(n, int) and n == 0 and c == TURN_STEP + 1:
                        pe.wait_ge(gate_added, 1)
                    if after is not None and TURN_STEP <= c < TURN_STEP + TPB:
                        turn(n + 1, c - TURN_STEP)
                    if room and isinstance(n, int) and n == 0 and c == chunks - 3:
                        pe.wait_ge(modulated, 2 * TPB - 1)
                        late_product(0)
                    if room and isinstance(n, int) and n == 0 and c == chunks - 2:
                        late_turn(0)
                        pe.wait_ge(modulated, 2 * TPB)
                        late_product(1)
                    if room and isinstance(n, int) and n == 0 and c == chunks - 1:
                        late_turn(1)
                        pe.wait_ge(late_chain, LATE_FIRST)
                        late_product(2)
                if room and isinstance(n, int) and n == 0:
                    late_turn(2)

            schedule(pe, first, block_step)

        @block.scalar
        def _(act):
            def modulate(st, n, tile):
                row = batch_row(st, n, tile)
                act.wait_ge(turned, TPB * n + tile + 1)
                if not gated and isinstance(n, int) and row == 0:
                    act.wait_ge(sh.table_loaded[name], 16)
                if room and st is not stages[0] and isinstance(n, int) and row == 0:
                    act.wait_ge(late_chain, LATE_DONE)
                target = xmod
                if isinstance(n, int) and n == 0:
                    target = xmods[tile % 2]
                    if tile >= 2:
                        act.wait_ge(xn_ready, tile - 1)
                else:
                    act.wait_ge(xn_ready, TPB * n + tile)
                for k in range(KC):
                    last = nc.scalar.activation(target[:, k, :], turn_ps[:, tile % 2, k * P:(k + 1) * P], ACT.Identity,
                                                bias=sh.tables[:, st.table, 1, k, bass.ds(row, 1)], scale=sh.tables[:, st.table, 0, k, bass.ds(row, 1)])
                last.then_inc(modulated, 1)

            def activate(st, n, c):
                act.wait_ge(m1_done, chunks * n + c + 1)
                if not (isinstance(n, int) and n == 0 and c == 0):
                    act.wait_ge(h_ready, chunks * n + c)
                nc.scalar.activation(g[:, :], m1_ps[:, c % 2, :], st.func, bias=st.bias1(c)).then_inc(act_done, 1)

            def piece_high(st, n, q, at, slot, turns):
                act.wait_ge(piece_loaded[slot], 16 * (turns + 1))
                if room and not isinstance(n, int):
                    act.wait_ge(late_turned, 2)
                if room and isinstance(n, int) and n == NBLK - 1:
                    act.wait_ge(late_stored, 16)
                nc.scalar.activation(sh.w[st.prefetch_region][:, HI, bass.ds(at, PIECE)], stage[:, slot, :], ACT.Copy).then_inc(piece_hi, 1)

            def first_high(q):
                at = first_pieces[q][1]
                act.wait_ge(first_loaded[q % FIRST_RING], 16 * (q // FIRST_RING + 1))
                nc.scalar.activation(sh.w[0][:, HI, at:at + PIECE], room.raw[q % FIRST_RING], ACT.Copy).then_inc(first_hi, 1)

            def first():
                if room:
                    act.dma_start(mask_u8[:, :], t["mask"]).then_inc(mask_loaded, 16)
                    act.wait_ge(cond_copied, 1)
                    nc.scalar.activation(room.silu, room.cond, ACT.Silu).then_inc(silu_done, 1)
                    first_high(0)
                    first_high(1)
                    act.wait_ge(first_table, 2)
                for tile in range(TPB):
                    modulate(stages[0], 0, tile)
                    if room and tile in (1, 2):
                        first_high(tile + 1)
                if room:
                    for q in range(4, 10):
                        first_high(q)

            def block_step(n, parity, before, st, after):
                activate(st, n, 0)
                for c in range(chunks):
                    if c + 1 < chunks:
                        activate(st, n, c + 1)
                    if room and isinstance(n, int) and n == 0 and c < 3:
                        first_high(10 + 2 * c)
                        first_high(11 + 2 * c)
                    if after is not None and TURN_STEP <= c < TURN_STEP + TPB:
                        modulate(after, n + 1, c - TURN_STEP)
                    if second_half_first and isinstance(n, int) and n == 0 and 2 * c < len(st.prefetch):
                        for q in (2 * c, 2 * c + 1):
                            piece_high(st, n, q, st.prefetch[q][1], q % STAGE_RING, q // STAGE_RING)
                    if not second_half_first and c in piece_steps(n):
                        q = 2 * n + (c == chunks - 1)
                        local_n = n - NBLK * stages.index(st)
                        piece_high(st, n, q, (2 * local_n + (c == chunks - 1)) * PIECE, 0, q)

            schedule(act, first, block_step)

        @block.vector
        def _(dve):
            def stats(st, n, parity, tile):
                row = TPB * n + tile
                if room and isinstance(n, int) and n == 0:
                    dve.wait_ge(first_x[tile], 16)
                elif isinstance(n, int) and n == 0:
                    dve.wait_ge(opening_x, 16 * TPB)
                else:
                    dve.wait_ge(x_loaded[tile], 16 * n)
                nc.vector.bn_stats(bn[:, tile, :], x[:, parity, tile, :]).then_inc(raw_stats, 1)
                dve.wait_ge(raw_stats, row + 1)
                dve.sem_inc(passed, 1)
                nc.vector.bn_aggr(mv[:, tile, :], bn[:, tile, :]).then_inc(stats_done, 1)
                dve.wait_ge(stats_done, row + 1)
                nc.vector.tensor_scalar(var_eps[:, tile:tile + 1], mv[:, tile, 1:2], st.eps, None, ALU.add).then_inc(var_done, 1)

            def normalise(st, n, parity, tile):
                row = TPB * n + tile
                dve.wait_ge(rstd_done, row + 1)
                r = rstd[:, tile:tile + 1]
                if st.masked:
                    nc.vector.tensor_tensor(rstd_m[:, tile:tile + 1], r, sh.mask[:, bass.ds(row, 1)], ALU.mult).then_inc(rstd_masked, 1)
                    dve.wait_ge(rstd_masked, row + 1)
                    r = rstd_m[:, tile:tile + 1]
                target = xhat
                if isinstance(n, int) and n == 0:
                    target = xhats[tile % 2]
                    if tile >= 2:
                        dve.wait_ge(turned, tile - 1)
                else:
                    dve.wait_ge(turned, row)
                nc.vector.tensor_scalar(target[:, :], x[:, parity, tile, :], mv[:, tile, 0:1], r,
                                        ALU.subtract, ALU.mult).then_inc(xhat_ready, 1)

            def split_xn(n, parity, tile):
                dve.wait_ge(modulated, TPB * n + tile + 1)
                hi = xn[:, parity, HI, :, tile * P:(tile + 1) * P]
                source = xmods[tile % 2] if isinstance(n, int) and n == 0 else xmod
                nc.vector.tensor_copy(hi, source[:, :, :]).then_inc(xhi_done, 1)
                dve.wait_ge(xhi_done, TPB * n + tile + 1)
                nc.vector.tensor_tensor(xn[:, parity, LO, :, tile * P:(tile + 1) * P], source[:, :, :], f32(hi),
                                        ALU.subtract).then_inc(xn_ready, 1)

            def split_h(n, c):
                dve.wait_ge(act_done, chunks * n + c + 1)
                if c >= 2 or (c == 0 and not (isinstance(n, int) and n == 0)):
                    dve.wait_ge(m2_done, (chunks - 1) * n + max(c - 1, 0))
                elif not (isinstance(n, int) and n == 0):
                    dve.wait_ge(y_done, TPB * n)
                nc.vector.tensor_copy(h[:, c % 2, HI, :], g[:, :]).then_inc(hhi_done, 1)
                dve.wait_ge(hhi_done, chunks * n + c + 1)
                nc.vector.tensor_tensor(h[:, c % 2, LO, :], g[:, :], f32(h[:, c % 2, HI, :]), ALU.subtract).then_inc(h_ready, 1)

            def finish(st, n, parity, tile):
                row = TPB * n + tile
                xt = x[:, parity, tile, :]
                dve.wait_ge(y_done, row + 1)
                if tile == 0 and gated:
                    dve.wait_ge(gate_loaded, 16 * (n + 1))
                if not gated:
                    dve.wait_ge(bias_added, row + 1)
                    nc.vector.tensor_tensor(xt, y_ps[:, tile, :], xt, ALU.add).then_inc(x_final, 1)
                    return
                if not (isinstance(n, int) and row == 0):
                    dve.wait_ge(x_final, row)
                if st.masked:
                    nc.vector.scalar_tensor_tensor(out=tmp[:, :], in0=y_ps[:, tile, :], scalar=sh.mask[:, bass.ds(row, 1)],
                                                   in1=gate_bc[:, tile, :], op0=ALU.mult, op1=ALU.mult).then_inc(y_scaled, 1)
                else:
                    nc.vector.tensor_tensor(tmp[:, :], y_ps[:, tile, :], gate_bc[:, tile, :], ALU.mult).then_inc(y_scaled, 1)
                dve.wait_ge(y_scaled, row + 1)
                dve.wait_ge(bias_added, row + 1)
                nc.vector.tensor_tensor(xt, xt, tmp[:, :], ALU.add).then_inc(x_final, 1)

            def piece_low(st, q, at, slot):
                w = sh.w[st.prefetch_region]
                dve.wait_ge(piece_hi, q + 1)
                nc.vector.tensor_tensor(w[:, LO, bass.ds(at, PIECE)], stage[:, slot, :],
                                        f32(w[:, HI, bass.ds(at, PIECE)]), ALU.subtract).then_inc(piece_done, 1)

            def late_copy(group):
                dve.wait_ge(late_multiplied, group + 1)
                if group == 2:
                    dve.wait_ge(late_turned, 1)
                nc.vector.tensor_copy(room.rows[group % 2], turn_ps[:, group % 2, 0:HALF_D]).then_inc(late_copied, 1)

            late_links = [0]

            def link(ins):
                late_links[0] += 1
                ins.then_inc(late_chain, 1)
                dve.wait_ge(late_chain, late_links[0])

            def late_tables(group):
                dve.wait_ge(late_turned, group + 1)
                raw = turn_ps[:, group % 2, 0:HALF_D].rearrange("p (j k b) -> p j k b", j=2, k=KC)
                bias_name = ("ffada_b", "bt_attn", "bt_ffn")[group]
                scale_tab, shift_tab = (sh.tables[:, 1, 0, :, :], sh.tables[:, 1, 1, :, :]) if group == 0 else room.tables[group - 1]
                scaled = scale_tab if group == 0 else room.scaled[group - 1]
                link(nc.vector.tensor_tensor(shift_tab, raw[:, 0], sh.vec(bias_name, 0), ALU.add))
                link(nc.vector.scalar_tensor_tensor(out=scaled, in0=raw[:, 1], scalar=1.0, in1=sh.vec(bias_name, 1),
                                                    op0=ALU.add, op1=ALU.add))
                if group:
                    norm, shifted = ("ln1", "ln2")[group - 1], room.shifted[group - 1]
                    link(nc.vector.tensor_tensor(scale_tab, scaled, sh.vec(norm + "_w", 0), ALU.mult))
                    link(nc.vector.tensor_tensor(shifted, scaled, sh.vec(norm + "_b", 0), ALU.mult))
                    link(nc.vector.tensor_tensor(shift_tab, shift_tab, shifted, ALU.add))

            def opening():
                dve.wait_ge(cond_turned, 1)
                nc.vector.tensor_copy(room.cond, cond_ps[:, 0:KC * B].rearrange("p (k b) -> p k b", k=KC)).then_inc(cond_copied, 1)
                dve.wait_ge(mask_loaded, 16)
                nc.vector.tensor_scalar(mask_f, mask_u8[:, :], 0.0, None, ALU.not_equal).then_inc(mask_f_done, 1)
                dve.wait_ge(mask_turned, 1)
                nc.vector.tensor_copy(sh.mask[:, :], cond_ps[:, P:P + B]).then_inc(mask_done, 1)

            def first_table_rows():
                dve.wait_ge(products_done, 1)
                nc.vector.tensor_copy(rows, item_ps[:, 0:HALF_D]).then_inc(rows_copied, 1)
                dve.wait_ge(vec_turned, 1)
                nc.vector.tensor_copy(sh.vecs[:, :], vec_ps[:, 0:N_VEC]).then_inc(vecs_done, 1)

            def make_first_table():
                dve.wait_ge(vecs_done, 1)
                dve.wait_ge(rows_turned, 1)
                raw = rows_ps[:, 0:HALF_D].rearrange("p (j k b) -> p j k b", j=2, k=KC)
                nc.vector.tensor_tensor(sh.tables[:, 0, 1, :, :], raw[:, 0], sh.vec("ada_b", 0), ALU.add).then_inc(first_table, 1)
                nc.vector.scalar_tensor_tensor(out=sh.tables[:, 0, 0, :, :], in0=raw[:, 1], scalar=1.0, in1=sh.vec("ada_b", 1),
                                               op0=ALU.add, op1=ALU.add).then_inc(first_table, 1)

            def make_gates():
                dve.wait_ge(row_loaded, 160)
                nc.vector.tensor_tensor(gates[0:2 * B, 1, :], gates[0:2 * B, 1, :], bwd_b2, ALU.add).then_inc(b2_added, 1)
                dve.wait_ge(products_done, 2)
                dve.wait_ge(b2_added, 1)
                nc.vector.tensor_tensor(gates[:, 0, :], turn_ps[:, 1, 0:HALF_D], gates[:, 0, :], ALU.add).then_inc(gate_added, 1)
                dve.wait_ge(gate_added, 1)
                nc.vector.tensor_tensor(gates[:, 1, :], gates[:, 0, :], gates[:, 1, :], ALU.mult).then_inc(gates_done, 1)

            def first_low(q):
                at = first_pieces[q][1]
                dve.wait_ge(first_hi, q + 1)
                nc.vector.tensor_tensor(sh.w[0][:, LO, at:at + PIECE], room.raw[q % FIRST_RING],
                                        f32(sh.w[0][:, HI, at:at + PIECE]), ALU.subtract).then_inc(first_lo_dve, 1)

            def first():
                if room:
                    opening()
                if room:
                    for tile in range(TPB):
                        stats(stages[0], 0, 0, tile)
                    first_table_rows()
                    normalise(stages[0], 0, 0, 0)
                    make_first_table()
                    normalise(stages[0], 0, 0, 1)
                else:
                    stats(stages[0], 0, 0, 0)
                    stats(stages[0], 0, 0, 1)
                    normalise(stages[0], 0, 0, 0)
                    stats(stages[0], 0, 0, 2)
                    normalise(stages[0], 0, 0, 1)
                    stats(stages[0], 0, 0, 3)
                split_xn(0, 0, 0)
                normalise(stages[0], 0, 0, 2)
                split_xn(0, 0, 1)
                normalise(stages[0], 0, 0, 3)
                if room:
                    first_low(0)
                split_xn(0, 0, 2)
                if room:
                    first_low(2)
                split_xn(0, 0, 3)
                if room:
                    first_low(4)
                    first_low(6)
                    first_low(8)

            def block_step(n, parity, before, st, after):
                for c in range(chunks):
                    split_h(n, c)
                    if room and isinstance(n, int) and n == 0 and c < 3:
                        first_low(10 + 2 * c)
                    if room and isinstance(n, int) and n == 0 and c == 1:
                        make_gates()
                    if c == 0 and not (isinstance(n, int) and n == 0):
                        finish(before, n - 1, 1 - parity, TPB - 1)
                    if after is not None:
                        if TURN_STEP + 1 <= c <= TURN_STEP + TPB:
                            split_xn(n + 1, 1 - parity, c - TURN_STEP - 1)
                        if TURN_STEP - 1 <= c < TURN_STEP - 1 + TPB:
                            stats(after, n + 1, 1 - parity, c - TURN_STEP + 1)
                        if TURN_STEP <= c < TURN_STEP + TPB:
                            normalise(after, n + 1, 1 - parity, c - TURN_STEP)
                    if second_half_first and isinstance(n, int) and n == 0 and 2 * c < len(st.prefetch):
                        for q in (2 * c, 2 * c + 1):
                            piece_low(st, q, st.prefetch[q][1], q % STAGE_RING)
                    if room and isinstance(n, int) and n == 0 and c == chunks - 2:
                        late_copy(0)
                    if room and isinstance(n, int) and n == 0 and c == chunks - 1:
                        late_copy(1)
                        late_tables(0)
                    if not second_half_first and c in piece_steps(n):
                        piece_low(st, 2 * n + (c == chunks - 1), (2 * (n - NBLK * stages.index(st)) + (c == chunks - 1)) * PIECE, 0)
                for tile in range(TPB - 1):
                    finish(st, n, parity, tile)
                if room and isinstance(n, int) and n == 0:
                    late_copy(2)
                    late_tables(1)
                    late_tables(2)

            schedule(dve, first, block_step)
            finish(stages[-1], total - 1, 1, TPB - 1)



TPP = 2
NPAIR = B // TPP
PT = TPP * P
HALF = HEADS // 2


def attention_phase(nc, sh, *, source, target, bo, eps, table, prefetch, prefetch_region, following):
    sem = lambda what: sh.semaphore(nc, "att_" + what)
    x_loaded = [sem(f"x_loaded{tile}") for tile in range(TPP)]
    residual_loaded = [sem(f"residual_loaded{tile}") for tile in range(TPP)]
    opening_x, stored = sh.opening_x["att"], sh.stored["att"]
    const_loaded = sem("const_loaded")
    passed = sem("passed")
    bv_hi, bv_ready, bvo_done, bo_ready = sem("bv_hi"), sem("bv_ready"), sem("bvo_done"), sem("bo_ready")
    raw_stats, stats_done, var_done, rstd_done = sem("raw_stats"), sem("stats_done"), sem("var_done"), sem("rstd_done")
    xhat_ready, turned, modulated, xhi_done, xn_ready = (
        sem("xhat_ready"), sem("turned"), sem("modulated"), sem("xhi_done"), sem("xn_ready"))
    kq_done, kq_hi, kq_ready, v_done, v_ready = sem("kq_done"), sem("kq_hi"), sem("kq_ready"), sem("v_done"), sem("v_ready")
    diag_zeroed, diag_loaded = sem("diag_zeroed"), sem("diag_loaded")
    scores_done, max_done, negmax_done, exp_done, inv_done, probs_ready = (
        sem("scores_done"), sem("max_done"), sem("negmax_done"), sem("exp_done"), sem("inv_done"), sem("probs_ready"))
    probs_turned, probsT_ready, out_part = sem("probs_turned"), sem("probsT_ready"), sem("out_part")
    out_hi, out_ready = sem("out_hi"), sem("out_ready")
    proj_done, x_final, bias_added = sem("proj_done"), sem("x_final"), sem("bias_added")
    piece_loaded, piece_hi, piece_done = sem("piece_loaded"), sem("piece_hi"), sem("piece_done")
    scale = float(HD) ** -0.5
    W = sh.w[0]

    def weight(part, matrix, k):
        at = (matrix * KC + k) * D
        return W[:, part, at:at + D]

    WK, WQ, WV, WO = range(4)

    with ExitStack() as local:
        sb = lambda what, shape, dt: local.enter_context(nc.sbuf_tensor("att_" + what, shape, dt))
        x = sh.x[:, 0, 0:TPP, :]
        xmod = sh.x[:, 0, TPP:2 * TPP, :].rearrange("p t (k q) -> p t k q", k=KC)
        residual = sh.x[:, 1, 0:TPP, :]
        v = sh.x[:, 1, TPP:2 * TPP, :]
        xn = sb("xn", [P, 2, KC, PT], F32R)
        q = sb("q", [P, 2, KC, PT], F32R)
        kst = sb("kst", [P, 2, KC, PT], F32R)
        kdiag = sb("kdiag", [P, 2, KC, HPC * P], F32R)
        probs = sb("probs", [P, HEADS, P], F32)
        probsT = sb("probsT", [P, 2, HPC * P], F32)
        oT = sb("oT", [P, 2, KC, P], F32R)
        bo_bc = sb("bo", [P, D], F32)
        bn = sb("bn", [P, 6], F32)
        mv = sb("mv", [P, TPP, 2], F32)
        var_eps = sb("var_eps", [P, TPP], F32)
        rstd = sb("rstd", [P, TPP], F32)
        smax = sb("smax", [P, HEADS], F32)
        negmax = sb("negmax", [P, HEADS], F32)
        rowsum = sb("rowsum", [P, HEADS], F32)
        inv = sb("inv", [P, HEADS], F32)
        stage = sb("stage", [P, PIECE], F32)
        s_ps = local.enter_context(nc.psum_tensor("att_s", [P, HEADS, P], F32))
        bank_ps = local.enter_context(nc.psum_tensor("att_banks", [P, 3, 512], F32))
        o_ps = local.enter_context(nc.psum_tensor("att_o", [P, KC, P], F32))
        bank = lambda n: bank_ps[:, n - 4, :]

        source_t = source.rearrange("(n p) d -> n p d", p=P)
        target_t = target.rearrange("(n p) d -> n p d", p=P)

        def schedule(eng, first, pair_step, last_tail):
            first()
            pair_step(0, False, True)
            with eng.Fori(0, NPAIR - 2) as i:
                pair_step(i + 1, True, True)
            pair_step(NPAIR - 1, True, False)
            last_tail()

        def probs_bank(tile, m):
            return 6 if m % 2 == 0 else 4 + tile

        def is_first(row):
            return isinstance(row, int) and row == 0

        block = local.enter_context(nc.Block())

        @block.sync
        def _(sp):
            def load_x(n, tile):
                sp.dma_start(x[:, tile, :], source_t[TPP * n + tile]).then_inc(x_loaded[tile], 16)

            def load_residual(n, tile):
                sp.dma_start(residual[:, tile, :], source_t[TPP * n + tile]).then_inc(residual_loaded[tile], 16)

            def diag(n, tile):
                sp.wait_ge(kq_ready, 2 * KC * n + KC)
                sp.sem_inc(passed, 1)
                if is_first(TPP * n + tile):
                    sp.wait_ge(diag_zeroed, 1)
                else:
                    sp.wait_ge(scores_done, 2 * (TPP * n + tile))
                    sp.sem_inc(passed, 1)
                for j in range(HPC):
                    rows = slice(j * HD, (j + 1) * HD)
                    sp.dma_start(f32(kdiag[rows, :, :, j * P:(j + 1) * P]), f32(kst[rows, :, :, tile * P:(tile + 1) * P])).then_inc(diag_loaded, 16)

            def store(n, tile):
                sp.wait_ge(x_final, TPP * n + tile + 1)
                sp.sem_inc(passed, 1)
                sp.dma_start(target_t[TPP * n + tile], residual[:, tile, :]).then_inc(stored[tile], 16)

            def first():
                for tile in range(TPB):
                    sp.wait_ge(sh.stored["mlp"][tile], 16 * 2 * NBLK)
                sp.dma_start(bo_bc[:, :], bo.rearrange("(a n) -> a n", a=1).to_broadcast([P, D])).then_inc(const_loaded, 16)

            def pair_step(n, before, more):
                if not more:
                    phase, next_table, place, tiles = following
                    sp.dma_start(sh.tables[:, place, :, :, :].rearrange("p a k b -> p (a k b)"),
                                 sh.tables_dram[:, next_table * 2 * KC * B:(next_table + 1) * 2 * KC * B]).then_inc(sh.table_loaded[phase], 16)
                    sp.wait_ge(xn_ready, B)
                    for tile in range(tiles):
                        sp.dma_start(sh.x[:, 0, tile, :], target_t[tile]).then_inc(sh.opening_x[phase], 16)
                if more:
                    for tile in range(TPP):
                        sp.wait_ge(turned, TPP * n + tile + 1)
                        sp.sem_inc(passed, 1)
                        load_x(n + 1, tile)
                diag(n, 0)
                if before:
                    store(n - 1, 0)
                    sp.wait_ge(stored[0], 16 * n)
                    sp.sem_inc(passed, 1)
                load_residual(n, 0)
                diag(n, 1)
                if before:
                    store(n - 1, 1)
                    sp.wait_ge(stored[1], 16 * n)
                    sp.sem_inc(passed, 1)
                load_residual(n, 1)

            def last_tail():
                store(NPAIR - 1, 0)
                store(NPAIR - 1, 1)

            schedule(sp, first, pair_step, last_tail)

        @block.gpsimd
        def _(pool):
            def rstd_of(row):
                at = row % TPP
                pool.wait_ge(var_done, row + 1)
                if row >= TPP:
                    pool.wait_ge(xhat_ready, row - TPP + 1)
                nc.gpsimd.tensor_tensor(rstd[:, at:at + 1], var_eps[:, at:at + 1], sh.neg_half[:, 0:1], ALU.pow).then_inc(rstd_done, 1)

            def add_bias(row):
                xt = residual[:, row % TPP, :]
                pool.wait_ge(residual_loaded[row % TPP], 16 * (row // TPP + 1))
                nc.gpsimd.tensor_tensor(xt, xt, bo_bc[:, :], ALU.add).then_inc(bias_added, 1)

            rstd_of(0)
            rstd_of(1)
            nc.gpsimd.memset(f32(kdiag[:, :, :, :]).rearrange("p a k c -> p (a k c)"), 0.0).then_inc(diag_zeroed, 1)
            pool.wait_ge(bo_ready, 1)
            for n in range(NPAIR):
                if n:
                    pool.wait_ge(piece_done, n)
                pool.dma_start(stage[:, :], prefetch[n][0]).then_inc(piece_loaded, 16)
                add_bias(TPP * n)
                if n + 1 < NPAIR:
                    rstd_of(TPP * n + 2)
                    rstd_of(TPP * n + 3)
                add_bias(TPP * n + 1)

        @block.tensor
        def _(pe):
            def product(out, steps):
                for s, (lhs, rhs) in enumerate(steps):
                    last = nc.tensor.matmul(out, lhs, rhs, start=s == 0, stop=s == len(steps) - 1)
                return last

            def turn(n, tile):
                pe.wait_ge(xhat_ready, TPP * n + tile + 1)
                if not is_first(n):
                    pe.wait_ge(v_ready, TPP * (n - 1) + tile + 1)
                for k in range(KC):
                    last = nc.tensor.transpose(bank(4 + tile)[:, k * P:(k + 1) * P], x[:, tile, k * P:(k + 1) * P], sh.ident[:, :])
                last.then_inc(turned, 1)

            def keys_queries(n, u):
                m, matrix = u % KC, (WK, WQ)[u // KC]
                product(bank(5 - u % 2)[:, 0:PT], [(weight(a, matrix, k)[:, m * P:(m + 1) * P], xn[:, b, k, :])
                                                   for k in range(KC) for a, b in MUL_HI_LO]).then_inc(kq_done, 1)

            def scores(n, tile, e):
                row = TPP * n + tile
                if e == 0:
                    pe.wait_ge(diag_loaded, 16 * HPC * (row + 1))
                if tile == 0:
                    pe.wait_ge(kq_ready, 2 * KC * n + KC + 2 * e + 2)
                if not is_first(row):
                    pe.wait_ge(exp_done, 2 * row - 1 + e)
                elif e == 0:
                    pe.wait_ge(bo_ready, 1)
                for m in (2 * e, 2 * e + 1):
                    last = product(s_ps[:, m * HPC:(m + 1) * HPC, :].rearrange("p h k -> p (h k)"),
                                   [(q[:, a, m, tile * P:(tile + 1) * P], kdiag[:, b, m, :]) for a, b in MUL_HI_LO])
                last.then_inc(scores_done, 1)

            def values(n, tile):
                product(bank(4 + tile), [(xn[:, a, k, tile * P:(tile + 1) * P], weight(b, WV, k))
                                         for k in range(KC) for a, b in MUL_HI_LO]).then_inc(v_done, 1)

            def turn_probs(row, tile, m):
                if m % 2 == 0:
                    pe.wait_ge(probs_ready, 2 * row + m // 2 + 1)
                if m >= 2:
                    pe.wait_ge(probsT_ready, KC * row + m - 1)
                for j in range(HPC):
                    last = nc.tensor.transpose(bank(probs_bank(tile, m))[:, j * P:(j + 1) * P], probs[:, m * HPC + j, :], sh.ident[:, :])
                last.then_inc(probs_turned, 1)

            def weigh(row, tile, m):
                if m == 0:
                    pe.wait_ge(v_ready, row + 1)
                    if not is_first(row):
                        pe.wait_ge(out_ready, row)
                pe.wait_ge(probsT_ready, KC * row + m + 1)
                for j in range(HPC):
                    head = m * HPC + j
                    last = nc.tensor.matmul(o_ps[j * HD:(j + 1) * HD, m, :], v[:, tile, head * HD:(head + 1) * HD],
                                            probsT[:, m % 2, j * P:(j + 1) * P], start=True, stop=True)
                last.then_inc(out_part, 1)

            def project(row):
                pe.wait_ge(out_ready, row + 1)
                product(bank(6), [(oT[:, a, k, :], weight(b, WO, k)) for k in range(KC) for a, b in MUL_HI_LO]).then_inc(proj_done, 1)

            def first():
                turn(0, 0)
                turn(0, 1)
                pe.wait_ge(bv_ready, 1)
                product(s_ps[:, 0:HPC, :].rearrange("p h k -> p (h k)"),
                        [(q[:, a, k, 0:P], weight(b, WO, k)) for k in range(KC) for a, b in MUL_HI_LO]).then_inc(bvo_done, 1)

            def pair_step(n, before, more):
                row = TPP * n
                pe.wait_ge(xn_ready, TPP * (n + 1))
                pe.wait_ge(modulated, TPP * (n + 1))
                keys_queries(n, 0)
                if before:
                    pe.wait_ge(probsT_ready, KC * (row - 1))
                else:
                    pe.wait_ge(modulated, 1)
                keys_queries(n, 1)
                for u in range(2, 2 * KC):
                    if u == KC and before:
                        project(row - 2)
                    pe.wait_ge(kq_ready, 2 * KC * n + u - 1)
                    keys_queries(n, u)
                scores(n, 0, 0)
                if before:
                    pe.wait_ge(x_final, row - 1)
                    turn_probs(row - 1, 1, 0)
                    pe.wait_ge(kq_ready, 2 * KC * n + 2 * KC - 1)
                    turn_probs(row - 1, 1, 1)
                scores(n, 0, 1)
                if before:
                    weigh(row - 1, 1, 0)
                    turn_probs(row - 1, 1, 2)
                    weigh(row - 1, 1, 1)
                    turn_probs(row - 1, 1, 3)
                pe.wait_ge(kq_ready, 2 * KC * (n + 1))
                values(n, 0)
                if before:
                    weigh(row - 1, 1, 2)
                    weigh(row - 1, 1, 3)
                values(n, 1)
                if before:
                    project(row - 1)
                if more:
                    turn(n + 1, 0)
                    turn(n + 1, 1)
                scores(n, 1, 0)
                if before:
                    pe.wait_ge(x_final, row)
                turn_probs(row, 0, 0)
                if more:
                    pe.wait_ge(modulated, row + 3)
                else:
                    pe.wait_ge(v_ready, row + 1)
                turn_probs(row, 0, 1)
                scores(n, 1, 1)
                weigh(row, 0, 0)
                turn_probs(row, 0, 2)
                weigh(row, 0, 1)
                turn_probs(row, 0, 3)
                weigh(row, 0, 2)
                weigh(row, 0, 3)

            def last_tail():
                row = B - 1
                project(row - 1)
                pe.wait_ge(x_final, row)
                turn_probs(row, 1, 0)
                pe.wait_ge(v_ready, B)
                turn_probs(row, 1, 1)
                weigh(row, 1, 0)
                turn_probs(row, 1, 2)
                weigh(row, 1, 1)
                turn_probs(row, 1, 3)
                weigh(row, 1, 2)
                weigh(row, 1, 3)
                project(row)

            schedule(pe, first, pair_step, last_tail)

        @block.scalar
        def _(act):
            def modulate(n, tile):
                row = TPP * n + tile
                act.wait_ge(turned, row + 1)
                if not is_first(n):
                    act.wait_ge(xn_ready, row - 1)
                for k in range(KC):
                    last = nc.scalar.activation(xmod[:, tile, k, :], bank(4 + tile)[:, k * P:(k + 1) * P], ACT.Identity,
                                                bias=sh.tables[:, table, 1, k, bass.ds(row, 1)], scale=sh.tables[:, table, 0, k, bass.ds(row, 1)])
                last.then_inc(modulated, 1)

            def copy_probsT(row, tile):
                for m in range(KC):
                    act.wait_ge(probs_turned, KC * row + m + 1)
                    if m >= 2 or not is_first(row):
                        act.wait_ge(out_part, KC * row + m - 1)
                    nc.scalar.activation(probsT[:, m % 2, :], bank(probs_bank(tile, m)), ACT.Copy).then_inc(probsT_ready, 1)

            def exponentials(row):
                for e in range(2):
                    act.wait_ge(negmax_done, 2 * row + e + 1)
                    if not is_first(row):
                        act.wait_ge(probs_turned, KC * row - 2 + 2 * e)
                    for head in range(HALF * e, HALF * (e + 1)):
                        last = nc.scalar.activation(probs[:, head, :], s_ps[:, head, :], ACT.Exp, bias=negmax[:, head:head + 1],
                                                    scale=scale, accum_out=rowsum[:, head:head + 1])
                    last.then_inc(exp_done, 1)

            def first():
                act.wait_ge(sh.table_loaded["att"], 16)
                modulate(0, 0)
                modulate(0, 1)

            def pair_step(n, before, more):
                row = TPP * n
                if before:
                    copy_probsT(row - 1, 1)
                exponentials(row)
                act.wait_ge(piece_loaded, 16 * (n + 1))
                nc.scalar.activation(sh.w[prefetch_region][:, HI, bass.ds(n * PIECE, PIECE)], stage[:, :], ACT.Copy).then_inc(piece_hi, 1)
                if more:
                    modulate(n + 1, 0)
                    modulate(n + 1, 1)
                copy_probsT(row, 0)
                exponentials(row + 1)

            schedule(act, first, pair_step, lambda: copy_probsT(B - 1, 1))

        @block.vector
        def _(dve):
            def vec(name, m):
                row = VEC_ROWS[name][0] + m
                return sh.vecs[:, row:row + 1]

            def stats(n, tile):
                row = TPP * n + tile
                if is_first(n):
                    dve.wait_ge(opening_x, 16 * TPP)
                else:
                    dve.wait_ge(x_loaded[tile], 16 * n)
                nc.vector.bn_stats(bn[:, :], x[:, tile, :]).then_inc(raw_stats, 1)
                dve.wait_ge(raw_stats, row + 1)
                dve.sem_inc(passed, 1)
                nc.vector.bn_aggr(mv[:, tile, :], bn[:, :]).then_inc(stats_done, 1)
                dve.wait_ge(stats_done, row + 1)
                nc.vector.tensor_scalar(var_eps[:, tile:tile + 1], mv[:, tile, 1:2], eps, None, ALU.add).then_inc(var_done, 1)

            def normalise(n, tile):
                row = TPP * n + tile
                dve.wait_ge(rstd_done, row + 1)
                nc.vector.tensor_scalar(x[:, tile, :], x[:, tile, :], mv[:, tile, 0:1], rstd[:, tile:tile + 1],
                                        ALU.subtract, ALU.mult).then_inc(xhat_ready, 1)

            def split_xn(n, tile):
                row = TPP * n + tile
                dve.wait_ge(modulated, row + 1)
                hi = xn[:, HI, :, tile * P:(tile + 1) * P]
                nc.vector.tensor_copy(hi, xmod[:, tile, :, :]).then_inc(xhi_done, 1)
                dve.wait_ge(xhi_done, row + 1)
                nc.vector.tensor_tensor(xn[:, LO, :, tile * P:(tile + 1) * P], xmod[:, tile, :, :], f32(hi),
                                        ALU.subtract).then_inc(xn_ready, 1)

            def split_kq(n, u):
                m, dst, bias = u % KC, (kst, q)[u // KC], ("bk", "bq")[u // KC]
                src = bank(5 - u % 2)[:, 0:PT]
                dve.wait_ge(kq_done, 2 * KC * n + u + 1)
                if u == 0 and not is_first(n):
                    dve.wait_ge(diag_loaded, 16 * HPC * TPP * n)
                nc.vector.tensor_scalar(dst[:, HI, m, :], src, vec(bias, m), None, ALU.add).then_inc(kq_hi, 1)
                dve.wait_ge(kq_hi, 2 * KC * n + u + 1)
                nc.vector.scalar_tensor_tensor(out=dst[:, LO, m, :], in0=src, scalar=vec(bias, m), in1=f32(dst[:, HI, m, :]),
                                               op0=ALU.add, op1=ALU.subtract).then_inc(kq_ready, 1)

            def row_max(row, e):
                heads = slice(HALF * e, HALF * (e + 1))
                dve.wait_ge(scores_done, 2 * row + e + 1)
                nc.vector.tensor_reduce(smax[:, heads], s_ps[:, heads, :], AX.X, ALU.max).then_inc(max_done, 1)
                dve.wait_ge(max_done, 2 * row + e + 1)
                nc.vector.tensor_scalar(negmax[:, heads], smax[:, heads], -scale, None, ALU.mult).then_inc(negmax_done, 1)

            def divide(row, e):
                heads = slice(HALF * e, HALF * (e + 1))
                dve.wait_ge(exp_done, 2 * row + e + 1)
                nc.vector.reciprocal(inv[:, heads], rowsum[:, heads]).then_inc(inv_done, 1)
                dve.wait_ge(inv_done, 2 * row + e + 1)
                nc.vector.tensor_tensor(probs[:, heads, :], probs[:, heads, :], inv[:, heads].unsqueeze(2).to_broadcast([P, HALF, P]),
                                        ALU.mult).then_inc(probs_ready, 1)

            def copy_values(n, tile):
                dve.wait_ge(v_done, TPP * n + tile + 1)
                nc.vector.tensor_copy(v[:, tile, :], bank(4 + tile)).then_inc(v_ready, 1)

            def split_out(row):
                dve.wait_ge(out_part, KC * (row + 1))
                nc.vector.tensor_copy(oT[:, HI, :, :], o_ps[:, :, :]).then_inc(out_hi, 1)
                dve.wait_ge(out_hi, row + 1)
                nc.vector.tensor_tensor(oT[:, LO, :, :], o_ps[:, :, :], f32(oT[:, HI, :, :]), ALU.subtract).then_inc(out_ready, 1)

            def finish(row, tile):
                xt = residual[:, tile, :]
                dve.wait_ge(proj_done, row + 1)
                dve.wait_ge(bias_added, row + 1)
                nc.vector.tensor_tensor(xt, bank(6), xt, ALU.add).then_inc(x_final, 1)

            def first():
                for tile in range(TPP):
                    stats(0, tile)
                row = VEC_ROWS["bv"][0]
                bv = sh.vecs[:, row:row + KC].unsqueeze(2).to_broadcast([P, KC, P])
                nc.vector.tensor_copy(q[:, HI, :, 0:P], bv).then_inc(bv_hi, 1)
                dve.wait_ge(bv_hi, 1)
                nc.vector.tensor_tensor(q[:, LO, :, 0:P], bv, f32(q[:, HI, :, 0:P]), ALU.subtract).then_inc(bv_ready, 1)
                normalise(0, 0)
                normalise(0, 1)
                split_xn(0, 0)
                split_xn(0, 1)
                dve.wait_ge(const_loaded, 16)
                dve.wait_ge(bvo_done, 1)
                nc.vector.tensor_tensor(bo_bc[:, :], s_ps[:, 0:HPC, :].rearrange("p h k -> p (h k)"), bo_bc[:, :], ALU.add).then_inc(bo_ready, 1)

            def pair_step(n, before, more):
                row = TPP * n
                for u in range(KC):
                    split_kq(n, u)
                if before:
                    divide(row - 1, 0)
                    divide(row - 1, 1)
                split_kq(n, KC)
                if before:
                    finish(row - 2, 0)
                for u in range(KC + 1, 2 * KC):
                    split_kq(n, u)
                row_max(row, 0)
                row_max(row, 1)
                if more:
                    stats(n + 1, 0)
                    stats(n + 1, 1)
                copy_values(n, 0)
                if before:
                    split_out(row - 1)
                if more:
                    normalise(n + 1, 0)
                    normalise(n + 1, 1)
                divide(row, 0)
                copy_values(n, 1)
                divide(row, 1)
                if before:
                    finish(row - 1, 1)
                if more:
                    split_xn(n + 1, 0)
                row_max(row + 1, 0)
                if more:
                    split_xn(n + 1, 1)
                row_max(row + 1, 1)
                dve.wait_ge(piece_hi, n + 1)
                nc.vector.tensor_tensor(sh.w[prefetch_region][:, LO, bass.ds(n * PIECE, PIECE)], stage[:, :],
                                        f32(sh.w[prefetch_region][:, HI, bass.ds(n * PIECE, PIECE)]), ALU.subtract).then_inc(piece_done, 1)
                split_out(row)

            def last_tail():
                finish(B - 2, 0)
                divide(B - 1, 0)
                divide(B - 1, 1)
                split_out(B - 1)
                finish(B - 1, 1)

            schedule(dve, first, pair_step, last_tail)




def cond_seq_kernel(nc, t, out):
    with ExitStack() as ctx:
        sh = Shared(nc)
        with nc.sbuf_tensor("room", [P, 2 * REGION], F32) as room_tile:
            room = Room(room_tile)
        second_half = ctx.enter_context(nc.sbuf_tensor("weights1", [P, 2, REGION], F32R))
        sh.w = [ctx.enter_context(nc.sbuf_tensor("weights0", [P, 2, REGION], F32R)), second_half]
        sh.x = ctx.enter_context(nc.sbuf_tensor("x_tiles", [P, 2, TPB, D], F32))
        sh.tables = ctx.enter_context(nc.sbuf_tensor("mod_tables", [P, 2, 2, KC, B], F32))
        sh.ident = ctx.enter_context(nc.sbuf_tensor("ident", [P, P], F32))
        sh.vecs = ctx.enter_context(nc.sbuf_tensor("vecs", [P, N_VEC], F32))
        sh.mask = ctx.enter_context(nc.sbuf_tensor("mask", [P, B], F32))
        sh.neg_half = ctx.enter_context(nc.sbuf_tensor("neg_half", [P, 4], F32))
        sh.tables_dram = nc.dram_tensor("late_tables", (P, 2 * 2 * KC * B), F32, kind="Internal").ap()
        sh.gates_dram = nc.dram_tensor("gate_rows", (2, B, D), F32, kind="Internal").ap()
        sh.gate_bias_dram = nc.dram_tensor("gate_bias_rows", (2, B, D), F32, kind="Internal").ap()
        x0 = t["x"].rearrange("b s d -> (b s) d")
        x1, x2, x3 = (nc.dram_tensor(f"x{n}", (B * P, D), F32, kind="Internal").ap() for n in (1, 2, 3))
        x4 = out.rearrange("b s d -> (b s) d")

        def vec_column(*names):
            columns = [VEC_ROWS[n][0] + r for n in names for r in range(VEC_ROWS[n][1])]
            return lambda c: sh.vecs[:, columns[c]:columns[c] + 1]

        def tiles(regions):
            first = lambda part, k, c: w1_view(regions[c // 8], part)[:, k, (c % 8) * P:(c % 8 + 1) * P]
            second = lambda part, c: w2_view(regions[c // 8], part)[:, c % 8, :]
            return first, second

        ff = mlp_pieces((t["ff_w1"][:, 0:512], t["ff_w1"][:, 512:1024]), (t["ff_w2"][0:512, :], t["ff_w2"][512:1024, :]))
        att = attention_pieces((t["wk"], t["wq"], t["wv"], t["wo"]))
        ffn = [mlp_pieces((t["w1"][:, h:h + 512], t["w1"][:, h + 512:h + 1024]), (t["w2"][h:h + 512, :], t["w2"][h + 512:h + 1024, :]))
               for h in (0, HID)]

        ssm_stage = Stage(x0, x1, tiles([sh.w[0]]), vec_column("ssm_b1", "bwd_b1"), ACT.Gelu, 1e-6, table=0, gate=0,
                          masked=True, prefetch=ff, prefetch_region=1)
        ff_stage = Stage(x1, x2, tiles([sh.w[1]]), vec_column("ff_b1"), ACT.Gelu_apprx_tanh, 1e-6, table=1, gate=1,
                         prefetch=att, prefetch_region=0, following=("att", 0, 0, TPP))
        mlp_phase(nc, sh, "mlp", [ssm_stage, ff_stage], chunks=HID // P, room=room, t=t)
        sh.end_phase(nc)
        attention_phase(nc, sh, source=x2, target=x3, bo=t["bo"], eps=1e-5, table=0, prefetch=ffn[0], prefetch_region=1,
                        following=("ffn", 1, 1, TPB))
        sh.end_phase(nc)
        ffn_stage = Stage(x3, x4, tiles([sh.w[1], sh.w[0]]), vec_column("b1"), ACT.Gelu, 1e-5, table=1, bias2=t["b2"],
                          prefetch=ffn[1], prefetch_region=0)
        mlp_phase(nc, sh, "ffn", [ffn_stage], chunks=2 * HID // P, second_half_first=True)


_INS = ["x", "cond_1024", "mask_BxS_bk0"] + ["L0_cond_" + n for n in (
    "ada_w", "ada_b", "ssm_w1", "ssm_b1", "ssm_w2", "ssm_b2", "bwd_w1", "bwd_b1", "bwd_w2", "bwd_b2",
    "ffada_w", "ffada_b", "ff_w1", "ff_b1", "ff_w2", "ff_b2")] + ["L1_cond_" + n for n in (
    "ln1_w", "ln1_b", "ln2_w", "ln2_b", "wq", "bq", "wk", "bk", "wv", "bv", "wo", "bo",
    "wt_attn", "bt_attn", "wt_ffn", "bt_ffn", "w1", "b1", "w2", "b2")]
_SHORT = {"cond_1024": "cond", "mask_BxS_bk0": "mask"}


def kernel(**inputs):
    import numpy as _np
    import concourse.bacc as _bacc
    from concourse import mybir as _mybir
    from concourse.bass_utils import run_bass_kernel_spmd as _run

    nc = _bacc.Bacc("TRN2", target_bir_lowering=False, num_devices=1)
    arrays, tensors = {}, {}
    for name in _INS:
        a = _np.ascontiguousarray(inputs[name])
        arrays[f"in_{name}_dram"] = a
        ap = nc.dram_tensor(f"in_{name}_dram", a.shape, _mybir.dt.from_np(a.dtype), kind="ExternalInput").ap()
        tensors[_SHORT.get(name, name.removeprefix("L0_cond_").removeprefix("L1_cond_"))] = ap
    out = nc.dram_tensor("out_0_dram", (B, P, D), _mybir.dt.float32, kind="ExternalOutput").ap()
    cond_seq_kernel(nc, tensors, out)
    r = _run(nc, [arrays], core_ids=[0])
    return r.results[0]["out_0_dram"]
```

```python
from contextlib import ExitStack

import concourse.bass as bass
from concourse import mybir

ALU = mybir.AluOpType
ACT = mybir.ActivationFunctionType
AX = mybir.AxisListType
F32 = mybir.dt.float32
F32R = mybir.dt.float32r
U8 = mybir.dt.uint8

P = 128
B = 32
D = 512
KC = D // P
HEADS = 16
HD = D // HEADS
HPC = P // HD
HI, LO = 0, 1
REGION = 2 * KC * D * 2
HID = 1024
PIECE = 512
MUL_HI_LO = ((HI, HI), (HI, LO), (LO, HI))

VEC_ROWS = {}
for _name, _rows in (("ssm_b1", 4), ("bwd_b1", 4), ("ff_b1", 8), ("b1", 16), ("bq", 4), ("bk", 4), ("bv", 4),
                     ("ada_b", 8), ("ffada_b", 8), ("bt_attn", 8), ("bt_ffn", 8),
                     ("ln1_w", 4), ("ln1_b", 4), ("ln2_w", 4), ("ln2_b", 4)):
    VEC_ROWS[_name] = (sum(r for _, r in VEC_ROWS.values()), _rows)
N_VEC = sum(r for _, r in VEC_ROWS.values())


def f32(ap):
    return ap.bitcast(F32)


def w1_view(region, part):
    return region[:, part, 0:KC * HID].rearrange("p (k h) -> p k h", k=KC)


def w2_view(region, part):
    return region[:, part, KC * HID:].rearrange("p (c n) -> p c n", n=D)


def mlp_pieces(w1_halves, w2_halves):
    pieces = []
    for k in range(KC):
        for half in range(2):
            pieces.append((w1_halves[half][k * P:(k + 1) * P, :], k * HID + half * PIECE))
    for c in range(HID // P):
        pieces.append((w2_halves[c // KC][(c % KC) * P:(c % KC + 1) * P, :], KC * HID + c * D))
    return pieces


def attention_pieces(matrices):
    return [(w[k * P:(k + 1) * P, :], (n * KC + k) * D) for n, w in enumerate(matrices) for k in range(KC)]




LATE_ITEMS = ((1, "shift"), (1, "scale"), (2, "shift"), (2, "scale"), (3, "shift"), (3, "scale"))
HALF_D = D // 2
FIRST_RING = 12


class Room:

    def __init__(self, room):
        slots = [half * REGION + 2 * PIECE + n * KC * D for half in range(2) for n in range(3)]
        self.weights = [room[:, at:at + KC * D].rearrange("p (k n) -> p k n", k=KC) for at in slots]
        raw = [half * REGION + n * PIECE for half in range(2) for n in range(2)]
        raw += [slots[n] + k * PIECE for n in (4, 5) for k in range(KC)]
        self.raw = [room[:, at:at + PIECE] for at in raw]
        spare = [slots[2] + KC * D, slots[5] + KC * D]
        size = KC * B
        cut = lambda at, n: room[:, at + n * size:at + (n + 1) * size].rearrange("p (k b) -> p k b", k=KC)
        self.tables = [[cut(spare[0], 2 * n + kind) for kind in range(2)] for n in range(2)]
        self.tables_row = room[:, spare[0]:spare[0] + 4 * size]
        self.scaled = [cut(spare[0], 4 + n) for n in range(2)]
        self.shifted = [cut(spare[0], 6 + n) for n in range(2)]
        self.cond, self.silu = cut(spare[1], 0), cut(spare[1], 1)
        self.rows = [room[:, at:at + HALF_D] for at in (spare[1] + 2 * size, spare[1] + 2 * size + HALF_D)]


class Shared:

    def __init__(self, nc):
        self.semaphores = []
        lasting = lambda name: nc.alloc_semaphore(name=name)
        self.table_loaded = {phase: lasting("table_loaded_" + phase) for phase in ("att", "ffn")}
        self.stored = {phase: [lasting(f"stored{tile}_{phase}") for tile in range(4)] for phase in ("mlp", "att", "ffn")}

    def semaphore(self, nc, name):
        self.semaphores.append(nc.alloc_semaphore(name=name))
        return self.semaphores[-1]

    def vec(self, name, part):
        row = VEC_ROWS[name][0] + KC * part
        return self.vecs[:, row:row + KC].unsqueeze(2).to_broadcast([P, KC, B])

    def end_phase(self, nc):
        nc.clear_and_free_semaphores(self.semaphores)
        nc.all_engine_barrier()
        self.semaphores = []



TPB = 4
NBLK = B // TPB
TOK = TPB * P


class Opening:
    masked = False

    def __init__(self, phase, source, token_tiles, eps, place, dram_place):
        self.phase, self.source, self.token_tiles, self.eps = phase, source.rearrange("(n p) d -> n p d", p=P), token_tiles, eps
        self.table, self.dram_place = place, dram_place


class Stage:

    token_tiles = TPB

    def __init__(self, source, target, tiles, bias1, func, eps, table, gate=None, bias2=None, masked=False,
                 prefetch=(), prefetch_region=0, following=None):
        self.following = following
        self.source = source.rearrange("(n p) d -> n p d", p=P)
        self.target = target.rearrange("(n p) d -> n p d", p=P)
        self.tiles, self.bias1, self.func, self.eps, self.table = tiles, bias1, func, eps, table
        self.gate, self.bias2, self.masked = gate, bias2, masked
        self.prefetch, self.prefetch_region = prefetch, prefetch_region


def mlp_phase(nc, sh, name, stages, *, chunks, second_half_first=False, room=None, t=None):
    sem = lambda what: sh.semaphore(nc, f"{name}_{what}")
    gated = stages[0].gate is not None
    x_loaded = [sem(f"x_loaded{tile}") for tile in range(TPB)]
    stored = sh.stored[name]
    if room:
        cond_loaded, vec_loaded, mask_loaded, row_loaded = sem("cond_loaded"), sem("vec_loaded"), sem("mask_loaded"), sem("row_loaded")
        zeroed, ident_done, mask_f_done, vecs_done, mask_done = (
            sem("zeroed"), sem("ident_done"), sem("mask_f_done"), sem("vecs_done"), sem("mask_done"))
        cond_turned, vec_turned, mask_turned, cond_copied, silu_done = (
            sem("cond_turned"), sem("vec_turned"), sem("mask_turned"), sem("cond_copied"), sem("silu_done"))
        ada_loaded = [sem(f"ada_loaded{r}") for r in range(4)]
        products_done, rows_copied, rows_turned, first_table = (
            sem("products_done"), sem("rows_copied"), sem("rows_turned"), sem("first_table"))
        b2_added, gate_added, gates_done, gates_stored = sem("b2_added"), sem("gate_added"), sem("gates_done"), sem("gates_stored")
        first_loaded = [sem(f"first_loaded{r}") for r in range(FIRST_RING)]
        first_hi, first_lo_dve, first_lo_pool = sem("first_hi"), sem("first_lo_dve"), sem("first_lo_pool")
        late_loaded = [sem(f"late_loaded{n}") for n in range(len(LATE_ITEMS))]
        ada_items = [t["ada_w"][:, 0:D], t["ada_w"][:, D:2 * D], t["ada_w"][:, 2 * D:3 * D], t["ffada_w"][:, 2 * D:3 * D]]
        late_source = {1: t["ffada_w"], 2: t["wt_attn"], 3: t["wt_ffn"]}
        first_pieces = mlp_pieces((t["ssm_w1"], t["bwd_w1"]), (t["ssm_w2"], t["bwd_w2"]))
        first_pieces = first_pieces[0:8:2] + first_pieces[1:8:2] + first_pieces[8:]
    gate_loaded, bias_loaded = sem("gate_loaded"), sem("bias_loaded")
    late_multiplied, late_copied, late_turned, late_stored, late_chain = (
        sem("late_multiplied"), sem("late_copied"), sem("late_turned"), sem("late_stored"), sem("late_chain"))
    LATE_FIRST = 2
    LATE_DONE = sum(1 if kind == "shift" or s == 1 else 4 for s, kind in LATE_ITEMS)
    passed = sem("passed")
    raw_stats, stats_done, var_done, rstd_done, rstd_masked = (
        sem("raw_stats"), sem("stats_done"), sem("var_done"), sem("rstd_done"), sem("rstd_masked"))
    xhat_ready, turned, modulated, xhi_done, xn_ready = (
        sem("xhat_ready"), sem("turned"), sem("modulated"), sem("xhi_done"), sem("xn_ready"))
    m1_done, act_done, hhi_done, h_ready, m2_done = (
        sem("m1_done"), sem("act_done"), sem("hhi_done"), sem("h_ready"), sem("m2_done"))
    y_done, x_final, y_scaled, bias_masked, bias_added = (
        sem("y_done"), sem("x_final"), sem("y_scaled"), sem("bias_masked"), sem("bias_added"))
    STAGE_RING = 6 if second_half_first else 1
    piece_loaded = [sem(f"piece_loaded{r}") for r in range(STAGE_RING)]
    piece_hi, piece_done = sem("piece_hi"), sem("piece_done")
    total = NBLK * len(stages)
    ln = lambda count: count if room else count - TPB
    reached = lambda count: isinstance(count, int) and count < 1
    following = stages[-1].following
    for order, st in enumerate(stages + ([following] if following else [])):
        st.order = order

    with ExitStack() as local:
        sb = lambda what, shape, dt: local.enter_context(nc.sbuf_tensor(f"{name}_{what}", shape, dt))
        ps = lambda what, shape: local.enter_context(nc.psum_tensor(f"{name}_{what}", shape, F32))
        x = sh.x
        xhat = sb("xhat", [P, D], F32)
        xmod = sb("xmod", [P, KC, P], F32)
        xn = sh.xn
        g = sb("g", [P, TOK], F32)
        h = sb("h", [P, 2, 2, TOK], F32R)
        bias = sb("bias", [P, D], F32)
        if gated:
            tmp = sb("tmp", [P, D], F32)
            gate_bc = sb("gate", [P, TPB, D], F32)
        xhats, xmods = (xhat, g), (xmod, bias[:, :].rearrange("p (k q) -> p k q", k=KC))
        bn = sb("bn", [P, TPB, 6], F32)
        mv = sb("mv", [P, TPB, 2], F32)
        var_eps = sb("var_eps", [P, TPB], F32)
        rstd = sb("rstd", [P, TPB], F32)
        rstd_m = sb("rstd_m", [P, TPB], F32)
        stage = sb("stage", [P, STAGE_RING, PIECE], F32)
        y_ps = ps("y", [P, TPB, D])
        m1_ps = ps("m1", [P, 2, TOK])
        turn_ps = ps("turn", [P, 2, KC * P])
        if room:
            mask_u8 = sb("mask_u8", [B, P], U8)
            cond = tmp[0:B, :]
            vec_rows, mask_f = g[:, 0:P], g[0:B, P:2 * P]
            gates = gate_bc[:, 0:2, 0:HALF_D]
            bwd_b2, rows = gate_bc[0:2 * B, 2, 0:HALF_D], gate_bc[:, 3, 0:HALF_D]
            cond_ps, vec_ps, item_ps, rows_ps = (y_ps[:, n, :] for n in range(TPB))

        def schedule(eng, first, block_step):
            first()
            for s, st in enumerate(stages):
                base = NBLK * s
                block_step(base, 0, stages[max(s - 1, 0)], st, st)
                with eng.Fori(0, NBLK // 2 - 1) as i:
                    block_step(2 * i + (base + 1), 1, st, st, st)
                    block_step(2 * i + (base + 2), 0, st, st, st)
                block_step(base + NBLK - 1, 1, st, st, stages[s + 1] if s + 1 < len(stages) else following)

        def batch_row(st, n, tile):
            return TPB * n + tile - B * st.order

        def piece_steps(n):
            return (TPB if room and isinstance(n, int) and n == 0 else 0, chunks - 1)

        TURN_STEP = 2

        block = local.enter_context(nc.Block())

        @block.sync
        def _(sp):
            def load_x(st, n, parity, tile):
                sp.dma_start(x[:, parity, tile, :], st.source[batch_row(st, n, tile)]).then_inc(x_loaded[tile], 16)

            def store(st, n, parity, tile):
                sp.wait_ge(x_final, TPB * n + tile + 1)
                sp.sem_inc(passed, 1)
                sp.dma_start(st.target[batch_row(st, n, tile)], x[:, parity, tile, :]).then_inc(stored[tile], 16)

            def load_gate(st, n):
                row = sh.gates_dram[st.gate].rearrange("(n t) d -> n (t d)", t=TPB)[bass.ds(n - NBLK * st.order, 1), :]
                sp.dma_start(gate_bc[:, :, :].rearrange("p t d -> p (t d)"), row.to_broadcast([P, TPB * D])).then_inc(gate_loaded, 16)

            def load_own_piece(q):
                if q >= STAGE_RING:
                    sp.wait_ge(piece_done, q - STAGE_RING + 1)
                sp.dma_start(stage[:, q % STAGE_RING, :], stages[0].prefetch[q][0]).then_inc(piece_loaded[q % STAGE_RING], 16)

            def load_raw(q):
                if q >= FIRST_RING:
                    sp.wait_ge(first_lo_pool if q % 2 else first_lo_dve, (q - FIRST_RING) // 2 + 1)
                sp.dma_start(room.raw[q % FIRST_RING], first_pieces[q][0]).then_inc(first_loaded[q % FIRST_RING], 16)

            def load_ada(n):
                sp.dma_start(room.weights[n], ada_items[n].rearrange("(k p) n -> p k n", p=P)).then_inc(ada_loaded[n], 16)

            def load_late(n):
                s, kind = LATE_ITEMS[n]
                at = D * ("shift", "scale").index(kind)
                sp.dma_start(room.weights[n], late_source[s][:, at:at + D].rearrange("(k p) n -> p k n", p=P)).then_inc(late_loaded[n], 16)

            def first():
                if room:
                    sp.dma_start(cond, t["cond"]).then_inc(cond_loaded, 16)
                    load_ada(0)
                    load_ada(1)
                    for tile in range(TPB):
                        load_x(stages[0], 0, 0, tile)
                    for vec_name, (row, count) in VEC_ROWS.items():
                        vector = t[vec_name][0:count * P].rearrange("(c p) -> c p", p=P)
                        sp.dma_start(vec_rows[row:row + count, :], vector).then_inc(vec_loaded, 16)
                    for q in range(10):
                        load_raw(q)
                    load_ada(2)
                    load_raw(10)
                    load_raw(11)
                    load_ada(3)
                    for q in range(12, len(first_pieces)):
                        load_raw(q)
                else:
                    for q in range(STAGE_RING):
                        load_own_piece(q)
                    for tile in range(TPP):
                        sp.wait_ge(sh.stored["att"][tile], 16 * NPAIR)
                    for tile in range(TPB):
                        load_x(stages[0], 0, 0, tile)

            def block_step(n, parity, before, st, after):
                if isinstance(n, int) and n == 0:
                    for tile in range(TPB):
                        sp.wait_ge(x_loaded[tile], 16)
                        load_x(after, 1, 1, tile)
                    if second_half_first:
                        for q in range(STAGE_RING, len(st.prefetch)):
                            load_own_piece(q)
                    if room:
                        sp.wait_ge(products_done, 1)
                        load_late(0)
                        load_late(1)
                        sp.wait_ge(gates_done, 1)
                        for s in range(2):
                            for half in range(2):
                                unit, columns = slice((2 * s + half) * B, (2 * s + half + 1) * B), slice(half * HALF_D, (half + 1) * HALF_D)
                                sp.dma_start(sh.gates_dram[s][:, columns], gates[unit, 0, :]).then_inc(gates_stored, 16)
                                sp.dma_start(sh.gate_bias_dram[s][:, columns], gates[unit, 1, :]).then_inc(gates_stored, 16)
                        for item in (2, 3):
                            sp.wait_ge(late_loaded[item - 2], 16)
                            load_late(item)
                        sp.wait_ge(first_lo_dve, len(first_pieces) // 2)
                        sp.wait_ge(first_lo_pool, len(first_pieces) // 2)
                        for item in (4, 5):
                            sp.wait_ge(late_loaded[item - 2], 16)
                            load_late(item)
                        sp.wait_ge(gates_stored, 128)
                        load_gate(stages[0], 0)
                        sp.wait_ge(late_chain, LATE_DONE)
                        sp.dma_start(sh.tables_dram, room.tables_row).then_inc(late_stored, 16)
                    return

                def load_next(tile):
                    if after is not None and tile < after.token_tiles:
                        sp.wait_ge(stored[tile], 16 * n)
                        sp.sem_inc(passed, 1)
                        load_x(after, n + 1, 1 - parity, tile)

                store(before, n - 1, 1 - parity, 0)
                store(before, n - 1, 1 - parity, 1)
                load_next(0)
                store(before, n - 1, 1 - parity, 2)
                load_next(1)
                store(before, n - 1, 1 - parity, 3)
                if gated:
                    load_gate(st, n)
                load_next(2)
                load_next(3)
                if following and isinstance(n, int) and n == NBLK:
                    sp.wait_ge(modulated, TPB * NBLK)
                    sp.wait_ge(late_stored, 16)
                    sp.dma_start(sh.tables[:, following.table, :, :, :].rearrange("p a k b -> p (a k b)"),
                                 sh.tables_dram[:, following.dram_place * 2 * KC * B:(following.dram_place + 1) * 2 * KC * B]
                                 ).then_inc(sh.table_loaded[following.phase], 16)

            schedule(sp, first, block_step)
            for tile in range(TPB):
                store(stages[-1], total - 1, 1, tile)
            if not following:
                for tile in range(TPB):
                    sp.wait_ge(stored[tile], 16 * total)

        @block.gpsimd
        def _(pool):
            def rstd_of(n, tile):
                pool.wait_ge(var_done, ln(TPB * n + tile + 1))
                if not reached(ln(TPB * (n - 1) + tile + 1)):
                    pool.wait_ge(xhat_ready, ln(TPB * (n - 1) + tile + 1))
                nc.gpsimd.tensor_tensor(rstd[:, tile:tile + 1], var_eps[:, tile:tile + 1], sh.neg_half[:, 0:1], ALU.pow).then_inc(rstd_done, 1)

            def add_bias(st, n, tile):
                row, added = batch_row(st, n, tile), TPB * n + tile
                xt = x[:, n % 2, tile, :]
                if not gated:
                    if n == 0:
                        pool.wait_ge(x_loaded[tile], 16)
                    nc.gpsimd.tensor_tensor(xt, xt, bias[:, :], ALU.add).then_inc(bias_added, 1)
                    return
                if added:
                    pool.wait_ge(bias_added, added)
                if not added:
                    pool.wait_ge(gates_stored, 128)
                    pool.wait_ge(xn_ready, TPB)
                pool.dma_start(bias[:, :], sh.gate_bias_dram[st.gate][row:row + 1, :].to_broadcast([P, D])).then_inc(bias_loaded, 16)
                pool.wait_ge(bias_loaded, 16 * (added + 1))
                if st.masked:
                    nc.gpsimd.tensor_scalar(bias[:, :], bias[:, :], sh.mask[:, row:row + 1], 1.0, ALU.mult, ALU.mult).then_inc(bias_masked, 1)
                    pool.wait_ge(bias_masked, added + 1)
                nc.gpsimd.tensor_tensor(xt, xt, bias[:, :], ALU.add).then_inc(bias_added, 1)

            def load_piece(st, q):
                if q >= STAGE_RING:
                    pool.wait_ge(piece_done, q - STAGE_RING + 1)
                pool.dma_start(stage[:, q % STAGE_RING, :], st.prefetch[q % len(st.prefetch)][0]).then_inc(piece_loaded[q % STAGE_RING], 16)

            def first_low(q):
                at = first_pieces[q][1]
                pool.wait_ge(first_hi, q + 1)
                nc.gpsimd.tensor_tensor(sh.w[0][:, LO, at:at + PIECE], room.raw[q % FIRST_RING],
                                        f32(sh.w[0][:, HI, at:at + PIECE]), ALU.subtract).then_inc(first_lo_pool, 1)

            if room:
                nc.gpsimd.memset(sh.ident[:, :], 0.0).then_inc(zeroed, 1)
                pool.wait_ge(zeroed, 1)
                nc.gpsimd.affine_select(out=sh.ident[:, :], in_=sh.ident[:, :], compare_op=ALU.not_equal, fill=1.0,
                                        base=0, pattern=[[-1, P]], channel_multiplier=1).then_inc(ident_done, 1)
                nc.gpsimd.memset(sh.neg_half[:, :], -0.5).then_inc(zeroed, 1)
                for half in range(2):
                    over_rows = lambda vector: vector[half * HALF_D:(half + 1) * HALF_D].rearrange("(a n) -> a n", a=1).to_broadcast([B, HALF_D])
                    ssm, ff = slice(half * B, (half + 1) * B), slice((2 + half) * B, (3 + half) * B)
                    pool.dma_start(gates[ssm, 0, :], over_rows(t["ada_b"][2 * D:3 * D])).then_inc(row_loaded, 16)
                    pool.dma_start(gates[ff, 0, :], over_rows(t["ffada_b"][2 * D:3 * D])).then_inc(row_loaded, 16)
                    pool.dma_start(gates[ssm, 1, :], over_rows(t["ssm_b2"])).then_inc(row_loaded, 16)
                    pool.dma_start(gates[ff, 1, :], over_rows(t["ff_b2"])).then_inc(row_loaded, 16)
                    pool.dma_start(bwd_b2[ssm], over_rows(t["bwd_b2"])).then_inc(row_loaded, 16)
                pool.wait_ge(zeroed, 2)
                rstd_of(0, 0)
                rstd_of(0, 1)
                first_low(1)
                rstd_of(0, 2)
                rstd_of(0, 3)
                for q in range(3, len(first_pieces), 2):
                    first_low(q)
            if not gated:
                pool.dma_start(bias[:, :], stages[0].bias2.rearrange("(a n) -> a n", a=1).to_broadcast([P, D])).then_inc(bias_loaded, 16)
                pool.wait_ge(bias_loaded, 16)
            if not second_half_first:
                load_piece(stages[0], 0)
            for n in range(total):
                st = stages[n // NBLK]
                if not reached(ln(TPB * (n + 1))):
                    pool.wait_ge(xhat_ready, ln(TPB * (n + 1)))
                if not second_half_first and not (room and n == 0):
                    load_piece(st, 2 * n + 1)
                for tile in range(TPB):
                    if n + 1 < total or (following and tile < following.token_tiles):
                        rstd_of(n + 1, tile)
                    if room and n == 0:
                        if tile == 2:
                            add_bias(st, n, 0)
                        if tile == 3:
                            load_piece(st, 1)
                            for late_tile in (1, 2, 3):
                                add_bias(st, n, late_tile)
                    else:
                        add_bias(st, n, tile)
                if not second_half_first:
                    if n + 1 < total:
                        load_piece(stages[(n + 1) // NBLK], 2 * n + 2)

        @block.tensor
        def _(pe):
            def turn(n, tile):
                source = xhats[tile % 2] if isinstance(n, int) and n == 0 else xhat
                pe.wait_ge(xhat_ready, ln(TPB * n + tile + 1))
                if not reached(ln(TPB * n + tile - 1)):
                    pe.wait_ge(modulated, ln(TPB * n + tile - 1))
                if room and not isinstance(n, int):
                    pe.wait_ge(late_chain, LATE_DONE)
                for k in range(KC):
                    last = nc.tensor.transpose(turn_ps[:, tile % 2, k * P:(k + 1) * P], source[:, k * P:(k + 1) * P], sh.ident[:, :])
                last.then_inc(turned, 1)

            def first_product(st, n, parity, c):
                if c == 0 and not reached(ln(TPB * (n + 1))):
                    pe.wait_ge(xn_ready, ln(TPB * (n + 1)))
                if not (isinstance(n, int) and n == 0 and c < 2):
                    pe.wait_ge(act_done, chunks * n + c - 1)
                if second_half_first and isinstance(n, int) and n == 0 and c == HID // P:
                    pe.wait_ge(piece_done, 2 * KC)
                if not second_half_first and isinstance(n, int) and n == NBLK * st.order and n and c == 0:
                    pe.wait_ge(piece_done, 2 * n)
                if room and isinstance(n, int) and n == 0 and c == 0:
                    pe.wait_ge(first_lo_dve, 2)
                    pe.wait_ge(first_lo_pool, 2)
                if room and isinstance(n, int) and n == 0 and c == KC:
                    pe.wait_ge(first_lo_dve, 4)
                    pe.wait_ge(first_lo_pool, 4)
                steps = [(k, a, b) for k in range(KC) for a, b in MUL_HI_LO]
                for s, (k, a, b) in enumerate(steps):
                    last = nc.tensor.matmul(m1_ps[:, c % 2, :], st.tiles[0](a, k, c), xn[:, parity, b, k, :],
                                            start=s == 0, stop=s == len(steps) - 1)
                last.then_inc(m1_done, 1)

            def second_product(st, n, c):
                if room and isinstance(n, int) and n == 0:
                    if c % 2:
                        pe.wait_ge(first_lo_pool, KC + c // 2 + 1)
                    else:
                        pe.wait_ge(first_lo_dve, KC + c // 2 + 1)
                if second_half_first and isinstance(n, int) and n == 0 and c >= HID // P:
                    pe.wait_ge(piece_done, 2 * KC + c - HID // P + 1)
                pe.wait_ge(h_ready, chunks * n + c + 1)
                for tile in range(TPB):
                    if c == 0 and not (isinstance(n, int) and n == 0):
                        if gated:
                            pe.wait_ge(y_scaled, TPB * (n - 1) + tile + 1)
                        else:
                            pe.wait_ge(x_final, TPB * (n - 1) + tile + 1)
                    for s, (a, b) in enumerate(MUL_HI_LO):
                        last = nc.tensor.matmul(y_ps[:, tile, :], h[:, c % 2, a, tile * P:(tile + 1) * P], st.tiles[1](b, c),
                                                start=c == 0 and s == 0, stop=c == chunks - 1 and s == 2)
                    if c == chunks - 1:
                        last.then_inc(y_done, 1)
                if c < chunks - 1:
                    last.then_inc(m2_done, 1)

            def pair_product(out, cond_in, weights):
                for k in range(KC):
                    for unit in range(4):
                        item, half = divmod(unit, 2)
                        last = nc.tensor.matmul(out[unit * B:(unit + 1) * B, 0:HALF_D], cond_in[:, k, :],
                                                weights[item][:, k, half * HALF_D:(half + 1) * HALF_D], start=k == 0, stop=k == KC - 1)
                return last

            def turn_pair(out, rows):
                by_unit = out[:, 0:HALF_D].rearrange("p (u c b) -> p c u b", u=4, c=2)
                for c in range(2):
                    last = nc.tensor.transpose(by_unit[:, c], rows[:, c * P:(c + 1) * P], sh.ident[:, :])
                return last

            def late_product(group):
                pe.wait_ge(late_loaded[2 * group], 16)
                pe.wait_ge(late_loaded[2 * group + 1], 16)
                pair_product(turn_ps[:, group % 2, :], room.cond if group else room.silu,
                             room.weights[2 * group:2 * group + 2]).then_inc(late_multiplied, 1)

            def late_turn(group):
                pe.wait_ge(late_copied, group + 1)
                turn_pair(turn_ps[:, group % 2, :], room.rows[group % 2]).then_inc(late_turned, 1)

            def ada_product(out, pair):
                pe.wait_ge(ada_loaded[2 * pair], 16)
                pe.wait_ge(ada_loaded[2 * pair + 1], 16)
                pair_product(out, room.silu, room.weights[2 * pair:2 * pair + 2]).then_inc(products_done, 1)

            def opening():
                pe.wait_ge(ident_done, 1)
                pe.wait_ge(cond_loaded, 16)
                for k in range(KC):
                    last = nc.tensor.transpose(cond_ps[:, k * B:(k + 1) * B], cond[:, k * P:(k + 1) * P], sh.ident[0:B, 0:B])
                last.then_inc(cond_turned, 1)
                pe.wait_ge(mask_f_done, 1)
                pe.wait_ge(cond_copied, 1)
                nc.tensor.transpose(cond_ps[:, P:P + B], mask_f, sh.ident[0:B, 0:B]).then_inc(mask_turned, 1)
                pe.wait_ge(silu_done, 1)
                ada_product(item_ps, 0)
                pe.wait_ge(vec_loaded, 16 * len(VEC_ROWS))
                nc.tensor.transpose(vec_ps[:, 0:N_VEC], vec_rows[0:N_VEC, :], sh.ident[0:N_VEC, 0:N_VEC]).then_inc(vec_turned, 1)
                pe.wait_ge(rows_copied, 1)
                turn_pair(rows_ps, rows).then_inc(rows_turned, 1)

            def first():
                if room:
                    opening()
                    for tile in range(TPB):
                        turn(0, tile)

            def block_step(n, parity, before, st, after):
                first_product(st, n, parity, 0)
                for c in range(chunks):
                    if c + 1 < chunks:
                        first_product(st, n, parity, c + 1)
                    second_product(st, n, c)
                    if room and isinstance(n, int) and n == 0 and c == 0:
                        pe.wait_ge(modulated, TPB)
                        ada_product(turn_ps[:, 1, :], 1)
                    if room and isinstance(n, int) and n == 0 and c == TURN_STEP + 1:
                        pe.wait_ge(gate_added, 1)
                    if after is not None and TURN_STEP <= c < TURN_STEP + after.token_tiles:
                        turn(n + 1, c - TURN_STEP)
                    if room and isinstance(n, int) and n == 0 and c == chunks - 3:
                        pe.wait_ge(modulated, 2 * TPB - 1)
                        late_product(0)
                    if room and isinstance(n, int) and n == 0 and c == chunks - 2:
                        late_turn(0)
                        pe.wait_ge(modulated, 2 * TPB)
                        late_product(1)
                    if room and isinstance(n, int) and n == 0 and c == chunks - 1:
                        late_turn(1)
                        pe.wait_ge(late_chain, LATE_FIRST)
                        late_product(2)
                if room and isinstance(n, int) and n == 0:
                    late_turn(2)

            schedule(pe, first, block_step)

        @block.scalar
        def _(act):
            def modulate(st, n, tile):
                row = batch_row(st, n, tile)
                act.wait_ge(turned, ln(TPB * n + tile + 1))
                if room and st.order == 1 and isinstance(n, int) and row == 0:
                    act.wait_ge(late_chain, LATE_DONE)
                if st is following and row == 0:
                    act.wait_ge(sh.table_loaded[following.phase], 16)
                target = xmod
                if isinstance(n, int) and n == 0:
                    target = xmods[tile % 2]
                    if tile >= 2:
                        act.wait_ge(xn_ready, tile - 1)
                elif not reached(ln(TPB * n + tile)):
                    act.wait_ge(xn_ready, ln(TPB * n + tile))
                for k in range(KC):
                    last = nc.scalar.activation(target[:, k, :], turn_ps[:, tile % 2, k * P:(k + 1) * P], ACT.Identity,
                                                bias=sh.tables[:, st.table, 1, k, bass.ds(row, 1)], scale=sh.tables[:, st.table, 0, k, bass.ds(row, 1)])
                last.then_inc(modulated, 1)

            def activate(st, n, c):
                act.wait_ge(m1_done, chunks * n + c + 1)
                if not (isinstance(n, int) and n == 0 and c == 0):
                    act.wait_ge(h_ready, chunks * n + c)
                nc.scalar.activation(g[:, :], m1_ps[:, c % 2, :], st.func, bias=st.bias1(c)).then_inc(act_done, 1)

            def piece_high(st, n, q, at, slot, turns):
                act.wait_ge(piece_loaded[slot], 16 * (turns + 1))
                if room and not isinstance(n, int):
                    act.wait_ge(late_turned, 2)
                if room and isinstance(n, int) and n == NBLK - 1:
                    act.wait_ge(late_stored, 16)
                nc.scalar.activation(sh.w[st.prefetch_region][:, HI, bass.ds(at, PIECE)], stage[:, slot, :], ACT.Copy).then_inc(piece_hi, 1)

            def first_high(q):
                at = first_pieces[q][1]
                act.wait_ge(first_loaded[q % FIRST_RING], 16 * (q // FIRST_RING + 1))
                nc.scalar.activation(sh.w[0][:, HI, at:at + PIECE], room.raw[q % FIRST_RING], ACT.Copy).then_inc(first_hi, 1)

            def first():
                if room:
                    act.dma_start(mask_u8[:, :], t["mask"]).then_inc(mask_loaded, 16)
                    act.wait_ge(cond_copied, 1)
                    nc.scalar.activation(room.silu, room.cond, ACT.Silu).then_inc(silu_done, 1)
                    first_high(0)
                    first_high(1)
                    act.wait_ge(first_table, 2)
                    for tile in range(TPB):
                        modulate(stages[0], 0, tile)
                        if tile in (1, 2):
                            first_high(tile + 1)
                    for q in range(4, 10):
                        first_high(q)

            def block_step(n, parity, before, st, after):
                activate(st, n, 0)
                for c in range(chunks):
                    if second_half_first and isinstance(n, int) and n == 0 and 2 * c < len(st.prefetch):
                        for q in (2 * c, 2 * c + 1):
                            piece_high(st, n, q, st.prefetch[q][1], q % STAGE_RING, q // STAGE_RING)
                    if room and isinstance(n, int) and n == 0 and c < 3:
                        first_high(10 + 2 * c)
                        first_high(11 + 2 * c)
                    if c + 1 < chunks:
                        activate(st, n, c + 1)
                    if after is not None and TURN_STEP <= c < TURN_STEP + after.token_tiles:
                        modulate(after, n + 1, c - TURN_STEP)
                    if not second_half_first and c in piece_steps(n):
                        q = 2 * n + (c == chunks - 1)
                        local_n = n - NBLK * st.order
                        piece_high(st, n, q, (2 * local_n + (c == chunks - 1)) * PIECE, 0, q)

            schedule(act, first, block_step)

        @block.vector
        def _(dve):
            def stats(st, n, parity, tile):
                count = ln(TPB * n + tile + 1)
                dve.wait_ge(x_loaded[tile], 16 * (n + 1))
                nc.vector.bn_stats(bn[:, tile, :], x[:, parity, tile, :]).then_inc(raw_stats, 1)
                dve.wait_ge(raw_stats, count)
                dve.sem_inc(passed, 1)
                nc.vector.bn_aggr(mv[:, tile, :], bn[:, tile, :]).then_inc(stats_done, 1)
                dve.wait_ge(stats_done, count)
                nc.vector.tensor_scalar(var_eps[:, tile:tile + 1], mv[:, tile, 1:2], st.eps, None, ALU.add).then_inc(var_done, 1)

            def normalise(st, n, parity, tile):
                row = TPB * n + tile
                dve.wait_ge(rstd_done, ln(row + 1))
                r = rstd[:, tile:tile + 1]
                if st.masked:
                    nc.vector.tensor_tensor(rstd_m[:, tile:tile + 1], r, sh.mask[:, bass.ds(row, 1)], ALU.mult).then_inc(rstd_masked, 1)
                    dve.wait_ge(rstd_masked, row + 1)
                    r = rstd_m[:, tile:tile + 1]
                target = xhat
                if isinstance(n, int) and n == 0:
                    target = xhats[tile % 2]
                    if tile >= 2:
                        dve.wait_ge(turned, tile - 1)
                elif not reached(ln(row)):
                    dve.wait_ge(turned, ln(row))
                nc.vector.tensor_scalar(target[:, :], x[:, parity, tile, :], mv[:, tile, 0:1], r,
                                        ALU.subtract, ALU.mult).then_inc(xhat_ready, 1)

            def split_xn(n, parity, tile):
                dve.wait_ge(modulated, ln(TPB * n + tile + 1))
                hi = xn[:, parity, HI, :, tile * P:(tile + 1) * P]
                source = xmods[tile % 2] if isinstance(n, int) and n == 0 else xmod
                nc.vector.tensor_copy(hi, source[:, :, :]).then_inc(xhi_done, 1)
                dve.wait_ge(xhi_done, ln(TPB * n + tile + 1))
                nc.vector.tensor_tensor(xn[:, parity, LO, :, tile * P:(tile + 1) * P], source[:, :, :], f32(hi),
                                        ALU.subtract).then_inc(xn_ready, 1)

            def split_h(n, c):
                dve.wait_ge(act_done, chunks * n + c + 1)
                if c >= 2 or (c == 0 and not (isinstance(n, int) and n == 0)):
                    dve.wait_ge(m2_done, (chunks - 1) * n + max(c - 1, 0))
                elif not (isinstance(n, int) and n == 0):
                    dve.wait_ge(y_done, TPB * n)
                nc.vector.tensor_copy(h[:, c % 2, HI, :], g[:, :]).then_inc(hhi_done, 1)
                dve.wait_ge(hhi_done, chunks * n + c + 1)
                nc.vector.tensor_tensor(h[:, c % 2, LO, :], g[:, :], f32(h[:, c % 2, HI, :]), ALU.subtract).then_inc(h_ready, 1)

            def finish(st, n, parity, tile):
                row = TPB * n + tile
                xt = x[:, parity, tile, :]
                dve.wait_ge(y_done, row + 1)
                if tile == 0 and gated:
                    dve.wait_ge(gate_loaded, 16 * (n + 1))
                if not gated:
                    dve.wait_ge(bias_added, row + 1)
                    nc.vector.tensor_tensor(xt, y_ps[:, tile, :], xt, ALU.add).then_inc(x_final, 1)
                    return
                if not (isinstance(n, int) and row == 0):
                    dve.wait_ge(x_final, row)
                if st.masked:
                    nc.vector.scalar_tensor_tensor(out=tmp[:, :], in0=y_ps[:, tile, :], scalar=sh.mask[:, bass.ds(row, 1)],
                                                   in1=gate_bc[:, tile, :], op0=ALU.mult, op1=ALU.mult).then_inc(y_scaled, 1)
                else:
                    nc.vector.tensor_tensor(tmp[:, :], y_ps[:, tile, :], gate_bc[:, tile, :], ALU.mult).then_inc(y_scaled, 1)
                dve.wait_ge(y_scaled, row + 1)
                dve.wait_ge(bias_added, row + 1)
                nc.vector.tensor_tensor(xt, xt, tmp[:, :], ALU.add).then_inc(x_final, 1)

            def piece_low(st, q, at, slot):
                w = sh.w[st.prefetch_region]
                dve.wait_ge(piece_hi, q + 1)
                nc.vector.tensor_tensor(w[:, LO, bass.ds(at, PIECE)], stage[:, slot, :],
                                        f32(w[:, HI, bass.ds(at, PIECE)]), ALU.subtract).then_inc(piece_done, 1)

            def late_copy(group):
                dve.wait_ge(late_multiplied, group + 1)
                if group == 2:
                    dve.wait_ge(late_turned, 1)
                nc.vector.tensor_copy(room.rows[group % 2], turn_ps[:, group % 2, 0:HALF_D]).then_inc(late_copied, 1)

            late_links = [0]

            def link(ins):
                late_links[0] += 1
                ins.then_inc(late_chain, 1)
                dve.wait_ge(late_chain, late_links[0])

            def late_tables(group):
                dve.wait_ge(late_turned, group + 1)
                raw = turn_ps[:, group % 2, 0:HALF_D].rearrange("p (j k b) -> p j k b", j=2, k=KC)
                bias_name = ("ffada_b", "bt_attn", "bt_ffn")[group]
                scale_tab, shift_tab = (sh.tables[:, 1, 0, :, :], sh.tables[:, 1, 1, :, :]) if group == 0 else room.tables[group - 1]
                scaled = scale_tab if group == 0 else room.scaled[group - 1]
                link(nc.vector.tensor_tensor(shift_tab, raw[:, 0], sh.vec(bias_name, 0), ALU.add))
                link(nc.vector.scalar_tensor_tensor(out=scaled, in0=raw[:, 1], scalar=1.0, in1=sh.vec(bias_name, 1),
                                                    op0=ALU.add, op1=ALU.add))
                if group:
                    norm, shifted = ("ln1", "ln2")[group - 1], room.shifted[group - 1]
                    link(nc.vector.tensor_tensor(scale_tab, scaled, sh.vec(norm + "_w", 0), ALU.mult))
                    link(nc.vector.tensor_tensor(shifted, scaled, sh.vec(norm + "_b", 0), ALU.mult))
                    link(nc.vector.tensor_tensor(shift_tab, shift_tab, shifted, ALU.add))

            def opening():
                dve.wait_ge(cond_turned, 1)
                nc.vector.tensor_copy(room.cond, cond_ps[:, 0:KC * B].rearrange("p (k b) -> p k b", k=KC)).then_inc(cond_copied, 1)
                dve.wait_ge(mask_loaded, 16)
                nc.vector.tensor_scalar(mask_f, mask_u8[:, :], 0.0, None, ALU.not_equal).then_inc(mask_f_done, 1)
                dve.wait_ge(mask_turned, 1)
                nc.vector.tensor_copy(sh.mask[:, :], cond_ps[:, P:P + B]).then_inc(mask_done, 1)

            def first_table_rows():
                dve.wait_ge(products_done, 1)
                nc.vector.tensor_copy(rows, item_ps[:, 0:HALF_D]).then_inc(rows_copied, 1)
                dve.wait_ge(vec_turned, 1)
                nc.vector.tensor_copy(sh.vecs[:, :], vec_ps[:, 0:N_VEC]).then_inc(vecs_done, 1)

            def make_first_table():
                dve.wait_ge(vecs_done, 1)
                dve.wait_ge(rows_turned, 1)
                raw = rows_ps[:, 0:HALF_D].rearrange("p (j k b) -> p j k b", j=2, k=KC)
                nc.vector.tensor_tensor(sh.tables[:, 0, 1, :, :], raw[:, 0], sh.vec("ada_b", 0), ALU.add).then_inc(first_table, 1)
                nc.vector.scalar_tensor_tensor(out=sh.tables[:, 0, 0, :, :], in0=raw[:, 1], scalar=1.0, in1=sh.vec("ada_b", 1),
                                               op0=ALU.add, op1=ALU.add).then_inc(first_table, 1)

            def make_gates():
                dve.wait_ge(row_loaded, 160)
                nc.vector.tensor_tensor(gates[0:2 * B, 1, :], gates[0:2 * B, 1, :], bwd_b2, ALU.add).then_inc(b2_added, 1)
                dve.wait_ge(products_done, 2)
                dve.wait_ge(b2_added, 1)
                nc.vector.tensor_tensor(gates[:, 0, :], turn_ps[:, 1, 0:HALF_D], gates[:, 0, :], ALU.add).then_inc(gate_added, 1)
                dve.wait_ge(gate_added, 1)
                nc.vector.tensor_tensor(gates[:, 1, :], gates[:, 0, :], gates[:, 1, :], ALU.mult).then_inc(gates_done, 1)

            def first_low(q):
                at = first_pieces[q][1]
                dve.wait_ge(first_hi, q + 1)
                nc.vector.tensor_tensor(sh.w[0][:, LO, at:at + PIECE], room.raw[q % FIRST_RING],
                                        f32(sh.w[0][:, HI, at:at + PIECE]), ALU.subtract).then_inc(first_lo_dve, 1)

            def first():
                if room:
                    opening()
                    for tile in range(TPB):
                        stats(stages[0], 0, 0, tile)
                    first_table_rows()
                    normalise(stages[0], 0, 0, 0)
                    make_first_table()
                    normalise(stages[0], 0, 0, 1)
                    normalise(stages[0], 0, 0, 2)
                    split_xn(0, 0, 0)
                    normalise(stages[0], 0, 0, 3)
                    split_xn(0, 0, 1)
                    first_low(0)
                    split_xn(0, 0, 2)
                    first_low(2)
                    split_xn(0, 0, 3)
                    first_low(4)
                    first_low(6)
                    first_low(8)

            def block_step(n, parity, before, st, after):
                for c in range(chunks):
                    split_h(n, c)
                    if room and isinstance(n, int) and n == 0 and c < 3:
                        first_low(10 + 2 * c)
                    if room and isinstance(n, int) and n == 0 and c == 2:
                        make_gates()
                    if c == 0 and not (isinstance(n, int) and n == 0):
                        finish(before, n - 1, 1 - parity, TPB - 1)
                    if after is not None:
                        if TURN_STEP + 1 <= c <= TURN_STEP + after.token_tiles:
                            split_xn(n + 1, 1 - parity, c - TURN_STEP - 1)
                        if TURN_STEP - 1 <= c < TURN_STEP - 1 + after.token_tiles:
                            stats(after, n + 1, 1 - parity, c - TURN_STEP + 1)
                        if TURN_STEP <= c < TURN_STEP + after.token_tiles:
                            normalise(after, n + 1, 1 - parity, c - TURN_STEP)
                    if second_half_first and isinstance(n, int) and n == 0 and 2 * c < len(st.prefetch):
                        for q in (2 * c, 2 * c + 1):
                            piece_low(st, q, st.prefetch[q][1], q % STAGE_RING)
                    if room and isinstance(n, int) and n == 0 and c == chunks - 2:
                        late_copy(0)
                    if room and isinstance(n, int) and n == 0 and c == chunks - 1:
                        late_copy(1)
                        late_tables(0)
                    if not second_half_first and c in piece_steps(n):
                        piece_low(st, 2 * n + (c == chunks - 1), (2 * (n - NBLK * st.order) + (c == chunks - 1)) * PIECE, 0)
                for tile in range(TPB - 1):
                    finish(st, n, parity, tile)
                if room and isinstance(n, int) and n == 0:
                    late_copy(2)
                    late_tables(1)
                    late_tables(2)

            schedule(dve, first, block_step)
            finish(stages[-1], total - 1, 1, TPB - 1)



TPP = 2
NPAIR = B // TPP
PT = TPP * P
HALF = HEADS // 2


def attention_phase(nc, sh, *, source, target, bo, eps, table, prefetch, prefetch_region, following):
    sem = lambda what: sh.semaphore(nc, "att_" + what)
    x_loaded = [sem(f"x_loaded{tile}") for tile in range(TPP)]
    residual_loaded = [sem(f"residual_loaded{tile}") for tile in range(TPP)]
    stored = sh.stored["att"]
    const_loaded = sem("const_loaded")
    passed = sem("passed")
    bv_hi, bv_ready, bvo_done, bo_ready = sem("bv_hi"), sem("bv_ready"), sem("bvo_done"), sem("bo_ready")
    raw_stats, stats_done, var_done, rstd_done = sem("raw_stats"), sem("stats_done"), sem("var_done"), sem("rstd_done")
    xhat_ready, turned, modulated, xhi_done, xn_ready = (
        sem("xhat_ready"), sem("turned"), sem("modulated"), sem("xhi_done"), sem("xn_ready"))
    kq_done, kq_hi, kq_ready, v_done, v_ready = sem("kq_done"), sem("kq_hi"), sem("kq_ready"), sem("v_done"), sem("v_ready")
    diag_zeroed, diag_loaded = sem("diag_zeroed"), sem("diag_loaded")
    scores_done, max_done, negmax_done, exp_done, inv_done, probs_ready = (
        sem("scores_done"), sem("max_done"), sem("negmax_done"), sem("exp_done"), sem("inv_done"), sem("probs_ready"))
    probs_turned, probsT_ready, out_part = sem("probs_turned"), sem("probsT_ready"), sem("out_part")
    out_hi, out_ready = sem("out_hi"), sem("out_ready")
    proj_done, x_final, bias_added = sem("proj_done"), sem("x_final"), sem("bias_added")
    piece_loaded, piece_hi, piece_done = sem("piece_loaded"), sem("piece_hi"), sem("piece_done")
    scale = float(HD) ** -0.5
    W = sh.w[0]

    def weight(part, matrix, k):
        at = (matrix * KC + k) * D
        return W[:, part, at:at + D]

    WK, WQ, WV, WO = range(4)

    with ExitStack() as local:
        sb = lambda what, shape, dt: local.enter_context(nc.sbuf_tensor("att_" + what, shape, dt))
        x = sh.x[:, 0, 0:TPP, :]
        xmod = sh.x[:, 0, TPP:2 * TPP, :].rearrange("p t (k q) -> p t k q", k=KC)
        residual = sh.x[:, 1, 0:TPP, :]
        v = sh.x[:, 1, TPP:2 * TPP, :]
        xn = sh.xn[:, 0, :, :, 0:PT]
        q = sh.xn[:, 0, :, :, PT:2 * PT]
        kst = sh.xn[:, 1, :, :, 0:PT]
        oT = sh.xn[:, 1, :, :, PT:PT + P]
        probsT = sh.probsT
        kdiag = sb("kdiag", [P, 2, KC, HPC * P], F32R)
        probs = sb("probs", [P, HEADS, P], F32)
        bo_bc = sb("bo", [P, D], F32)
        bn = sb("bn", [P, 6], F32)
        mv = sb("mv", [P, TPP, 2], F32)
        var_eps = sb("var_eps", [P, TPP], F32)
        rstd = sb("rstd", [P, TPP], F32)
        smax = sb("smax", [P, HEADS], F32)
        negmax = sb("negmax", [P, HEADS], F32)
        rowsum = sb("rowsum", [P, HEADS], F32)
        inv = sb("inv", [P, HEADS], F32)
        stage = sb("stage", [P, PIECE], F32)
        s_ps = local.enter_context(nc.psum_tensor("att_s", [P, HEADS, P], F32))
        bank_ps = local.enter_context(nc.psum_tensor("att_banks", [P, 3, 512], F32))
        o_ps = local.enter_context(nc.psum_tensor("att_o", [P, KC, P], F32))
        bank = lambda n: bank_ps[:, n - 4, :]

        source_t = source.rearrange("(n p) d -> n p d", p=P)
        target_t = target.rearrange("(n p) d -> n p d", p=P)

        def schedule(eng, first, pair_step, last_tail):
            first()
            pair_step(0, False)
            with eng.Fori(0, NPAIR - 2) as i:
                pair_step(i + 1, True)
            pair_step(NPAIR - 1, True)
            last_tail()

        def probs_bank(tile, m):
            return 6 if m % 2 == 0 else 4 + tile

        def is_first(row):
            return isinstance(row, int) and row == 0

        def is_next(n):
            return isinstance(n, int) and n >= NPAIR

        block = local.enter_context(nc.Block())

        @block.sync
        def _(sp):
            def load_x(n, tile):
                if is_next(n):
                    rows = following.source[TPP * (n - NPAIR) + tile]
                else:
                    rows = source_t[TPP * n + tile]
                if not (isinstance(n, int) and n == 1):
                    sp.wait_ge(turned, TPP * (n - 2) + tile + 1)
                    sp.sem_inc(passed, 1)
                sp.dma_start(x[:, tile, :], rows).then_inc(x_loaded[tile], 16)

            def load_residual(n, tile):
                sp.dma_start(residual[:, tile, :], source_t[TPP * n + tile]).then_inc(residual_loaded[tile], 16)

            def diag(n, tile):
                sp.wait_ge(kq_ready, 2 * KC * n + KC)
                sp.sem_inc(passed, 1)
                if is_first(TPP * n + tile):
                    sp.wait_ge(diag_zeroed, 1)
                else:
                    sp.wait_ge(scores_done, 2 * (TPP * n + tile))
                    sp.sem_inc(passed, 1)
                for j in range(HPC):
                    rows = slice(j * HD, (j + 1) * HD)
                    sp.dma_start(f32(kdiag[rows, :, :, j * P:(j + 1) * P]), f32(kst[rows, :, :, tile * P:(tile + 1) * P])).then_inc(diag_loaded, 16)

            def store(n, tile):
                sp.wait_ge(x_final, TPP * n + tile + 1)
                sp.sem_inc(passed, 1)
                sp.dma_start(target_t[TPP * n + tile], residual[:, tile, :]).then_inc(stored[tile], 16)

            def first():
                for tile in range(TPB):
                    sp.wait_ge(sh.stored["mlp"][tile], 16 * 2 * NBLK)
                sp.dma_start(sh.tables[:, following.table, :, :, :].rearrange("p a k b -> p (a k b)"),
                             sh.tables_dram[:, following.dram_place * 2 * KC * B:(following.dram_place + 1) * 2 * KC * B]
                             ).then_inc(sh.table_loaded[following.phase], 16)
                sp.dma_start(bo_bc[:, :], bo.rearrange("(a n) -> a n", a=1).to_broadcast([P, D])).then_inc(const_loaded, 16)

            def pair_step(n, before):
                for tile in range(TPP):
                    load_x(n + 1, tile)
                diag(n, 0)
                if before:
                    store(n - 1, 0)
                    sp.wait_ge(stored[0], 16 * n)
                    sp.sem_inc(passed, 1)
                load_residual(n, 0)
                diag(n, 1)
                if before:
                    store(n - 1, 1)
                    sp.wait_ge(stored[1], 16 * n)
                    sp.sem_inc(passed, 1)
                load_residual(n, 1)

            def last_tail():
                for tile in range(TPP):
                    load_x(NPAIR + 1, tile)
                store(NPAIR - 1, 0)
                store(NPAIR - 1, 1)

            schedule(sp, first, pair_step, last_tail)

        @block.gpsimd
        def _(pool):
            def rstd_of(row):
                at = row % TPP
                pool.wait_ge(var_done, row + 1 - TPP)
                if row >= 2 * TPP:
                    pool.wait_ge(xhat_ready, row + 1 - 2 * TPP)
                nc.gpsimd.tensor_tensor(rstd[:, at:at + 1], var_eps[:, at:at + 1], sh.neg_half[:, 0:1], ALU.pow).then_inc(rstd_done, 1)

            def add_bias(row):
                xt = residual[:, row % TPP, :]
                pool.wait_ge(residual_loaded[row % TPP], 16 * (row // TPP + 1))
                nc.gpsimd.tensor_tensor(xt, xt, bo_bc[:, :], ALU.add).then_inc(bias_added, 1)

            nc.gpsimd.memset(f32(kdiag[:, :, :, :]).rearrange("p a k c -> p (a k c)"), 0.0).then_inc(diag_zeroed, 1)
            pool.wait_ge(bo_ready, 1)
            for n in range(NPAIR):
                if n:
                    pool.wait_ge(piece_done, n)
                pool.dma_start(stage[:, :], prefetch[n][0]).then_inc(piece_loaded, 16)
                add_bias(TPP * n)
                rstd_of(TPP * n + 2)
                rstd_of(TPP * n + 3)
                add_bias(TPP * n + 1)
            rstd_of(B + 2)
            rstd_of(B + 3)

        @block.tensor
        def _(pe):
            def product(out, steps):
                for s, (lhs, rhs) in enumerate(steps):
                    last = nc.tensor.matmul(out, lhs, rhs, start=s == 0, stop=s == len(steps) - 1)
                return last

            def turn(n, tile):
                pe.wait_ge(xhat_ready, TPP * (n - 1) + tile + 1)
                if not (is_next(n) and n > NPAIR):
                    pe.wait_ge(v_ready, TPP * (n - 1) + tile + 1)
                for k in range(KC):
                    last = nc.tensor.transpose(bank(4 + tile)[:, k * P:(k + 1) * P], x[:, tile, k * P:(k + 1) * P], sh.ident[:, :])
                last.then_inc(turned, 1)

            def keys_queries(n, u):
                m, matrix = u % KC, (WK, WQ)[u // KC]
                product(bank(5 - u % 2)[:, 0:PT], [(weight(a, matrix, k)[:, m * P:(m + 1) * P], xn[:, b, k, :])
                                                   for k in range(KC) for a, b in MUL_HI_LO]).then_inc(kq_done, 1)

            def scores(n, tile, e):
                row = TPP * n + tile
                if e == 0:
                    pe.wait_ge(diag_loaded, 16 * HPC * (row + 1))
                if tile == 0:
                    pe.wait_ge(kq_ready, 2 * KC * n + KC + 2 * e + 2)
                if not is_first(row):
                    pe.wait_ge(exp_done, 2 * row - 1 + e)
                elif e == 0:
                    pe.wait_ge(bo_ready, 1)
                for m in (2 * e, 2 * e + 1):
                    last = product(s_ps[:, m * HPC:(m + 1) * HPC, :].rearrange("p h k -> p (h k)"),
                                   [(q[:, a, m, tile * P:(tile + 1) * P], kdiag[:, b, m, :]) for a, b in MUL_HI_LO])
                last.then_inc(scores_done, 1)

            def values(n, tile):
                product(bank(4 + tile), [(xn[:, a, k, tile * P:(tile + 1) * P], weight(b, WV, k))
                                         for k in range(KC) for a, b in MUL_HI_LO]).then_inc(v_done, 1)

            def turn_probs(row, tile, m):
                if m % 2 == 0:
                    pe.wait_ge(probs_ready, 2 * row + m // 2 + 1)
                if m >= 2:
                    pe.wait_ge(probsT_ready, KC * row + m - 1)
                for j in range(HPC):
                    last = nc.tensor.transpose(bank(probs_bank(tile, m))[:, j * P:(j + 1) * P], probs[:, m * HPC + j, :], sh.ident[:, :])
                last.then_inc(probs_turned, 1)

            def weigh(row, tile, m):
                if m == 0:
                    pe.wait_ge(v_ready, row + 1)
                    if not is_first(row):
                        pe.wait_ge(out_ready, row)
                pe.wait_ge(probsT_ready, KC * row + m + 1)
                for j in range(HPC):
                    head = m * HPC + j
                    last = nc.tensor.matmul(o_ps[j * HD:(j + 1) * HD, m, :], v[:, tile, head * HD:(head + 1) * HD],
                                            probsT[:, m % 2, j, :], start=True, stop=True)
                last.then_inc(out_part, 1)

            def project(row):
                pe.wait_ge(out_ready, row + 1)
                product(bank(6), [(oT[:, a, k, :], weight(b, WO, k)) for k in range(KC) for a, b in MUL_HI_LO]).then_inc(proj_done, 1)

            def first_keys(n):
                pe.wait_ge(xn_ready, TPP * n)
                pe.wait_ge(modulated, TPP * n)
                keys_queries(n, 0)

            def first():
                keys_queries(0, 0)

            def pair_step(n, before):
                row = TPP * n
                if before:
                    pe.wait_ge(probsT_ready, KC * (row - 1))
                keys_queries(n, 1)
                for u in range(2, 2 * KC):
                    if u == KC and before:
                        project(row - 2)
                    elif u == KC:
                        pe.wait_ge(bv_ready, 1)
                        product(s_ps[:, 0:HPC, :].rearrange("p h k -> p (h k)"),
                                [(oT[:, a, k, :], weight(b, WO, k)) for k in range(KC) for a, b in MUL_HI_LO]).then_inc(bvo_done, 1)
                    pe.wait_ge(kq_ready, 2 * KC * n + u - 1)
                    keys_queries(n, u)
                scores(n, 0, 0)
                if before:
                    pe.wait_ge(x_final, row - 1)
                    turn_probs(row - 1, 1, 0)
                    pe.wait_ge(kq_ready, 2 * KC * n + 2 * KC - 1)
                    turn_probs(row - 1, 1, 1)
                scores(n, 0, 1)
                if before:
                    weigh(row - 1, 1, 0)
                    turn_probs(row - 1, 1, 2)
                    weigh(row - 1, 1, 1)
                    turn_probs(row - 1, 1, 3)
                pe.wait_ge(kq_ready, 2 * KC * (n + 1))
                values(n, 0)
                if before:
                    weigh(row - 1, 1, 2)
                    weigh(row - 1, 1, 3)
                values(n, 1)
                if before:
                    project(row - 1)
                turn(n + 1, 0)
                turn(n + 1, 1)
                scores(n, 1, 0)
                if before:
                    pe.wait_ge(x_final, row)
                turn_probs(row, 0, 0)
                pe.wait_ge(modulated, row + 1)
                turn_probs(row, 0, 1)
                scores(n, 1, 1)
                weigh(row, 0, 0)
                turn_probs(row, 0, 2)
                weigh(row, 0, 1)
                turn_probs(row, 0, 3)
                if not (isinstance(n, int) and n == NPAIR - 1):
                    first_keys(n + 1)
                weigh(row, 0, 2)
                weigh(row, 0, 3)

            def last_tail():
                row = B - 1
                project(row - 1)
                pe.wait_ge(x_final, row)
                turn_probs(row, 1, 0)
                pe.wait_ge(modulated, B)
                turn_probs(row, 1, 1)
                weigh(row, 1, 0)
                turn_probs(row, 1, 2)
                weigh(row, 1, 1)
                turn_probs(row, 1, 3)
                weigh(row, 1, 2)
                weigh(row, 1, 3)
                turn(NPAIR + 1, 0)
                turn(NPAIR + 1, 1)
                project(row)

            schedule(pe, first, pair_step, last_tail)

        @block.scalar
        def _(act):
            def modulate(n, tile):
                row = TPP * n + tile
                act.wait_ge(turned, row + 1 - TPP)
                if not (isinstance(n, int) and n == 1):
                    act.wait_ge(xn_ready, row - 1 - TPP)
                place = table
                if is_next(n):
                    row, place = row - B, following.table
                    act.wait_ge(sh.table_loaded[following.phase], 16)
                for k in range(KC):
                    last = nc.scalar.activation(xmod[:, tile, k, :], bank(4 + tile)[:, k * P:(k + 1) * P], ACT.Identity,
                                                bias=sh.tables[:, place, 1, k, bass.ds(row, 1)], scale=sh.tables[:, place, 0, k, bass.ds(row, 1)])
                last.then_inc(modulated, 1)

            def copy_probsT(row, tile):
                for m in range(KC):
                    act.wait_ge(probs_turned, KC * row + m + 1)
                    if m >= 2 or not is_first(row):
                        act.wait_ge(out_part, KC * row + m - 1)
                    nc.scalar.activation(probsT[:, m % 2, :, :], bank(probs_bank(tile, m)).rearrange("p (j q) -> p j q", j=HPC),
                                         ACT.Copy).then_inc(probsT_ready, 1)

            def exponentials(row):
                for e in range(2):
                    act.wait_ge(negmax_done, 2 * row + e + 1)
                    if not is_first(row):
                        act.wait_ge(probs_turned, KC * row - 2 + 2 * e)
                    for head in range(HALF * e, HALF * (e + 1)):
                        last = nc.scalar.activation(probs[:, head, :], s_ps[:, head, :], ACT.Exp, bias=negmax[:, head:head + 1],
                                                    scale=scale, accum_out=rowsum[:, head:head + 1])
                    last.then_inc(exp_done, 1)

            def first():
                pass

            def pair_step(n, before):
                row = TPP * n
                if before:
                    copy_probsT(row - 1, 1)
                exponentials(row)
                act.wait_ge(piece_loaded, 16 * (n + 1))
                nc.scalar.activation(sh.w[prefetch_region][:, HI, bass.ds(n * PIECE, PIECE)], stage[:, :], ACT.Copy).then_inc(piece_hi, 1)
                modulate(n + 1, 0)
                modulate(n + 1, 1)
                copy_probsT(row, 0)
                exponentials(row + 1)

            def last_tail():
                copy_probsT(B - 1, 1)
                modulate(NPAIR + 1, 0)
                modulate(NPAIR + 1, 1)

            schedule(act, first, pair_step, last_tail)

        @block.vector
        def _(dve):
            def vec(name, m):
                row = VEC_ROWS[name][0] + m
                return sh.vecs[:, row:row + 1]

            def stats(n, tile):
                count = TPP * (n - 1) + tile + 1
                dve.wait_ge(x_loaded[tile], 16 * n)
                nc.vector.bn_stats(bn[:, :], x[:, tile, :]).then_inc(raw_stats, 1)
                dve.wait_ge(raw_stats, count)
                dve.sem_inc(passed, 1)
                nc.vector.bn_aggr(mv[:, tile, :], bn[:, :]).then_inc(stats_done, 1)
                dve.wait_ge(stats_done, count)
                nc.vector.tensor_scalar(var_eps[:, tile:tile + 1], mv[:, tile, 1:2], following.eps if is_next(n) else eps, None, ALU.add).then_inc(var_done, 1)

            def normalise(n, tile):
                dve.wait_ge(rstd_done, TPP * (n - 1) + tile + 1)
                nc.vector.tensor_scalar(x[:, tile, :], x[:, tile, :], mv[:, tile, 0:1], rstd[:, tile:tile + 1],
                                        ALU.subtract, ALU.mult).then_inc(xhat_ready, 1)

            def split_xn(n, tile):
                place = q if is_next(n) and n > NPAIR else xn
                count = TPP * (n - 1) + tile + 1
                dve.wait_ge(modulated, count)
                hi = place[:, HI, :, tile * P:(tile + 1) * P]
                nc.vector.tensor_copy(hi, xmod[:, tile, :, :]).then_inc(xhi_done, 1)
                dve.wait_ge(xhi_done, count)
                nc.vector.tensor_tensor(place[:, LO, :, tile * P:(tile + 1) * P], xmod[:, tile, :, :], f32(hi),
                                        ALU.subtract).then_inc(xn_ready, 1)

            def split_kq(n, u):
                m, dst, bias = u % KC, (kst, q)[u // KC], ("bk", "bq")[u // KC]
                src = bank(5 - u % 2)[:, 0:PT]
                dve.wait_ge(kq_done, 2 * KC * n + u + 1)
                if u == 0 and not is_first(n):
                    dve.wait_ge(diag_loaded, 16 * HPC * TPP * n)
                nc.vector.tensor_scalar(dst[:, HI, m, :], src, vec(bias, m), None, ALU.add).then_inc(kq_hi, 1)
                dve.wait_ge(kq_hi, 2 * KC * n + u + 1)
                nc.vector.scalar_tensor_tensor(out=dst[:, LO, m, :], in0=src, scalar=vec(bias, m), in1=f32(dst[:, HI, m, :]),
                                               op0=ALU.add, op1=ALU.subtract).then_inc(kq_ready, 1)

            def row_max(row, e):
                heads = slice(HALF * e, HALF * (e + 1))
                dve.wait_ge(scores_done, 2 * row + e + 1)
                nc.vector.tensor_reduce(smax[:, heads], s_ps[:, heads, :], AX.X, ALU.max).then_inc(max_done, 1)
                dve.wait_ge(max_done, 2 * row + e + 1)
                nc.vector.tensor_scalar(negmax[:, heads], smax[:, heads], -scale, None, ALU.mult).then_inc(negmax_done, 1)

            def divide(row, e):
                heads = slice(HALF * e, HALF * (e + 1))
                dve.wait_ge(exp_done, 2 * row + e + 1)
                nc.vector.reciprocal(inv[:, heads], rowsum[:, heads]).then_inc(inv_done, 1)
                dve.wait_ge(inv_done, 2 * row + e + 1)
                nc.vector.tensor_tensor(probs[:, heads, :], probs[:, heads, :], inv[:, heads].unsqueeze(2).to_broadcast([P, HALF, P]),
                                        ALU.mult).then_inc(probs_ready, 1)

            def copy_values(n, tile):
                dve.wait_ge(v_done, TPP * n + tile + 1)
                nc.vector.tensor_copy(v[:, tile, :], bank(4 + tile)).then_inc(v_ready, 1)

            def split_out(row):
                dve.wait_ge(out_part, KC * (row + 1))
                nc.vector.tensor_copy(oT[:, HI, :, :], o_ps[:, :, :]).then_inc(out_hi, 1)
                dve.wait_ge(out_hi, row + 1)
                nc.vector.tensor_tensor(oT[:, LO, :, :], o_ps[:, :, :], f32(oT[:, HI, :, :]), ALU.subtract).then_inc(out_ready, 1)

            def finish(row, tile):
                xt = residual[:, tile, :]
                dve.wait_ge(proj_done, row + 1)
                dve.wait_ge(bias_added, row + 1)
                nc.vector.tensor_tensor(xt, bank(6), xt, ALU.add).then_inc(x_final, 1)

            def first():
                row = VEC_ROWS["bv"][0]
                bv = sh.vecs[:, row:row + KC].unsqueeze(2).to_broadcast([P, KC, P])
                nc.vector.tensor_copy(oT[:, HI, :, :], bv).then_inc(bv_hi, 1)
                dve.wait_ge(bv_hi, 1)
                nc.vector.tensor_tensor(oT[:, LO, :, :], bv, f32(oT[:, HI, :, :]), ALU.subtract).then_inc(bv_ready, 1)

            def pair_step(n, before):
                row = TPP * n
                split_kq(n, 0)
                split_kq(n, 1)
                if before:
                    split_out(row - 2)
                split_kq(n, 2)
                split_kq(n, 3)
                if before:
                    divide(row - 1, 0)
                    finish(row - 2, 0)
                split_kq(n, KC)
                if not before:
                    dve.wait_ge(const_loaded, 16)
                    dve.wait_ge(bvo_done, 1)
                    nc.vector.tensor_tensor(bo_bc[:, :], s_ps[:, 0:HPC, :].rearrange("p h k -> p (h k)"), bo_bc[:, :], ALU.add).then_inc(bo_ready, 1)
                split_kq(n, KC + 1)
                if before:
                    divide(row - 1, 1)
                split_kq(n, KC + 2)
                split_kq(n, KC + 3)
                row_max(row, 0)
                row_max(row, 1)
                stats(n + 1, 0)
                stats(n + 1, 1)
                copy_values(n, 0)
                if before:
                    split_out(row - 1)
                normalise(n + 1, 0)
                normalise(n + 1, 1)
                divide(row, 0)
                copy_values(n, 1)
                divide(row, 1)
                if before:
                    finish(row - 1, 1)
                split_xn(n + 1, 0)
                row_max(row + 1, 0)
                split_xn(n + 1, 1)
                row_max(row + 1, 1)
                dve.wait_ge(piece_hi, n + 1)
                nc.vector.tensor_tensor(sh.w[prefetch_region][:, LO, bass.ds(n * PIECE, PIECE)], stage[:, :],
                                        f32(sh.w[prefetch_region][:, HI, bass.ds(n * PIECE, PIECE)]), ALU.subtract).then_inc(piece_done, 1)

            def last_tail():
                split_out(B - 2)
                stats(NPAIR + 1, 0)
                stats(NPAIR + 1, 1)
                divide(B - 1, 0)
                finish(B - 2, 0)
                divide(B - 1, 1)
                normalise(NPAIR + 1, 0)
                normalise(NPAIR + 1, 1)
                split_out(B - 1)
                split_xn(NPAIR + 1, 0)
                finish(B - 1, 1)
                split_xn(NPAIR + 1, 1)

            schedule(dve, first, pair_step, last_tail)




def cond_seq_kernel(nc, t, out):
    with ExitStack() as ctx:
        sh = Shared(nc)
        with nc.sbuf_tensor("room", [P, 2 * REGION], F32) as room_tile:
            room = Room(room_tile)
        second_half = ctx.enter_context(nc.sbuf_tensor("weights1", [P, 2, REGION], F32R))
        sh.w = [ctx.enter_context(nc.sbuf_tensor("weights0", [P, 2, REGION], F32R)), second_half]
        with nc.sbuf_tensor("probsT_room", [P, 2, 2, KC, TOK], F32) as probsT_room:
            sh.probsT = probsT_room[:, 1, :, :, PT + P:PT + 2 * P]
        sh.xn = ctx.enter_context(nc.sbuf_tensor("xn", [P, 2, 2, KC, TOK], F32R))
        sh.x = ctx.enter_context(nc.sbuf_tensor("x_tiles", [P, 2, TPB, D], F32))
        sh.tables = ctx.enter_context(nc.sbuf_tensor("mod_tables", [P, 2, 2, KC, B], F32))
        sh.ident = ctx.enter_context(nc.sbuf_tensor("ident", [P, P], F32))
        sh.vecs = ctx.enter_context(nc.sbuf_tensor("vecs", [P, N_VEC], F32))
        sh.mask = ctx.enter_context(nc.sbuf_tensor("mask", [P, B], F32))
        sh.neg_half = ctx.enter_context(nc.sbuf_tensor("neg_half", [P, 4], F32))
        sh.tables_dram = nc.dram_tensor("late_tables", (P, 2 * 2 * KC * B), F32, kind="Internal").ap()
        sh.gates_dram = nc.dram_tensor("gate_rows", (2, B, D), F32, kind="Internal").ap()
        sh.gate_bias_dram = nc.dram_tensor("gate_bias_rows", (2, B, D), F32, kind="Internal").ap()
        x0 = t["x"].rearrange("b s d -> (b s) d")
        x1, x2, x3 = (nc.dram_tensor(f"x{n}", (B * P, D), F32, kind="Internal").ap() for n in (1, 2, 3))
        x4 = out.rearrange("b s d -> (b s) d")

        def vec_column(*names):
            columns = [VEC_ROWS[n][0] + r for n in names for r in range(VEC_ROWS[n][1])]
            return lambda c: sh.vecs[:, columns[c]:columns[c] + 1]

        def tiles(regions):
            first = lambda part, k, c: w1_view(regions[c // 8], part)[:, k, (c % 8) * P:(c % 8 + 1) * P]
            second = lambda part, c: w2_view(regions[c // 8], part)[:, c % 8, :]
            return first, second

        ff = mlp_pieces((t["ff_w1"][:, 0:512], t["ff_w1"][:, 512:1024]), (t["ff_w2"][0:512, :], t["ff_w2"][512:1024, :]))
        att = attention_pieces((t["wk"], t["wq"], t["wv"], t["wo"]))
        ffn = [mlp_pieces((t["w1"][:, h:h + 512], t["w1"][:, h + 512:h + 1024]), (t["w2"][h:h + 512, :], t["w2"][h + 512:h + 1024, :]))
               for h in (0, HID)]

        ssm_stage = Stage(x0, x1, tiles([sh.w[0]]), vec_column("ssm_b1", "bwd_b1"), ACT.Gelu, 1e-6, table=0, gate=0,
                          masked=True, prefetch=ff, prefetch_region=1)
        ff_stage = Stage(x1, x2, tiles([sh.w[1]]), vec_column("ff_b1"), ACT.Gelu_apprx_tanh, 1e-6, table=1, gate=1,
                         prefetch=att, prefetch_region=0, following=Opening("att", x2, TPP, 1e-5, place=0, dram_place=0))
        mlp_phase(nc, sh, "mlp", [ssm_stage, ff_stage], chunks=HID // P, room=room, t=t)
        sh.end_phase(nc)
        attention_phase(nc, sh, source=x2, target=x3, bo=t["bo"], eps=1e-5, table=0, prefetch=ffn[0], prefetch_region=1,
                        following=Opening("ffn", x3, TPB, 1e-5, place=1, dram_place=1))
        sh.end_phase(nc)
        ffn_stage = Stage(x3, x4, tiles([sh.w[1], sh.w[0]]), vec_column("b1"), ACT.Gelu, 1e-5, table=1, bias2=t["b2"],
                          prefetch=ffn[1], prefetch_region=0)
        mlp_phase(nc, sh, "ffn", [ffn_stage], chunks=2 * HID // P, second_half_first=True)


_INS = ["x", "cond_1024", "mask_BxS_bk0"] + ["L0_cond_" + n for n in (
    "ada_w", "ada_b", "ssm_w1", "ssm_b1", "ssm_w2", "ssm_b2", "bwd_w1", "bwd_b1", "bwd_w2", "bwd_b2",
    "ffada_w", "ffada_b", "ff_w1", "ff_b1", "ff_w2", "ff_b2")] + ["L1_cond_" + n for n in (
    "ln1_w", "ln1_b", "ln2_w", "ln2_b", "wq", "bq", "wk", "bk", "wv", "bv", "wo", "bo",
    "wt_attn", "bt_attn", "wt_ffn", "bt_ffn", "w1", "b1", "w2", "b2")]
_SHORT = {"cond_1024": "cond", "mask_BxS_bk0": "mask"}


def kernel(**inputs):
    import numpy as _np
    import concourse.bacc as _bacc
    from concourse import mybir as _mybir
    from concourse.bass_utils import run_bass_kernel_spmd as _run

    nc = _bacc.Bacc("TRN2", target_bir_lowering=False, num_devices=1)
    arrays, tensors = {}, {}
    for name in _INS:
        a = _np.ascontiguousarray(inputs[name])
        arrays[f"in_{name}_dram"] = a
        ap = nc.dram_tensor(f"in_{name}_dram", a.shape, _mybir.dt.from_np(a.dtype), kind="ExternalInput").ap()
        tensors[_SHORT.get(name, name.removeprefix("L0_cond_").removeprefix("L1_cond_"))] = ap
    out = nc.dram_tensor("out_0_dram", (B, P, D), _mybir.dt.float32, kind="ExternalOutput").ap()
    cond_seq_kernel(nc, tensors, out)
    r = _run(nc, [arrays], core_ids=[0])
    return r.results[0]["out_0_dram"]
```
